# Optimizing a Trainium2 kernel written in Bass

```python
import numpy as np
import jax
import jax.numpy as jnp

def _softmax(x, axis=-1):
    return jax.nn.softmax(x, axis=axis)

def _gelu(x):
    return jax.nn.gelu(x, approximate=True)

def _silu(x):
    return jax.nn.silu(x)

def _sigmoid(x):
    return jax.nn.sigmoid(x)

def _layernorm(x, axis=-1, eps=1e-05):
    m = jnp.mean(x, axis=axis, keepdims=True)
    v = jnp.var(x, axis=axis, keepdims=True)
    return (x - m) / jnp.sqrt(v + eps)

def _scatter_add(tgt, idx, src, axis=0):
    return tgt.at[idx].add(src)

def _segment_sum(src, seg, n):
    return jax.ops.segment_sum(src, seg, n)
kernel_name = 'mk_prb_d2_jaxref_r8_58c9eb'

def setup_inputs(seed: int=0):
    np.random.seed(seed)
    _w = jnp.asarray

    def _L0_attn_setup():
        import jax, jax.numpy as jnp
        import numpy as np
        B, T, HIDDEN = (2, 128, 128)
        NUM_HEADS = 6
        HEAD_K = 128
        HEAD_V = 32
        KEY_DIM = NUM_HEADS * HEAD_K
        VALUE_DIM = NUM_HEADS * HEAD_V
        CONV_K = 4
        NORM_EPS = 1e-05
        L2_EPS = 1e-06

        def _causal_conv_silu(x, w):
            K = w.shape[-1]
            t = x.shape[1]
            xp = jnp.pad(x, ((0, 0), (K - 1, 0), (0, 0)))
            y = sum((xp[:, j:j + t, :] * w[:, j] for j in range(K)))
            return y * jax.nn.sigmoid(y)

        def _l2norm(x):
            return x * jax.lax.rsqrt(jnp.sum(x * x, axis=-1, keepdims=True) + L2_EPS)

        def _gated_delta_rule(q, k, v, g, beta):
            scale = q.shape[-1] ** (-0.5)
            q = _l2norm(q) * scale
            k = _l2norm(k)

            def step(S, inp):
                q_t, k_t, v_t, g_t, b_t = inp
                S = S * jnp.exp(g_t)[..., None, None]
                kv = jnp.einsum('bhk,bhkv->bhv', k_t, S)
                delta = (v_t - kv) * b_t[..., None]
                S = S + jnp.einsum('bhk,bhv->bhkv', k_t, delta)
                o_t = jnp.einsum('bhk,bhkv->bhv', q_t, S)
                return (S, o_t)
            S0 = jnp.zeros((q.shape[0], q.shape[2], q.shape[3], v.shape[3]), q.dtype)
            xs = tuple((jnp.moveaxis(a, 1, 0) for a in (q, k, v, g, beta)))
            _, o = jax.lax.scan(step, S0, xs)
            return jnp.moveaxis(o, 0, 1)
        key = jax.random.key(seed)
        ks = jax.random.split(key, 14)
        s = 0.02
        return {'hidden_states': jax.random.normal(ks[0], (B, T, HIDDEN), jnp.float32), 'q_w': jax.random.normal(ks[1], (KEY_DIM, HIDDEN), jnp.float32) * s, 'k_w': jax.random.normal(ks[2], (KEY_DIM, HIDDEN), jnp.float32) * s, 'v_w': jax.random.normal(ks[3], (VALUE_DIM, HIDDEN), jnp.float32) * s, 'a_w': jax.random.normal(ks[4], (NUM_HEADS, HIDDEN), jnp.float32) * s, 'b_w': jax.random.normal(ks[5], (NUM_HEADS, HIDDEN), jnp.float32) * s, 'g_w': jax.random.normal(ks[6], (VALUE_DIM, HIDDEN), jnp.float32) * s, 'o_w': jax.random.normal(ks[7], (HIDDEN, VALUE_DIM), jnp.float32) * s, 'conv_q_w': jax.random.normal(ks[8], (KEY_DIM, CONV_K), jnp.float32) * 0.3, 'conv_k_w': jax.random.normal(ks[9], (KEY_DIM, CONV_K), jnp.float32) * 0.3, 'conv_v_w': jax.random.normal(ks[10], (VALUE_DIM, CONV_K), jnp.float32) * 0.3, 'A_log': jnp.log(jax.random.uniform(ks[11], (NUM_HEADS,), jnp.float32, 1.0, 16.0)), 'dt_bias': jax.random.normal(ks[12], (NUM_HEADS,), jnp.float32) * 0.5, 'norm_weight': jnp.ones((VALUE_DIM,), jnp.float32)}
    _L0_attn_in = _L0_attn_setup()

    def _L0_ffn_setup():
        import jax, jax.numpy as jnp
        import numpy as np
        DIM = 128
        DEPTH = 6
        HEADS = 16
        DIM_HEAD = 64
        WINDOW = 32
        INNER = HEADS * DIM_HEAD
        DIM_INNER = int(DIM * 4 * 2 / 3)
        QK_SCALE = 8.0

        def shift_tokens(t):
            a, s = jnp.split(t, 2, -1)
            s = jnp.pad(s, ((0, 0), (1, 0), (0, 0)))[:, :-1]
            return jnp.concatenate([a, s], -1)

        def l2norm(t):
            return t / jnp.maximum(jnp.linalg.norm(t, axis=-1, keepdims=True), 1e-12)

        def rotate_half(x):
            x1, x2 = jnp.split(x, 2, -1)
            return jnp.concatenate([-x2, x1], -1)

        def rotary_tables(n):
            half = jnp.arange(0, DIM_HEAD, 2, dtype=jnp.float32)
            inv_freq = 1.0 / 10000.0 ** (half / DIM_HEAD)
            t = jnp.arange(n, dtype=jnp.float32)
            freqs = t[:, None] * inv_freq[None, :]
            freqs = jnp.concatenate([freqs, freqs], -1)
            base_scale = (half + 0.4 * DIM_HEAD) / (1.4 * DIM_HEAD)
            power = (t - n // 2) / (WINDOW // 2)
            scale = base_scale[None, :] ** power[:, None]
            scale = jnp.concatenate([scale, scale], -1)
            return (freqs, scale)

        def local_attention(q, k, v):
            b, h, n, d = q.shape
            w = WINDOW
            nw = n // w
            bq = q.reshape(b, h, nw, w, d)
            bk = k.reshape(b, h, nw, w, d)
            bv = v.reshape(b, h, nw, w, d)

            def look(t):
                p = jnp.pad(t, ((0, 0), (0, 0), (1, 0), (0, 0), (0, 0)))
                return jnp.concatenate([p[:, :, :nw], p[:, :, 1:]], axis=3)
            bk2, bv2 = (look(bk), look(bv))
            seq = jnp.arange(n).reshape(nw, w)
            seq_p = jnp.pad(seq, ((1, 0), (0, 0)), constant_values=-1)
            jt = jnp.concatenate([seq_p[:nw], seq_p[1:]], axis=1)
            it = seq[:, :, None]
            jb = jt[:, None, :]
            mask = (it < jb) | (it > jb + w) | (jb == -1)
            sim = jnp.einsum('bhwie,bhwje->bhwij', bq, bk2) * QK_SCALE
            sim = jnp.where(mask, -jnp.finfo(sim.dtype).max, sim)
            attn = jax.nn.softmax(sim, -1)
            out = jnp.einsum('bhwij,bhwje->bhwie', attn, bv2)
            return out.reshape(b, h, n, d)

        def attn_layer(x, Wqkv, qs, ksc, Wo):
            b, n, _ = x.shape
            qkv = x @ Wqkv
            q, k, v = jnp.split(qkv, 3, -1)
            sh = lambda t: t.reshape(b, n, HEADS, DIM_HEAD).transpose(0, 2, 1, 3)
            q, k, v = (sh(q), sh(k), sh(v))
            q = l2norm(q) * qs
            k = l2norm(k) * ksc
            freqs, scale = rotary_tables(n)
            cos, sin = (jnp.cos(freqs), jnp.sin(freqs))
            q = q * cos * scale + rotate_half(q) * sin * scale
            inv = 1.0 / scale
            k = k * cos * inv + rotate_half(k) * sin * inv
            out = local_attention(q, k, v)
            out = out.transpose(0, 2, 1, 3).reshape(b, n, INNER)
            return out @ Wo

        def ffn_layer(x, g, bln, W1, b1, W2, b2):
            mu = x.mean(-1, keepdims=True)
            var = ((x - mu) ** 2).mean(-1, keepdims=True)
            xn = (x - mu) / jnp.sqrt(var + 1e-05) * g + bln
            hg = xn @ W1 + b1
            a, gate = jnp.split(hg, 2, -1)
            return a * jax.nn.gelu(gate, approximate=False) @ W2 + b2
        key = jax.random.key(seed)
        ks = jax.random.split(key, 8)
        B, N = (2, 256)
        init = lambda k, shape: jax.random.normal(k, shape, jnp.float32) * 0.02
        return {'x': jax.random.normal(ks[0], (B, N, DIM), jnp.float32), 'Wqkv': init(ks[1], (DEPTH, DIM, 3 * INNER)), 'q_scale': jnp.ones((DEPTH, DIM_HEAD), jnp.float32), 'k_scale': jnp.ones((DEPTH, DIM_HEAD), jnp.float32), 'Wo': init(ks[2], (DEPTH, INNER, DIM)), 'ln_g': jnp.ones((DEPTH, DIM), jnp.float32), 'ln_b': jnp.zeros((DEPTH, DIM), jnp.float32), 'W1': init(ks[3], (DEPTH, DIM, 2 * DIM_INNER)), 'b1': jnp.zeros((DEPTH, 2 * DIM_INNER), jnp.float32), 'W2': init(ks[4], (DEPTH, DIM_INNER, DIM)), 'b2': jnp.zeros((DEPTH, DIM), jnp.float32)}
    _L0_ffn_in = _L0_ffn_setup()

    def _L1_attn_setup():
        import jax, jax.numpy as jnp
        import numpy as np
        EMBED_DIM = 128
        NUM_HEADS = 16
        HEAD_DIM = EMBED_DIM // NUM_HEADS
        WINDOW = 128
        key = jax.random.key(seed)
        ks = jax.random.split(key, 9)
        B, S, E = (4, 512, EMBED_DIM)
        s = 1.0 / np.sqrt(E)
        return {'x': jax.random.normal(ks[0], (B, S, E), jnp.float32), 'Wq': jax.random.normal(ks[1], (E, E), jnp.float32) * s, 'bq': jnp.zeros((E,), jnp.float32), 'Wk': jax.random.normal(ks[2], (E, E), jnp.float32) * s, 'bk': jnp.zeros((E,), jnp.float32), 'Wv': jax.random.normal(ks[3], (E, E), jnp.float32) * s, 'bv': jnp.zeros((E,), jnp.float32), 'Wo': jax.random.normal(ks[4], (E, E), jnp.float32) * s, 'bo': jnp.zeros((E,), jnp.float32)}
    _L1_attn_in = _L1_attn_setup()

    def _L1_ffn_setup():
        import jax, jax.numpy as jnp
        import numpy as np
        NUM_COLUMNS = 16
        INPUT_DIM = 128
        NUM_NEURONS = 32
        SPARSITY = 0.05
        B, S = (4, 256)

        def _l2norm(v, axis=-1, eps=1e-12):
            n = jnp.sqrt(jnp.sum(v * v, axis=axis, keepdims=True))
            return v / jnp.maximum(n, eps)
        key = jax.random.key(seed)
        ks = jax.random.split(key, 12)
        D, C, N = (INPUT_DIM, NUM_COLUMNS, NUM_NEURONS)
        inp = {'x': jax.random.normal(ks[0], (B, S, D), dtype=jnp.float32), 'col_emb': jax.random.normal(ks[1], (C, D), dtype=jnp.float32) * 0.02, 'gate_w1': jax.random.normal(ks[2], (D, D // 2), dtype=jnp.float32) / np.sqrt(D), 'gate_b1': jnp.zeros((D // 2,), dtype=jnp.float32), 'gate_w2': jax.random.normal(ks[3], (D // 2, C), dtype=jnp.float32) / np.sqrt(D // 2), 'gate_b2': jnp.zeros((C,), dtype=jnp.float32), 'W_cols': jax.random.normal(ks[4], (C, D, N), dtype=jnp.float32) / np.sqrt(D), 'b_cols': jnp.zeros((C, N), dtype=jnp.float32), 'proj_w': jax.random.normal(ks[5], (C * N, D), dtype=jnp.float32) / np.sqrt(C * N), 'proj_b': jnp.zeros((D,), dtype=jnp.float32), 'ln_g': jnp.ones((D,), dtype=jnp.float32), 'ln_b': jnp.zeros((D,), dtype=jnp.float32)}
        return inp
    _L1_ffn_in = _L1_ffn_setup()
    _d = {'L0_attn_hidden_states': _L0_attn_in['hidden_states'], 'L0_attn_q_w': _L0_attn_in['q_w'], 'L0_attn_k_w': _L0_attn_in['k_w'], 'L0_attn_v_w': _L0_attn_in['v_w'], 'L0_attn_a_w': _L0_attn_in['a_w'], 'L0_attn_b_w': _L0_attn_in['b_w'], 'L0_attn_g_w': _L0_attn_in['g_w'], 'L0_attn_o_w': _L0_attn_in['o_w'], 'L0_attn_conv_q_w': _L0_attn_in['conv_q_w'], 'L0_attn_conv_k_w': _L0_attn_in['conv_k_w'], 'L0_attn_conv_v_w': _L0_attn_in['conv_v_w'], 'L0_attn_A_log': _L0_attn_in['A_log'], 'L0_attn_dt_bias': _L0_attn_in['dt_bias'], 'L0_attn_norm_weight': _L0_attn_in['norm_weight'], 'L0_ffn_Wqkv': _L0_ffn_in['Wqkv'], 'L0_ffn_q_scale': _L0_ffn_in['q_scale'], 'L0_ffn_k_scale': _L0_ffn_in['k_scale'], 'L0_ffn_Wo': _L0_ffn_in['Wo'], 'L0_ffn_ln_g': _L0_ffn_in['ln_g'], 'L0_ffn_ln_b': _L0_ffn_in['ln_b'], 'L0_ffn_W1': _L0_ffn_in['W1'], 'L0_ffn_b1': _L0_ffn_in['b1'], 'L0_ffn_W2': _L0_ffn_in['W2'], 'L0_ffn_b2': _L0_ffn_in['b2'], 'L1_attn_Wq': _L1_attn_in['Wq'], 'L1_attn_bq': _L1_attn_in['bq'], 'L1_attn_Wk': _L1_attn_in['Wk'], 'L1_attn_bk': _L1_attn_in['bk'], 'L1_attn_Wv': _L1_attn_in['Wv'], 'L1_attn_bv': _L1_attn_in['bv'], 'L1_attn_Wo': _L1_attn_in['Wo'], 'L1_attn_bo': _L1_attn_in['bo'], 'L1_ffn_col_emb': _L1_ffn_in['col_emb'], 'L1_ffn_gate_w1': _L1_ffn_in['gate_w1'], 'L1_ffn_gate_b1': _L1_ffn_in['gate_b1'], 'L1_ffn_gate_w2': _L1_ffn_in['gate_w2'], 'L1_ffn_gate_b2': _L1_ffn_in['gate_b2'], 'L1_ffn_W_cols': _L1_ffn_in['W_cols'], 'L1_ffn_b_cols': _L1_ffn_in['b_cols'], 'L1_ffn_proj_w': _L1_ffn_in['proj_w'], 'L1_ffn_proj_b': _L1_ffn_in['proj_b'], 'L1_ffn_ln_g': _L1_ffn_in['ln_g'], 'L1_ffn_ln_b': _L1_ffn_in['ln_b']}
    _x0 = _d['L0_attn_hidden_states']
    _d['L0_attn_hidden_states'] = jax.random.normal(jax.random.fold_in(jax.random.key(seed), 1), (2, 1024, 128), dtype=_x0.dtype)
    del _x0
    return _d

def reference(L0_attn_hidden_states, L0_attn_q_w, L0_attn_k_w, L0_attn_v_w, L0_attn_a_w, L0_attn_b_w, L0_attn_g_w, L0_attn_o_w, L0_attn_conv_q_w, L0_attn_conv_k_w, L0_attn_conv_v_w, L0_attn_A_log, L0_attn_dt_bias, L0_attn_norm_weight, L0_ffn_Wqkv, L0_ffn_q_scale, L0_ffn_k_scale, L0_ffn_Wo, L0_ffn_ln_g, L0_ffn_ln_b, L0_ffn_W1, L0_ffn_b1, L0_ffn_W2, L0_ffn_b2, L1_attn_Wq, L1_attn_bq, L1_attn_Wk, L1_attn_bk, L1_attn_Wv, L1_attn_bv, L1_attn_Wo, L1_attn_bo, L1_ffn_col_emb, L1_ffn_gate_w1, L1_ffn_gate_b1, L1_ffn_gate_w2, L1_ffn_gate_b2, L1_ffn_W_cols, L1_ffn_b_cols, L1_ffn_proj_w, L1_ffn_proj_b, L1_ffn_ln_g, L1_ffn_ln_b):

    def _L0_attn_ref(hidden_states, q_w, k_w, v_w, a_w, b_w, g_w, o_w, conv_q_w, conv_k_w, conv_v_w, A_log, dt_bias, norm_weight):
        import jax, jax.numpy as jnp
        import numpy as np
        B, T, HIDDEN = (2, 128, 128)
        NUM_HEADS = 6
        HEAD_K = 128
        HEAD_V = 32
        KEY_DIM = NUM_HEADS * HEAD_K
        VALUE_DIM = NUM_HEADS * HEAD_V
        CONV_K = 4
        NORM_EPS = 1e-05
        L2_EPS = 1e-06

        def _causal_conv_silu(x, w):
            K = w.shape[-1]
            t = x.shape[1]
            xp = jnp.pad(x, ((0, 0), (K - 1, 0), (0, 0)))
            y = sum((xp[:, j:j + t, :] * w[:, j] for j in range(K)))
            return y * jax.nn.sigmoid(y)

        def _l2norm(x):
            return x * jax.lax.rsqrt(jnp.sum(x * x, axis=-1, keepdims=True) + L2_EPS)

        def _gated_delta_rule(q, k, v, g, beta):
            scale = q.shape[-1] ** (-0.5)
            q = _l2norm(q) * scale
            k = _l2norm(k)

            def step(S, inp):
                q_t, k_t, v_t, g_t, b_t = inp
                S = S * jnp.exp(g_t)[..., None, None]
                kv = jnp.einsum('bhk,bhkv->bhv', k_t, S)
                delta = (v_t - kv) * b_t[..., None]
                S = S + jnp.einsum('bhk,bhv->bhkv', k_t, delta)
                o_t = jnp.einsum('bhk,bhkv->bhv', q_t, S)
                return (S, o_t)
            S0 = jnp.zeros((q.shape[0], q.shape[2], q.shape[3], v.shape[3]), q.dtype)
            xs = tuple((jnp.moveaxis(a, 1, 0) for a in (q, k, v, g, beta)))
            _, o = jax.lax.scan(step, S0, xs)
            return jnp.moveaxis(o, 0, 1)
        hs = hidden_states
        b, t, _ = hs.shape
        q = _causal_conv_silu(hs @ q_w.T, conv_q_w)
        k = _causal_conv_silu(hs @ k_w.T, conv_k_w)
        v = _causal_conv_silu(hs @ v_w.T, conv_v_w)
        beta = jax.nn.sigmoid(hs @ b_w.T)
        g = -jnp.exp(A_log) * jax.nn.softplus(hs @ a_w.T + dt_bias)
        q = q.reshape(b, t, NUM_HEADS, HEAD_K)
        k = k.reshape(b, t, NUM_HEADS, HEAD_K)
        v = v.reshape(b, t, NUM_HEADS, HEAD_V)
        o = _gated_delta_rule(q, k, v, g, beta).reshape(b, t, VALUE_DIM)
        gate = hs @ g_w.T
        o = o * (gate * jax.nn.sigmoid(gate))
        o = o * jax.lax.rsqrt(jnp.mean(o * o, axis=-1, keepdims=True) + NORM_EPS) * norm_weight
        return o @ o_w.T

    def _L0_ffn_ref(x, Wqkv, q_scale, k_scale, Wo, ln_g, ln_b, W1, b1, W2, b2):
        import jax, jax.numpy as jnp
        import numpy as np
        DIM = 128
        DEPTH = 6
        HEADS = 16
        DIM_HEAD = 64
        WINDOW = 32
        INNER = HEADS * DIM_HEAD
        DIM_INNER = int(DIM * 4 * 2 / 3)
        QK_SCALE = 8.0

        def shift_tokens(t):
            a, s = jnp.split(t, 2, -1)
            s = jnp.pad(s, ((0, 0), (1, 0), (0, 0)))[:, :-1]
            return jnp.concatenate([a, s], -1)

        def l2norm(t):
            return t / jnp.maximum(jnp.linalg.norm(t, axis=-1, keepdims=True), 1e-12)

        def rotate_half(x):
            x1, x2 = jnp.split(x, 2, -1)
            return jnp.concatenate([-x2, x1], -1)

        def rotary_tables(n):
            half = jnp.arange(0, DIM_HEAD, 2, dtype=jnp.float32)
            inv_freq = 1.0 / 10000.0 ** (half / DIM_HEAD)
            t = jnp.arange(n, dtype=jnp.float32)
            freqs = t[:, None] * inv_freq[None, :]
            freqs = jnp.concatenate([freqs, freqs], -1)
            base_scale = (half + 0.4 * DIM_HEAD) / (1.4 * DIM_HEAD)
            power = (t - n // 2) / (WINDOW // 2)
            scale = base_scale[None, :] ** power[:, None]
            scale = jnp.concatenate([scale, scale], -1)
            return (freqs, scale)

        def local_attention(q, k, v):
            b, h, n, d = q.shape
            w = WINDOW
            nw = n // w
            bq = q.reshape(b, h, nw, w, d)
            bk = k.reshape(b, h, nw, w, d)
            bv = v.reshape(b, h, nw, w, d)

            def look(t):
                p = jnp.pad(t, ((0, 0), (0, 0), (1, 0), (0, 0), (0, 0)))
                return jnp.concatenate([p[:, :, :nw], p[:, :, 1:]], axis=3)
            bk2, bv2 = (look(bk), look(bv))
            seq = jnp.arange(n).reshape(nw, w)
            seq_p = jnp.pad(seq, ((1, 0), (0, 0)), constant_values=-1)
            jt = jnp.concatenate([seq_p[:nw], seq_p[1:]], axis=1)
            it = seq[:, :, None]
            jb = jt[:, None, :]
            mask = (it < jb) | (it > jb + w) | (jb == -1)
            sim = jnp.einsum('bhwie,bhwje->bhwij', bq, bk2) * QK_SCALE
            sim = jnp.where(mask, -jnp.finfo(sim.dtype).max, sim)
            attn = jax.nn.softmax(sim, -1)
            out = jnp.einsum('bhwij,bhwje->bhwie', attn, bv2)
            return out.reshape(b, h, n, d)

        def attn_layer(x, Wqkv, qs, ksc, Wo):
            b, n, _ = x.shape
            qkv = x @ Wqkv
            q, k, v = jnp.split(qkv, 3, -1)
            sh = lambda t: t.reshape(b, n, HEADS, DIM_HEAD).transpose(0, 2, 1, 3)
            q, k, v = (sh(q), sh(k), sh(v))
            q = l2norm(q) * qs
            k = l2norm(k) * ksc
            freqs, scale = rotary_tables(n)
            cos, sin = (jnp.cos(freqs), jnp.sin(freqs))
            q = q * cos * scale + rotate_half(q) * sin * scale
            inv = 1.0 / scale
            k = k * cos * inv + rotate_half(k) * sin * inv
            out = local_attention(q, k, v)
            out = out.transpose(0, 2, 1, 3).reshape(b, n, INNER)
            return out @ Wo

        def ffn_layer(x, g, bln, W1, b1, W2, b2):
            mu = x.mean(-1, keepdims=True)
            var = ((x - mu) ** 2).mean(-1, keepdims=True)
            xn = (x - mu) / jnp.sqrt(var + 1e-05) * g + bln
            hg = xn @ W1 + b1
            a, gate = jnp.split(hg, 2, -1)
            return a * jax.nn.gelu(gate, approximate=False) @ W2 + b2
        for i in range(DEPTH):
            x = attn_layer(shift_tokens(x), Wqkv[i], q_scale[i], k_scale[i], Wo[i]) + x
            x = ffn_layer(shift_tokens(x), ln_g[i], ln_b[i], W1[i], b1[i], W2[i], b2[i]) + x
        return x

    def _L1_attn_ref(x, Wq, bq, Wk, bk, Wv, bv, Wo, bo):
        import jax, jax.numpy as jnp
        import numpy as np
        EMBED_DIM = 128
        NUM_HEADS = 16
        HEAD_DIM = EMBED_DIM // NUM_HEADS
        WINDOW = 128
        B, S, E = x.shape
        H, D, W = (NUM_HEADS, HEAD_DIM, WINDOW)
        scale = jnp.sqrt(jnp.asarray(D, x.dtype))

        def heads(t):
            return t.reshape(B, S, H, D).transpose(0, 2, 1, 3)
        q = heads(x @ Wq + bq)
        k = heads(x @ Wk + bk)
        v = heads(x @ Wv + bv)
        offs = jnp.arange(-W, W + 1)
        idx = jnp.arange(S)[:, None] + offs[None, :]
        valid = (idx >= 0) & (idx < S)
        idxc = jnp.clip(idx, 0, S - 1)
        k_win = k[:, :, idxc, :]
        v_win = v[:, :, idxc, :]
        scores = jnp.einsum('bhsd,bhswd->bhsw', q, k_win) / scale
        scores = jnp.where(valid[None, None], scores, jnp.asarray(-jnp.inf, scores.dtype))
        attn = jax.nn.softmax(scores, axis=-1)
        out = jnp.einsum('bhsw,bhswd->bhsd', attn, v_win)
        out = out.transpose(0, 2, 1, 3).reshape(B, S, E)
        return out @ Wo + bo

    def _L1_ffn_ref(x, col_emb, gate_w1, gate_b1, gate_w2, gate_b2, W_cols, b_cols, proj_w, proj_b, ln_g, ln_b):
        import jax, jax.numpy as jnp
        import numpy as np
        NUM_COLUMNS = 16
        INPUT_DIM = 128
        NUM_NEURONS = 32
        SPARSITY = 0.05
        B, S = (4, 256)

        def _l2norm(v, axis=-1, eps=1e-12):
            n = jnp.sqrt(jnp.sum(v * v, axis=axis, keepdims=True))
            return v / jnp.maximum(n, eps)
        Bq, Sq, D = x.shape
        C = col_emb.shape[0]
        similarity = jnp.einsum('bsd,cd->bsc', _l2norm(x), _l2norm(col_emb))
        h = jax.nn.gelu(x @ gate_w1 + gate_b1, approximate=False)
        gate_values = jax.nn.sigmoid(h @ gate_w2 + gate_b2)
        logits = similarity + gate_values
        k = max(1, int(C * SPARSITY))
        _, top_idx = jax.lax.top_k(logits, k)
        mask = jnp.sum(jax.nn.one_hot(top_idx, C, dtype=logits.dtype), axis=-2)
        weights = mask * jax.nn.softmax(logits, axis=-1)
        cols = jax.nn.gelu(jnp.einsum('bsd,cdn->bscn', x, W_cols) + b_cols, approximate=False)
        cols = cols * weights[..., None]
        combined = cols.reshape(Bq, Sq, -1)
        y = combined @ proj_w + proj_b + x
        mu = jnp.mean(y, axis=-1, keepdims=True)
        var = jnp.mean((y - mu) ** 2, axis=-1, keepdims=True)
        out = (y - mu) * jax.lax.rsqrt(var + 1e-05) * ln_g + ln_b
        return out
    x = L0_attn_hidden_states
    xn = _layernorm(x, axis=-1)
    x = x + _L0_attn_ref(xn, L0_attn_q_w, L0_attn_k_w, L0_attn_v_w, L0_attn_a_w, L0_attn_b_w, L0_attn_g_w, L0_attn_o_w, L0_attn_conv_q_w, L0_attn_conv_k_w, L0_attn_conv_v_w, L0_attn_A_log, L0_attn_dt_bias, L0_attn_norm_weight) + _L0_ffn_ref(xn, L0_ffn_Wqkv, L0_ffn_q_scale, L0_ffn_k_scale, L0_ffn_Wo, L0_ffn_ln_g, L0_ffn_ln_b, L0_ffn_W1, L0_ffn_b1, L0_ffn_W2, L0_ffn_b2)
    xn = _layernorm(x, axis=-1)
    x = x + _L1_attn_ref(xn, L1_attn_Wq, L1_attn_bq, L1_attn_Wk, L1_attn_bk, L1_attn_Wv, L1_attn_bv, L1_attn_Wo, L1_attn_bo) + _L1_ffn_ref(xn, L1_ffn_col_emb, L1_ffn_gate_w1, L1_ffn_gate_b1, L1_ffn_gate_w2, L1_ffn_gate_b2, L1_ffn_W_cols, L1_ffn_b_cols, L1_ffn_proj_w, L1_ffn_proj_b, L1_ffn_ln_g, L1_ffn_ln_b)
    return x

_drawn_inputs = setup_inputs


def setup_inputs(seed=0):
    import zlib

    import numpy as np

    out = dict(_drawn_inputs(seed))
    spreads = {'L0_attn_norm_weight': (1.0, 0.6),
     'L0_ffn_q_scale': (1.0, 0.6),
     'L0_ffn_k_scale': (1.0, 0.6),
     'L0_ffn_ln_g': (1.0, 0.6),
     'L0_ffn_ln_b': (0.0, 0.8),
     'L0_ffn_b1': (0.0, 0.8),
     'L0_ffn_b2': (0.0, 0.1),
     'L1_attn_bq': (0.0, 2.0),
     'L1_attn_bk': (0.0, 2.0),
     'L1_attn_bv': (0.0, 0.547),
     'L1_attn_bo': (0.0, 0.632),
     'L1_ffn_gate_b1': (0.0, 0.8),
     'L1_ffn_gate_b2': (0.0, 2.0),
     'L1_ffn_b_cols': (0.0, 2.0),
     'L1_ffn_proj_b': (0.0, 0.8),
     'L1_ffn_ln_g': (1.0, 0.2),
     'L1_ffn_ln_b': (0.0, 0.57)}
    factors = {'L0_attn_q_w': 8.0,
     'L0_attn_k_w': 8.0,
     'L0_attn_v_w': 8.0,
     'L0_attn_a_w': 8.0,
     'L0_attn_b_w': 8.0,
     'L0_attn_g_w': 8.0,
     'L0_attn_o_w': 8.0,
     'L0_attn_conv_q_w': 8.0,
     'L0_attn_conv_k_w': 8.0,
     'L0_attn_conv_v_w': 8.0,
     'L0_attn_A_log': 8.0,
     'L0_attn_dt_bias': 8.0,
     'L0_ffn_W1': 3.647,
     'L0_ffn_W2': 3.571,
     'L1_ffn_col_emb': 8.0,
     'L1_ffn_gate_w1': 8.0,
     'L1_ffn_gate_w2': 8.0,
     'L1_ffn_W_cols': 8.0,
     'L1_ffn_proj_w': 8.0,
     'L1_attn_Wq': 3.823,
     'L1_attn_Wk': 3.095}
    for name, (base, spread) in spreads.items():
        noise = np.random.default_rng([zlib.crc32(name.encode()), seed]).standard_normal(out[name].shape)
        drawn = base * np.exp(spread * noise) if base else spread * noise
        out[name] = jnp.asarray(drawn.astype(out[name].dtype))
    for name, factor in factors.items():
        out[name] = (out[name] * factor).astype(out[name].dtype)
    return out
```

```python
from contextlib import ExitStack

import numpy as np

import concourse.bass as bass
from concourse import mybir

F32 = mybir.dt.float32
BF16 = mybir.dt.bfloat16
I32 = mybir.dt.int32
ALU = mybir.AluOpType
ACT = mybir.ActivationFunctionType
AX = mybir.AxisListType.X

P = 128
BATCH, SEQ, D = 2, 1024, 128
NT = BATCH * SEQ // P
TB = SEQ // P
NEG = -1e30
EXP_MAX = 87.0


def buffers(nc, ctx):
    taken = []

    def sb(name, shape, dt=F32):
        return ctx.enter_context(nc.sbuf_tensor(name, shape, dt))

    def ps(name, shape, dt=F32):
        return ctx.enter_context(nc.psum_tensor(name, shape, dt))

    def sem(name):
        taken.append(nc.alloc_semaphore(name))
        return taken[-1]

    def clear():
        if taken:
            nc.clear_and_free_semaphores(taken)
            nc.all_engine_barrier()

    ctx.callback(clear)
    return sb, ps, sem


RSQRT_STEPS = 15


def rsqrt(eng, y, x, tmp, low, shift, done, n, tick):
    def step(ins, k):
        ins.then_inc(done, 1)
        eng.wait_ge(done, n + k)
        eng.sem_inc(tick, 1)

    step(eng.tensor_scalar(x, x, shift, low, ALU.add, ALU.max), 1)
    step(eng.tensor_scalar(y.bitcast(I32), x.bitcast(I32), -0.5, float(0x5F3759DF), ALU.mult, ALU.add), 2)
    step(eng.tensor_scalar(x, x, -0.5, None, ALU.mult), 3)
    for i in range(3):
        step(eng.tensor_tensor(tmp, y, y, ALU.mult), 4 * i + 4)
        step(eng.tensor_tensor(tmp, tmp, x, ALU.mult), 4 * i + 5)
        step(eng.tensor_scalar(tmp, tmp, 1.5, None, ALU.add), 4 * i + 6)
        last = eng.tensor_tensor(y, tmp, y, ALU.mult)
        if i < 2:
            step(last, 4 * i + 7)
    last.then_inc(done, 1)

def normalise(nc, x, xn, xnT, ident, tag, add=None):
    GT = 4
    with ExitStack() as ctx:
        sb, ps, sem = buffers(nc, ctx)
        st = sb(tag + "_st", [P, NT, 6])
        mv = sb(tag + "_mv", [P, NT, 2])
        rstd = sb(tag + "_rstd", [P, NT])
        tmp = sb(tag + "_tmp", [P, NT])
        tp = [ps(f"{tag}_tp{i}", [P, GT, P]) for i in range(2)]
        sum_rdy, st_rdy, mv_rdy, rs_rdy, centred, xn_rdy, tp_done, xnT_rdy, tick = (sem(f"{tag}_{s}") for s in (
            "sum_rdy", "st_rdy", "mv_rdy", "rs_rdy", "centred", "xn_rdy", "tp_done", "xnT_rdy", "tick"))
        block = ctx.enter_context(nc.Block())

        @block.vector
        def _(dve):
            if add is not None:
                dve.tensor_tensor(x[:], x[:], add[:], ALU.add).then_inc(sum_rdy, 1)
                dve.wait_ge(sum_rdy, 1)
            for t in range(NT):
                dve.bn_stats(st[:, t, :], x[:, t, :]).then_inc(st_rdy, 1)
            dve.wait_ge(st_rdy, NT)
            for t in range(NT):
                dve.bn_aggr(mv[:, t, :], st[:, t, :]).then_inc(mv_rdy, 1)
            dve.wait_ge(mv_rdy, NT)
            for g in range(NT // GT):
                s = slice(GT * g, GT * g + GT)
                dve.tensor_tensor(xn[:, s, :], x[:, s, :], mv[:, s, 0:1].to_broadcast([P, GT, D]), ALU.subtract).then_inc(centred, 1)
            dve.wait_ge(rs_rdy, RSQRT_STEPS)
            for g in range(NT // GT):
                s = slice(GT * g, GT * g + GT)
                dve.wait_ge(centred, g + 1)
                dve.tensor_tensor(xn[:, s, :], xn[:, s, :],
                                  rstd[:, s].rearrange("p (t o) -> p t o", o=1).to_broadcast([P, GT, D]), ALU.mult).then_inc(xn_rdy, 1)

        @block.gpsimd
        def _(pool):
            pool.wait_ge(mv_rdy, NT)
            rsqrt(pool, rstd[:], mv[:, :, 1], tmp[:], 0.0, 1e-5, rs_rdy, 0, tick)

        @block.tensor
        def _(pe):
            for g in range(NT // GT):
                pe.wait_ge(xn_rdy, g + 1)
                if g >= 2:
                    pe.wait_ge(xnT_rdy, g - 1)
                for k in range(GT):
                    mm = pe.transpose(tp[g % 2][:, k, :], xn[:, GT * g + k, :], ident[:])
                mm.then_inc(tp_done, 1)

        @block.scalar
        def _(act):
            for g in range(NT // GT):
                act.wait_ge(tp_done, g + 1)
                act.activation(xnT(GT * g, GT), tp[g % 2][:].rearrange("p t q -> p (t q)"), ACT.Copy).then_inc(xnT_rdy, 1)
            act.wait_ge(xnT_rdy, NT // GT)


def gated_delta(nc, x, xn, ident, identb, dram):
    with ExitStack() as ctx:
        sb, ps, sem = buffers(nc, ctx)
        qT = sb("qT", [P, GH, BATCH * SEQ])
        kT = sb("kT", [P, GH, BATCH * SEQ])
        vT = sb("vT", [P, len(VB), BATCH * SEQ])
        gate = sb("gate", [P, NT, VD])
        beta = sb("beta", [P, NT, GH])
        logdecay = sb("logdecay", [P, NT, GH])
        decay = sb("decay", [P, 3, NT, GH])
        rinv = sb("rinv", [P, 2 * GH, NT])
        cleared = sem("cleared")
        with ExitStack() as first:
            xnT = first.enter_context(nc.sbuf_tensor("xnT", [P, BATCH, KCONV - 1 + SEQ], F32))
            with nc.Block() as block:
                @block.vector
                def _(dve):
                    dve.memset(xnT[:, :, 0:KCONV - 1], 0.0)
                    dve.memset(vT[:], 0.0).then_inc(cleared, 1)
                    dve.wait_ge(cleared, 1)
            normalise(nc, x, xn, lambda t, n: xnT[:, t // TB, KCONV - 1 + P * (t % TB):KCONV - 1 + P * (t % TB + n)], ident, "n0")
            delta_inputs(nc, xnT, qT, kT, vT, gate, (beta, logdecay), rinv, decay, dram)
        delta_chunks(nc, x[:].rearrange("p t d -> p (t d)"), ident, identb, qT, kT, vT, gate, beta, logdecay, rinv, decay, dram)
        delta_outputs(nc, x, ident, gate, dram)

GH, HK, HV, KCONV = 6, 128, 32, 4
KD, VD = GH * HK, GH * HV
VB = [(0, 128), (128, VD - 128)]
NBLK = 2 * GH + len(VB)
LEVELS = 7
SMALL = NT * GH
SERIES = range(15, 1, -2)
GATE_G = 13 + len(SERIES)


def delta_inputs(nc, xnT, qT, kT, vT, gate, beta, rinv, decay, dram):
    beta, logdecay = beta
    with ExitStack() as ctx:
        sb, ps, sem = buffers(nc, ctx)
        w_qkv = sb("d_w_qkv", [P, 2 * KD + VD])
        w_abg = sb("d_w_abg", [P, 2 * GH + VD])
        w_conv = sb("d_w_conv", [P, NBLK, KCONV])
        dt_bias = sb("d_dt_bias", [P, GH])
        a_log = sb("d_a_log", [P, GH])
        tri = sb("d_tri", [P, 3, P])
        raw = [sb(f"d_raw{i}", [P, KCONV - 1 + SEQ]) for i in range(2)]
        conv = [sb(f"d_conv{i}", [P, SEQ]) for i in range(2)]
        sqd = [sb(f"d_sqd{i}", [P, SEQ]) for i in range(2)]
        rs_tmp = sb("d_rs_tmp", [P, 2 * GH * NT])
        zab = sb("d_zab", [P, NT, 2 * GH])
        za = sb("d_za", [P, NT, GH])
        e1 = sb("d_e1", [P, NT, GH])
        s1 = sb("d_s1", [P, NT, GH])
        s2 = sb("d_s2", [P, NT, GH])
        pl = sb("d_pl", [P, NT, GH])
        ssq = sb("d_ssq", [P, 2 * GH * NT])

        proj = [ps(f"d_proj{i}", [P, SEQ]) for i in range(2)]
        norms = ps("d_norms", [P, 512])
        zp = [ps(f"d_zp{i}", [P, 512]) for i in range(2)]
        sums = ps("d_sums", [P, 512])

        w_ld = sem("d_w_ld")
        init = sem("d_init")
        proj_done = sem("d_proj_done")
        raw_rdy = sem("d_raw_rdy")
        conv_rdy = sem("d_conv_rdy")
        tap_rdy = sem("d_tap_rdy")
        silu_rdy = sem("d_silu_rdy")
        sqd_rdy = sem("d_sqd_rdy")
        norm_done = sem("d_norm_done")
        z_done = sem("d_z_done")
        z_rdy = sem("d_z_rdy")
        gate_step = sem("d_gate_step")
        act_step = sem("d_act_step")
        ssq_rdy = sem("d_ssq_rdy")
        rinv_step = sem("d_rinv_step")
        rinv_rdy = sem("d_rinv_rdy")
        sums_done = sem("d_sums_done")
        tick = {e: sem(f"d_tick_{e}") for e in ("pe", "act", "dve", "pool")}

        def rows(f):
            return P if f < 2 * GH else VB[f - 2 * GH][1]

        def convolved(f, b):
            if f < GH:
                return qT[:, f, bass.ds(b * SEQ, SEQ)]
            if f < 2 * GH:
                return kT[:, f - GH, bass.ds(b * SEQ, SEQ)]
            return vT[0:rows(f), f - 2 * GH, bass.ds(b * SEQ, SEQ)]

        block = ctx.enter_context(nc.Block())

        @block.sync
        def _(sp):
            for dst, src in ((w_qkv[:], dram["d_w_qkv"]), (w_abg[:], dram["d_w_abg"]), (w_conv[:], dram["d_w_conv"]),
                             (dt_bias[:], dram["d_dt_bias"].broadcast_to([P, GH])),
                             (a_log[:], dram["d_a_log"].broadcast_to([P, GH])), (tri[:], dram["d_tri"])):
                sp.dma_start(dst, src).then_inc(w_ld, 16)

        @block.tensor
        def _(pe):
            pe.wait_ge(w_ld, 96)
            pe.wait_ge(init, 1)
            with pe.Fori(0, BATCH) as b:
                for f in range(NBLK):
                    i = b * NBLK + f
                    m = rows(f)
                    pe.wait_ge(raw_rdy, i + 1)
                    pe.sem_inc(tick["pe"], 1)
                    for c in range(SEQ // 512):
                        mm = pe.matmul(proj[f % 2][0:m, 512 * c:512 * c + 512], w_qkv[:, P * f:P * f + m],
                                       xnT[:, bass.ds(b, 1), KCONV - 1 + 512 * c:KCONV - 1 + 512 * c + 512],
                                       start=True, stop=True)
                    mm.then_inc(proj_done, 1)
                    if f >= 2:
                        pe.wait_ge(sqd_rdy, b * 2 * GH + f - 1)
                        for k in range(TB):
                            mm = pe.matmul(norms[:, bass.ds(b * TB + (f - 2) * NT + k, 1)],
                                           sqd[f % 2][:, P * k:P * k + P], tri[:, 2, 0:1], start=True, stop=True,
                                           skip_group_check=True)
                        mm.then_inc(norm_done, 1)
            for t in range(NT):
                b, k = t // TB, t % TB
                if t >= 2:
                    pe.wait_ge(z_rdy, t - 1)
                pe.matmul(zp[t % 2][:, 0:2 * GH + VD], xnT[:, b, KCONV - 1 + P * k:KCONV - 1 + P * k + P], w_abg[:],
                          start=True, stop=True).then_inc(z_done, 1)
            pe.wait_ge(gate_step, GATE_G)
            for a in range(3):
                mm = pe.matmul(sums[:, SMALL * a:SMALL * a + SMALL], tri[:, a, :], logdecay[:].rearrange("p t h -> p (t h)"),
                               start=True, stop=True, skip_group_check=True)
            mm.then_inc(sums_done, 1)

        @block.scalar
        def _(act):
            act.wait_ge(init, 1)
            with act.Fori(0, BATCH) as b:
                def keep_raw(f):
                    i = b * NBLK + f
                    m = rows(f)
                    act.wait_ge(proj_done, i + 1)
                    act.wait_ge(conv_rdy, i + 1)
                    act.activation(raw[f % 2][0:m, KCONV - 1:], proj[f % 2][0:m, :], ACT.Copy).then_inc(raw_rdy, 1)

                keep_raw(0)
                for f in range(NBLK):
                    i = b * NBLK + f
                    m = rows(f)
                    if f + 1 < NBLK:
                        keep_raw(f + 1)
                    act.wait_ge(conv_rdy, i + 3)
                    act.sem_inc(tick["act"], 1)
                    act.activation(convolved(f, b), conv[f % 2][0:m, :], ACT.Silu).then_inc(silu_rdy, 1)
                    if f < 2 * GH:
                        act.wait_ge(silu_rdy, i + 3)
                        act.wait_ge(norm_done, b * 2 * GH + f + 1)
                        act.sem_inc(tick["act"], 1)
                        act.activation(sqd[f % 2][:], convolved(f, b), ACT.Square).then_inc(sqd_rdy, 1)
            for t in range(NT):
                act.wait_ge(z_done, t + 1)
                act.activation(gate[:, t, :], zp[t % 2][:, 2 * GH:2 * GH + VD], ACT.Silu)
                act.activation(zab[:, t, :], zp[t % 2][:, 0:2 * GH], ACT.Copy).then_inc(z_rdy, 1)
            act.wait_ge(z_rdy, NT)
            act.wait_ge(gate_step, 1)
            act.activation(beta[:], beta[:], ACT.Exp, scale=-1.0).then_inc(act_step, 1)
            act.activation(a_log[:], a_log[:], ACT.Exp).then_inc(act_step, 1)
            act.wait_ge(gate_step, 3)
            act.activation(e1[:], s1[:], ACT.Exp, scale=-1.0).then_inc(act_step, 1)
            act.wait_ge(sums_done, 1)
            act.activation(decay[:].rearrange("p a t h -> p (a t h)"), sums[:, 0:3 * SMALL], ACT.Exp).then_inc(act_step, 1)
            act.wait_ge(act_step, 4)

        @block.vector
        def _(dve):
            for i in range(2):
                dve.memset(raw[i][:, 0:KCONV - 1], 0.0).then_inc(init, 1) if i else dve.memset(raw[i][:, 0:KCONV - 1], 0.0)
            dve.sem_inc(raw_rdy, 2)
            dve.sem_inc(conv_rdy, 2)
            dve.sem_inc(silu_rdy, 2)
            dve.sem_inc(norm_done, 2)
            dve.wait_ge(w_ld, 96)
            with dve.Fori(0, BATCH) as b:
                for f in range(NBLK):
                    i = b * NBLK + f
                    m = rows(f)
                    x, y = raw[f % 2], conv[f % 2][0:m, :]
                    dve.wait_ge(raw_rdy, i + 3)
                    dve.wait_ge(silu_rdy, i + 1)
                    dve.tensor_scalar(y, x[0:m, 0:SEQ], w_conv[0:m, f, 0:1], None, ALU.mult).then_inc(tap_rdy, 1)
                    for j in range(1, KCONV):
                        dve.wait_ge(tap_rdy, i * (KCONV - 1) + j)
                        dve.sem_inc(tick["dve"], 1)
                        dve.scalar_tensor_tensor(y, x[0:m, j:j + SEQ], w_conv[0:m, f, j:j + 1], y, ALU.mult, ALU.add)\
                           .then_inc(tap_rdy if j < KCONV - 1 else conv_rdy, 1)
            dve.wait_ge(norm_done, 2 * 2 * GH + 2)
            dve.tensor_copy(ssq[:], norms[:, 0:2 * GH * NT]).then_inc(ssq_rdy, 1)

            steps = 0

            def step(ins):
                nonlocal steps
                steps += 1
                ins.then_inc(gate_step, 1)
                dve.wait_ge(gate_step, steps)

            def over(row):
                return row[:].rearrange("p (o h) -> p o h", o=1).to_broadcast([P, NT, GH])

            dve.wait_ge(z_rdy, NT)
            step(dve.tensor_scalar(beta[:], zab[:, :, GH:2 * GH], -EXP_MAX, None, ALU.max))
            step(dve.tensor_tensor(za[:], zab[:, :, 0:GH], over(dt_bias), ALU.add))
            step(dve.scalar_tensor_tensor(s1[:], za[:], -1.0, za[:], ALU.mult, ALU.max))
            dve.wait_ge(act_step, 3)
            step(dve.tensor_scalar(s2[:], e1[:], 2.0, None, ALU.add))
            step(dve.reciprocal(s2[:], s2[:]))
            step(dve.tensor_tensor(s1[:], e1[:], s2[:], ALU.mult))
            step(dve.tensor_tensor(s2[:], s1[:], s1[:], ALU.mult))
            step(dve.tensor_scalar(pl[:], s2[:], 1.0 / 17, None, ALU.mult))
            for k in SERIES:
                step(dve.scalar_tensor_tensor(pl[:], pl[:], 1.0 / k, s2[:], ALU.add, ALU.mult))
            step(dve.scalar_tensor_tensor(pl[:], pl[:], 1.0, s1[:], ALU.add, ALU.mult))
            step(dve.tensor_scalar(za[:], za[:], 0.0, None, ALU.max))
            step(dve.scalar_tensor_tensor(pl[:], pl[:], 2.0, za[:], ALU.mult, ALU.add))
            step(dve.scalar_tensor_tensor(logdecay[:], pl[:], -1.0, over(a_log), ALU.mult, ALU.mult))
            assert steps == GATE_G - 1
            step(dve.tensor_scalar(logdecay[:], logdecay[:], NEG, None, ALU.max))
            step(dve.tensor_scalar(beta[:], beta[:], 1.0, None, ALU.add))
            step(dve.reciprocal(beta[:], beta[:]))

        @block.gpsimd
        def _(pool):
            pool.wait_ge(ssq_rdy, 1)
            flat = rinv[:].rearrange("p f t -> p (f t)")
            rsqrt(pool, flat, ssq[:], rs_tmp[:], 0.0, 1e-6, rinv_step, 0, tick["pool"])
            pool.wait_ge(rinv_step, RSQRT_STEPS)
            pool.tensor_scalar(rinv[:, 0:GH, :], rinv[:, 0:GH, :], float(HK) ** -0.5, None, ALU.mult).then_inc(rinv_rdy, 1)
            pool.wait_ge(rinv_rdy, 1)


def delta_chunks(nc, spare, ident, identb, qT, kT, vT, gate, beta, logdecay, rinv, decay, dram):
    with ExitStack() as ctx:
        sb, ps, sem = buffers(nc, ctx)
        tri = sb("c_tri", [P, 3, P])
        causal = sb("c_causal", [P, P], BF16)
        blocks = sb("c_blocks", [P, LEVELS, P], BF16)
        two = range(BATCH)

        def each(name, shape, dt=F32):
            return [sb(f"c_{name}{b}", shape, dt) for b in two]

        kt_in = each("kt_in", [P, GH, P])
        kq = each("kq", [P, GH, 2, P])
        vt_in = each("vt_in", [P, 2, P])
        kn = each("kn", [P, GH, P])
        kb = each("kb", [P, GH, P])
        m1 = each("m1", [P, GH, P])
        atm1 = each("atm1", [P, GH, P])
        gt = each("gt", [P, GH, P])
        at = each("at", [P, GH, P])
        mt = [spare[:, GH * P * b:GH * P * (b + 1)].rearrange("p (h t) -> p h t", h=GH) for b in two]
        bv = [spare[:, 2 * GH * P + VD * b:2 * GH * P + VD * (b + 1)].rearrange("p (h v) -> p h v", h=GH) for b in two]
        rhs = each("rhs", [P, GH, HV])
        upd = each("upd", [P, GH, HV])
        state = each("state", [P, GH, HV])
        knT, u, inv, invT, out = kt_in, kb, kt_in, gt, bv
        atm = [m1, atm1]

        g0 = [ps(f"c_g0{b}", [P, 1024]) for b in two]
        g1 = [ps(f"c_g1{b}", [P, 1024]) for b in two]

        def heads(buf):
            return buf[:, 0:GH * P].rearrange("p (h t) -> p h t", h=GH)

        def sems(name):
            return [sem(f"c_{name}{b}") for b in two]

        const_ld = sem("c_const_ld")
        init = sem("c_init")
        tile_in, turned, kn_rdy, m1_rdy, kb_rdy, kdec_rdy = (sems(x) for x in
            ("tile_in", "turned", "kn_rdy", "m1_rdy", "kb_rdy", "kdec_rdy"))
        kT_done, kT_rdy, gam_done, gt_rdy, kk_done, qk_done = (sems(x) for x in
            ("kT_done", "kT_rdy", "gam_done", "gt_rdy", "kk_done", "qk_done"))
        at_rdy, mt_rdy, atm_rdy, tt0_rdy, t0_done, t0_rdy = (sems(x) for x in
            ("at_rdy", "mt_rdy", "atm_rdy", "tt0_rdy", "t0_done", "t0_rdy"))
        u_done, u_rdy, w_done, t_rdy, tt_done, tt_rdy, ttf_rdy = (sems(x) for x in
            ("u_done", "u_rdy", "w_done", "t_rdy", "tt_done", "tt_rdy", "ttf_rdy"))
        po_done, rhs_step, d_done, d_rdy, od_done, s_step, s_rdy, o_step, out_rdy = (sems(x) for x in
            ("po_done", "rhs_step", "d_done", "d_rdy", "od_done", "s_step", "s_rdy", "o_step", "out_rdy"))
        tick = {e: sem(f"c_tick_{e}") for e in ("pe", "act", "dve", "pool")}
        LV = LEVELS - 1
        block = ctx.enter_context(nc.Block())

        @block.sync
        def _(sp):
            sp.dma_start(tri[:], dram["d_tri"]).then_inc(const_ld, 16)
            sp.dma_start(causal[:], dram["d_causal"]).then_inc(const_ld, 16)
            sp.dma_start(blocks[:], dram["d_blocks"]).then_inc(const_ld, 16)

        @block.tensor
        def _(pe):
            pe.wait_ge(const_ld, 48)
            pe.wait_ge(init, 1)
            with pe.Fori(0, TB) as i:
                for b in two:
                    pe.wait_ge(tile_in[b], i + 1)
                    pe.wait_ge(out_rdy[b], i + 1)
                    for h in range(GH):
                        pe.transpose(heads(g0[b])[:, h, :], kt_in[b][:, h, :], ident[:])
                    for c, (c0, cn) in enumerate(VB):
                        mm = pe.transpose(g1[b][:, c0:c0 + cn], vt_in[b][0:cn, c, :], ident[0:cn, 0:cn])
                    mm.then_inc(turned[b], 1)
                for b in two:
                    pe.wait_ge(kn_rdy[b], i + 1)
                    for h in range(GH):
                        mm = pe.transpose(heads(g0[b])[:, h, :], kn[b][:, h, :], ident[:])
                    mm.then_inc(kT_done[b], 1)
                    pe.wait_ge(kb_rdy[b], i + 1)
                    for h in range(GH):
                        mm = pe.transpose(heads(g1[b])[:, h, :], kb[b][:, h, :], ident[:])
                    mm.then_inc(kT_done[b], 1)
                for b in two:
                    pe.wait_ge(kT_rdy[b], i * 2 + 1)
                    pe.wait_ge(m1_rdy[b], i + 1)
                    for h0, hn in ((0, 4), (4, 2)):
                        pe.matmul(heads(g0[b])[:, h0:h0 + hn, :], identb[:],
                                  causal[:].rearrange("p (o t) -> p o t", o=1).to_broadcast([P, hn, P]),
                                  start=True, stop=False, skip_group_check=True)
                        for h in range(h0, h0 + hn):
                            mm = pe.matmul(heads(g0[b])[:, h, :], m1[b][:, h, :], tri[:, 0, :], start=False, stop=True,
                                           skip_group_check=True)
                    mm.then_inc(gam_done[b], 1)
                for b in two:
                    pe.wait_ge(kT_rdy[b], i * 2 + 2)
                    for h in range(GH):
                        mm = pe.matmul(heads(g1[b])[:, h, :], knT[b][:, h, :], kq[b][:, h, 0, :], start=True, stop=True,
                                       skip_group_check=True)
                    mm.then_inc(kk_done[b], 1)
                    pe.wait_ge(gt_rdy[b], i + 1)
                    for h in range(GH):
                        mm = pe.matmul(heads(g0[b])[:, h, :], knT[b][:, h, :], kq[b][:, h, 1, :], start=True, stop=True,
                                       skip_group_check=True)
                    mm.then_inc(qk_done[b], 1)
                for b in two:
                    pe.wait_ge(tt0_rdy[b], i + 1)
                    for h in range(GH):
                        mm = pe.transpose(heads(g1[b])[:, h, :], invT[b][:, h, :], ident[:])
                    mm.then_inc(t0_done[b], 1)
                for l in range(1, LEVELS):
                    for b in two:
                        pe.wait_ge(atm_rdy[b], i * LEVELS + l + 1)
                        if l == 1:
                            pe.wait_ge(t0_rdy[b], i + 1)
                            pe.wait_ge(mt_rdy[b], i + 1)
                        else:
                            pe.wait_ge(t_rdy[b], i * (LV - 1) + l - 1)
                            pe.wait_ge(tt_rdy[b], i * (LV - 1) + l - 1)
                        for h in range(GH):
                            mm = pe.matmul(heads(g0[b])[:, h, :], atm[l % 2][b][:, h, :], inv[b][:, h, :], start=True,
                                           stop=True, skip_group_check=True)
                        mm.then_inc(u_done[b], 1)
                    for b in two:
                        pe.wait_ge(u_rdy[b], i * LV + l)
                        for h in range(GH):
                            if l < LV:
                                mm = pe.matmul(heads(g1[b])[:, h, :], invT[b][:, h, :], u[b][:, h, :], start=True,
                                               stop=True, skip_group_check=True)
                            else:
                                mm = pe.matmul(heads(g1[b])[:, h, :], u[b][:, h, :], invT[b][:, h, :], start=True,
                                               stop=True, skip_group_check=True)
                        mm.then_inc(w_done[b], 1)
                    if l < LV:
                        for b in two:
                            pe.wait_ge(t_rdy[b], i * (LV - 1) + l)
                            for h in range(GH):
                                mm = pe.transpose(heads(g0[b])[:, h, :], inv[b][:, h, :], ident[:])
                            mm.then_inc(tt_done[b], 1)
                for b in two:
                    pe.wait_ge(ttf_rdy[b], i + 1)
                    pe.wait_ge(s_rdy[b], i + 1)
                    for a in range(2):
                        for h in range(GH):
                            mm = pe.matmul(g1[b][:, VD * a + HV * h:VD * a + HV * h + HV], kq[b][:, h, a, :],
                                           state[b][:, h, :], start=True, stop=True, skip_group_check=True)
                    mm.then_inc(po_done[b], 1)
                for b in two:
                    pe.wait_ge(rhs_step[b], i * 2 + 2)
                    for h in range(GH):
                        mm = pe.matmul(g0[b][:, HV * h:HV * h + HV], invT[b][:, h, :], rhs[b][:, h, :], start=True,
                                       stop=True, skip_group_check=True)
                    mm.then_inc(d_done[b], 1)
                for b in two:
                    pe.wait_ge(d_rdy[b], i + 1)
                    pe.wait_ge(kdec_rdy[b], i + 1)
                    for h in range(GH):
                        pe.matmul(g0[b][:, 512 + HV * h:512 + HV * h + HV], mt[b][:, h, :], upd[b][:, h, :], start=True,
                                  stop=True, skip_group_check=True)
                    for h in range(GH):
                        mm = pe.matmul(g0[b][:, 512 + VD + HV * h:512 + VD + HV * h + HV], kn[b][:, h, :],
                                       upd[b][:, h, :], start=True, stop=True, skip_group_check=True)
                    mm.then_inc(od_done[b], 1)

        @block.scalar
        def _(act):
            def keep(dst, src, done, value, rdy, func=ACT.Copy):
                act.wait_ge(done, value)
                act.activation(dst, src, func).then_inc(rdy, 1)

            with act.Fori(0, TB) as i:
                for b in two:
                    keep(knT[b][:], heads(g0[b]), kT_done[b], i * 2 + 1, kT_rdy[b])
                    keep(kq[b][:, :, 0, :], heads(g1[b]), kT_done[b], i * 2 + 2, kT_rdy[b])
                for b in two:
                    keep(gt[b][:], heads(g0[b]), gam_done[b], i + 1, gt_rdy[b], ACT.Exp)
                for b in two:
                    keep(inv[b][:], heads(g1[b]), t0_done[b], i + 1, t0_rdy[b])
                for l in range(1, LEVELS):
                    for b in two:
                        keep(u[b][:], heads(g0[b]), u_done[b], i * LV + l, u_rdy[b])
                    if l < LV:
                        for b in two:
                            keep(invT[b][:], heads(g0[b]), tt_done[b], i * (LV - 1) + l, tt_rdy[b])
                for b in two:
                    keep(upd[b][:].rearrange("p h v -> p (h v)"), g0[b][:, 0:VD], d_done[b], i + 1, d_rdy[b])

        @block.vector
        def _(dve):
            def across(small, n):
                return small.rearrange("p (h o) -> p h o", o=1).to_broadcast([P, GH, n])

            for b in two:
                mm = dve.memset(state[b][:], 0.0)
            mm.then_inc(init, 1)
            for b in two:
                dve.sem_inc(s_rdy[b], 1)
                dve.sem_inc(out_rdy[b], 1)
            dve.wait_ge(const_ld, 48)
            with dve.Fori(0, TB) as i:
                for b in two:
                    t0 = i * P + b * SEQ
                    dve.tensor_copy(kq[b][:, :, 1, :], qT[:, :, bass.ds(t0, P)])
                    dve.tensor_copy(vt_in[b][:], vT[:, :, bass.ds(t0, P)])
                    dve.tensor_copy(kt_in[b][:], kT[:, :, bass.ds(t0, P)]).then_inc(tile_in[b], 1)
                for b in two:
                    t = i + b * TB
                    small = lambda x: x.rearrange("p a h -> p (a h)")
                    dve.wait_ge(turned[b], i + 1)
                    dve.tensor_tensor(bv[b], g1[b][:, 0:VD].rearrange("p (h v) -> p h v", h=GH),
                                      across(small(beta[:, bass.ds(t, 1), :]), HV), ALU.mult)
                    dve.tensor_tensor(kn[b][:], heads(g0[b]),
                                      across(rinv[:, GH:2 * GH, bass.ds(t, 1)].rearrange("p h a -> p (h a)"), P),
                                      ALU.mult).then_inc(kn_rdy[b], 1)
                for b in two:
                    dve.wait_ge(gt_rdy[b], i + 1)
                    dve.wait_ge(kk_done[b], i + 1)
                    dve.tensor_tensor(at[b][:], heads(g1[b]), gt[b][:], ALU.mult).then_inc(at_rdy[b], 1)
                    dve.wait_ge(qk_done[b], i + 1)
                    dve.tensor_tensor(mt[b], heads(g0[b]), gt[b][:], ALU.mult).then_inc(mt_rdy[b], 1)
                for b in two:
                    dve.wait_ge(mt_rdy[b], i + 1)
                    dve.wait_ge(atm_rdy[b], i * LEVELS + 1)
                    dve.tensor_tensor(invT[b][:], ident[:].rearrange("p (o t) -> p o t", o=1).to_broadcast([P, GH, P]),
                                      atm[0][b][:], ALU.subtract).then_inc(tt0_rdy[b], 1)
                for l in range(1, LV):
                    for b in two:
                        dve.wait_ge(w_done[b], i * LV + l)
                        dve.tensor_tensor(inv[b][:], inv[b][:], heads(g1[b]), ALU.subtract).then_inc(t_rdy[b], 1)
                for b in two:
                    dve.wait_ge(w_done[b], i * LV + LV)
                    dve.tensor_tensor(invT[b][:], invT[b][:], heads(g1[b]), ALU.subtract).then_inc(ttf_rdy[b], 1)
                small = lambda x: x.rearrange("p a h -> p (a h)")
                for b in two:
                    t = i + b * TB
                    upto = across(small(decay[:, 0, bass.ds(t, 1), :]), HV)
                    whole = across(small(decay[:, 2, bass.ds(t, 1), :]), HV)
                    po = g1[b][:, 0:2 * VD].rearrange("p (a h v) -> p a h v", a=2, h=GH)
                    dve.wait_ge(po_done[b], i + 1)
                    dve.tensor_tensor(rhs[b][:], po[:, 0], upto, ALU.mult).then_inc(rhs_step[b], 1)
                    dve.wait_ge(rhs_step[b], i * 2 + 1)
                    dve.tensor_tensor(rhs[b][:], bv[b], rhs[b][:], ALU.subtract).then_inc(rhs_step[b], 1)
                    dve.tensor_tensor(state[b][:], state[b][:], whole, ALU.mult).then_inc(s_step[b], 1)
                    dve.wait_ge(rhs_step[b], i * 2 + 2)
                    dve.tensor_tensor(out[b], po[:, 1], upto, ALU.mult).then_inc(o_step[b], 1)
                for b in two:
                    t = i + b * TB
                    od = g0[b][:, 512:512 + 2 * VD].rearrange("p (a h v) -> p a h v", a=2, h=GH)
                    dve.wait_ge(od_done[b], i + 1)
                    dve.wait_ge(s_step[b], i + 1)
                    dve.tensor_tensor(state[b][:], state[b][:], od[:, 1], ALU.add).then_inc(s_rdy[b], 1)
                    dve.wait_ge(o_step[b], i * 3 + 1)
                    dve.tensor_tensor(out[b], out[b], od[:, 0], ALU.add).then_inc(o_step[b], 1)
                    dve.wait_ge(o_step[b], i * 3 + 2)
                    dve.tensor_tensor(out[b], out[b],
                                      across(rinv[:, 0:GH, bass.ds(t, 1)].rearrange("p h a -> p (h a)"), HV),
                                      ALU.mult).then_inc(o_step[b], 1)
                    dve.wait_ge(o_step[b], i * 3 + 3)
                    gt_tile = gate[:, bass.ds(t, 1), :].rearrange("p a f -> p (a f)")
                    dve.tensor_tensor(gt_tile, out[b].rearrange("p h v -> p (h v)"), gt_tile, ALU.mult)\
                       .then_inc(out_rdy[b], 1)
            for b in two:
                dve.wait_ge(out_rdy[b], TB + 1)

        @block.gpsimd
        def _(pool):
            def across(small):
                return small.rearrange("p a h -> p (a h)").rearrange("p (h o) -> p h o", o=1).to_broadcast([P, GH, P])

            def over(mask):
                return mask.rearrange("p (o t) -> p o t", o=1).to_broadcast([P, GH, P])

            pool.wait_ge(const_ld, 48)
            with pool.Fori(0, TB) as i:
                for b in two:
                    t = i + b * TB
                    pool.wait_ge(u_done[b], i * LV)
                    pool.sem_inc(tick["pool"], 1)
                    pool.tensor_tensor(m1[b][:], over(tri[:, 1, :]), across(logdecay[:, bass.ds(t, 1), :]),
                                       ALU.mult).then_inc(m1_rdy[b], 1)
                for b in two:
                    t = i + b * TB
                    pool.wait_ge(kn_rdy[b], i + 1)
                    pool.sem_inc(tick["pool"], 1)
                    pool.tensor_tensor(kb[b][:], kn[b][:], across(beta[:, bass.ds(t, 1), :]), ALU.mult).then_inc(kb_rdy[b], 1)
                for b in two:
                    t = i + b * TB
                    pool.wait_ge(kT_done[b], i * 2 + 1)
                    pool.wait_ge(kb_rdy[b], i + 1)
                    pool.sem_inc(tick["pool"], 1)
                    pool.tensor_tensor(kn[b][:], kn[b][:], across(decay[:, 1, bass.ds(t, 1), :]), ALU.mult)\
                        .then_inc(kdec_rdy[b], 1)
                for l in range(LEVELS):
                    for b in two:
                        if l == 0:
                            pool.wait_ge(at_rdy[b], i + 1)
                        elif l == 2:
                            pool.wait_ge(tt0_rdy[b], i + 1)
                        elif l > 2:
                            pool.wait_ge(u_done[b], i * LV + l - 2)
                        pool.tensor_tensor(atm[l % 2][b][:], at[b][:], over(blocks[:, l, :]), ALU.mult)\
                            .then_inc(atm_rdy[b], 1)


def delta_outputs(nc, x, ident, og, dram):
    with ExitStack() as ctx:
        sb, ps, sem = buffers(nc, ctx)
        nw = sb("o_nw", [P, VD])
        wo = sb("o_wo", [P, len(VB), D])
        sq = [sb(f"o_sq{i}", [P, VD]) for i in range(2)]
        ms = sb("o_ms", [P, NT])
        rstd = sb("o_rstd", [P, NT])
        tmp = sb("o_tmp", [P, NT])
        on = [sb(f"o_on{i}", [P, VD]) for i in range(2)]
        oT = [sb(f"o_oT{i}", [P, len(VB), P]) for i in range(2)]
        tp = [ps(f"o_tp{i}", [P, 512]) for i in range(2)]
        yp = [ps(f"o_yp{i}", [P, 512]) for i in range(2)]
        x_ld, w_ld, ms_rdy, rs_rdy, on_rdy, tp_done, oT_rdy, y_done, x_rdy, tick = (sem("o_" + s) for s in (
            "x_ld", "w_ld", "ms_rdy", "rs_rdy", "on_rdy", "tp_done", "oT_rdy", "y_done", "x_rdy", "tick"))
        block = ctx.enter_context(nc.Block())

        @block.sync
        def _(sp):
            sp.dma_start(nw[:], dram["d_nw"].broadcast_to([P, VD])).then_inc(w_ld, 16)
            sp.dma_start(wo[:], dram["d_wo"]).then_inc(w_ld, 16)

        @block.scalar
        def _(act):
            act.dma_start(x[:], dram["x"].rearrange("(t p) d -> p t d", p=P)).then_inc(x_ld, 16)
            for t in range(NT):
                if t >= 2:
                    act.wait_ge(ms_rdy, t - 1)
                act.activation(sq[t % 2][:], og[:, t, :], ACT.Square, scale=float(VD) ** -0.5, accum_out=ms[:, t:t + 1]).then_inc(ms_rdy, 1)
            for t in range(NT):
                act.wait_ge(tp_done, t + 1)
                for c, (c0, cn) in enumerate(VB):
                    last = act.activation(oT[t % 2][0:cn, c, :], tp[t % 2][0:cn, P * c:P * c + P], ACT.Copy)
                last.then_inc(oT_rdy, 1)

        @block.gpsimd
        def _(pool):
            pool.wait_ge(ms_rdy, NT)
            rsqrt(pool, rstd[:], ms[:], tmp[:], 0.0, 1e-5, rs_rdy, 0, tick)

        @block.vector
        def _(dve):
            dve.wait_ge(w_ld, 32)
            dve.wait_ge(rs_rdy, RSQRT_STEPS)
            dve.wait_ge(x_ld, 16)
            for t in range(NT):
                if t >= 2:
                    dve.wait_ge(tp_done, t - 1)
                dve.scalar_tensor_tensor(on[t % 2][:], og[:, t, :], rstd[:, t:t + 1], nw[:], ALU.mult, ALU.mult).then_inc(on_rdy, 1)
                if t >= 1:
                    dve.wait_ge(y_done, t)
                    dve.tensor_tensor(x[:, t - 1, :], x[:, t - 1, :], yp[(t - 1) % 2][:, 0:D], ALU.add).then_inc(x_rdy, 1)
            dve.wait_ge(y_done, NT)
            dve.tensor_tensor(x[:, NT - 1, :], x[:, NT - 1, :], yp[(NT - 1) % 2][:, 0:D], ALU.add).then_inc(x_rdy, 1)
            dve.wait_ge(x_rdy, NT)

        @block.tensor
        def _(pe):
            pe.wait_ge(w_ld, 32)
            for t in range(NT):
                pe.wait_ge(on_rdy, t + 1)
                if t >= 2:
                    pe.wait_ge(oT_rdy, t - 1)
                for c, (c0, cn) in enumerate(VB):
                    mm = pe.transpose(tp[t % 2][0:cn, P * c:P * c + P], on[t % 2][:, c0:c0 + cn], ident[:])
                mm.then_inc(tp_done, 1)
                pe.wait_ge(oT_rdy, t + 1)
                if t >= 2:
                    pe.wait_ge(x_rdy, t - 1)
                for c, (c0, cn) in enumerate(VB):
                    mm = pe.matmul(yp[t % 2][:, 0:D], oT[t % 2][0:cn, c, :], wo[0:cn, c, :], start=(c == 0), stop=(c == 1))
                mm.then_inc(y_done, 1)


def delta_constants():
    r, t = np.arange(P)[:, None], np.arange(P)[None, :]
    tri = np.stack([r <= t, r > t, np.ones((P, P), bool)], 1).astype(np.float32)
    causal = np.where(t < r, np.float32(NEG), np.float32(0))
    blocks = np.stack([(r // (2 * n) == t // (2 * n)) & (t % (2 * n) >= n) & (r % (2 * n) < n)
                       for n in (1 << l for l in range(LEVELS))], 1).astype(np.float32)
    return np.ascontiguousarray(tri), causal, np.ascontiguousarray(blocks)


def pack_delta_weights(q_w, k_w, v_w, a_w, b_w, g_w, o_w, conv_q_w, conv_k_w, conv_v_w):
    w_qkv = np.ascontiguousarray(np.concatenate([q_w, k_w, v_w], 0).T)
    w_abg = np.ascontiguousarray(np.concatenate([a_w, b_w, g_w], 0).T)
    conv = np.zeros((NBLK * P, KCONV), np.float32)
    conv[0:2 * KD + VD] = np.concatenate([conv_q_w, conv_k_w, conv_v_w], 0)
    wo = np.zeros((len(VB) * P, D), np.float32)
    wo[0:VD] = o_w.T
    return (w_qkv, w_abg, np.ascontiguousarray(conv.reshape(NBLK, P, KCONV).transpose(1, 0, 2)),
            np.ascontiguousarray(wo.reshape(len(VB), P, D).transpose(1, 0, 2)))

DEPTH, HEADS, DH, WIN = 6, 16, 64, 32
INNER = HEADS * DH
DFF = int(D * 4 * 2 / 3)
HP = HEADS // 2
NWIN = P // WIN
FB = [(0, 128), (128, 128), (256, DFF - 256)]
C_QKV, C_WO = 0, 3 * INNER
C_W1 = C_WO + HP * D
C_W2 = C_W1 + 2 * DFF
C_B1 = C_W2 + len(FB) * D
C_LN = C_B1 + 2 * len(FB)
NWC = C_LN + 2
PADK = P - WIN


def local_layers(nc, h, ident, identb, dram):
    with ExitStack() as ctx:
        sb, ps, sem = buffers(nc, ctx)

        wts = [sb(f"l_wts{i}", [P, NWC]) for i in range(2)]
        scales = [sb(f"l_scales{i}", [P, 4, DH]) for i in range(2)]
        b2row = [sb(f"l_b2row{i}", [1, D]) for i in range(2)]
        raw_tab = sb("l_raw_tab", [P, 4, TB, DH])
        tab = sb("l_tab", [P, 4, NT, DH])
        maskb = sb("l_maskb", [P, NT, 2 * WIN], BF16)
        carried = sb("l_carried", [P, NT])
        ones_row = sb("l_ones_row", [1, P])
        hcur = [sb(f"l_hcur{i}", [P, D]) for i in range(2)]
        xs = [sb(f"l_xs{i}", [P, 1 + P]) for i in range(2)]
        sq = sb("l_sq", [P, 2, 512])
        ss = sb("l_ss", [P, 2 * HEADS])
        rn = sb("l_rn", [P, 2 * HEADS])
        rn_tmp = sb("l_rn_tmp", [P, 2 * HEADS])
        rot_a = sb("l_rot_a", [P, 4, 512])
        rot_b = sb("l_rot_b", [P, 4, 512])
        qk = sb("l_qk", [P, 4, 512])
        qT = [sb(f"l_qT{i}", [P, HP, P]) for i in range(2)]
        kT = [sb(f"l_kT{i}", [P, HP, WIN + P]) for i in range(2)]
        v = [sb(f"l_v{i}", [P, HEADS, DH + 1]) for i in range(2)]
        vprev = sb("l_vprev", [P, HEADS, DH + 1])
        mx = sb("l_mx", [P, HEADS])
        sd = sb("l_sd", [P, HEADS, 2 * WIN])
        pw = sb("l_pw", [P, HEADS, 2 * P])
        pT = sb("l_pT", [P, HEADS, P])
        pTp = sb("l_pTp", [P, HEADS, WIN])
        rsum = sb("l_rsum", [P, HEADS])
        on = sb("l_on", [P, HEADS, DH])
        oT = sb("l_oT", [P, HP, P])
        GT = 4
        hgrp = sb("l_hgrp", [P, GT, D])
        xs4 = [sb(f"l_xs4{i}", [P, 1 + GT * P]) for i in range(2)]
        st = sb("l_st", [P, GT, 6])
        mv = sb("l_mv", [P, GT, 2])
        rstd = sb("l_rstd", [P, GT])
        rstd_tmp = sb("l_rstd_tmp", [P, GT])
        xn = sb("l_xn", [P, GT, D])
        xnT = sb("l_xnT", [P, GT * P])
        gl = sb("l_gl", [P, 3, 512])
        u = sb("l_u", [P, 3, 512])

        bank = [ps(f"l_bank{i}", [P, 512]) for i in range(2)]
        score = ps("l_score", [P, HEADS, 2 * WIN])
        tp = [ps(f"l_tp{i}", [P, 512]) for i in range(2)]
        misc = [ps(f"l_misc{i}", [P, 512]) for i in range(2)]

        const_ld = sem("l_const_ld")
        init = sem("l_init")
        w_ld = [sem(f"l_w_ld{i}") for i in range(2)]
        layer_done = sem("l_layer_done")
        tab_rdy = sem("l_tab_rdy")
        hcur_rdy = sem("l_hcur_rdy")
        xT_done = sem("l_xT_done")
        xs_rdy = sem("l_xs_rdy")
        carry_rdy = sem("l_carry_rdy")
        proj_done = sem("l_proj_done")
        sq_rdy = sem("l_sq_rdy")
        v_rdy = sem("l_v_rdy")
        ss_rdy = sem("l_ss_rdy")
        rope_rdy = sem("l_rope_rdy")
        rn_rdy = sem("l_rn_rdy")
        rot_sum = sem("l_rot_sum")
        qk_rdy = sem("l_qk_rdy")
        qkT_done = sem("l_qkT_done")
        qkT_rdy = sem("l_qkT_rdy")
        kprev_rdy = sem("l_kprev_rdy")
        s_done = sem("l_s_done")
        mx_rdy = sem("l_mx_rdy")
        sd_rdy = sem("l_sd_rdy")
        p_rdy = sem("l_p_rdy")
        pT_done = sem("l_pT_done")
        pT_rdy = sem("l_pT_rdy")
        pv_done = sem("l_pv_done")
        vprev_rdy = sem("l_vprev_rdy")
        rs_rdy = sem("l_rs_rdy")
        on_rdy = sem("l_on_rdy")
        oT_done = sem("l_oT_done")
        oT_rdy = sem("l_oT_rdy")
        y_done = sem("l_y_done")
        h_rdy = sem("l_h_rdy")
        g_hgrp = sem("l_g_hgrp")
        g_xT = sem("l_g_xT")
        g_xs = sem("l_g_xs")
        g_back = sem("l_g_back")
        g_st = sem("l_g_st")
        g_mv = sem("l_g_mv")
        g_rstd = sem("l_g_rstd")
        g_xn = sem("l_g_xn")
        g_xnT = sem("l_g_xnT")
        g_xnT_rdy = sem("l_g_xnT_rdy")
        g_w1 = sem("l_g_w1")
        g_gl = sem("l_g_gl")
        g_u = sem("l_g_u")
        g_y = sem("l_g_y")
        g_h = sem("l_g_h")
        tick = {e: sem(f"l_tick_{e}") for e in ("pe", "act", "dve", "pool")}

        PAIRS = DEPTH // 2
        block = ctx.enter_context(nc.Block())

        def by_layer(eng, attention, geglu):
            with eng.Fori(0, PAIRS) as lp:
                for par in range(2):
                    attention(lp, par, lp * (2 * NT) + par * NT)
                    geglu(lp, par, lp * 8 + par * 4)

        def slot(head):
            return HP * (head % 2) + head // 2

        def by_tile(eng, front, back, n0):
            front(0, n0, 0)
            with eng.Fori(0, NT // 2 - 1) as j:
                back(j * 2, n0 + j * 2, 0, front=(j * 2 + 1, n0 + j * 2 + 1, 1))
                back(j * 2 + 1, n0 + j * 2 + 1, 1, front=(j * 2 + 2, n0 + j * 2 + 2, 0))
            back(NT - 2, n0 + NT - 2, 0, front=(NT - 1, n0 + NT - 1, 1))
            back(NT - 1, n0 + NT - 1, 1, front=None)

        @block.sync
        def _(sp):
            sp.dma_start(raw_tab[:], dram["l_tables"]).then_inc(const_ld, 16)
            sp.dma_start(maskb[:], dram["l_mask"]).then_inc(const_ld, 16)
            sp.dma_start(carried[:], dram["l_carried"]).then_inc(const_ld, 16)
            with sp.Fori(0, PAIRS) as lp:
                for par in range(2):
                    sp.wait_ge(layer_done, lp * 2 + par + 1)
                    sp.dma_start(wts[par][:], dram["l_wts"][bass.ds(lp * 2 + par, 1)].rearrange("a p n -> (a p) n")).then_inc(w_ld[par], 16)
                    sp.dma_start(scales[par][:].rearrange("p a d -> p (a d)"),
                                 dram["l_scales"][bass.ds(lp * 2 + par, 1)].broadcast_to([P, 4 * DH])).then_inc(w_ld[par], 16)
                    sp.dma_start(b2row[par][:], dram["l_b2"][bass.ds(lp * 2 + par, 1)]).then_inc(w_ld[par], 16)

        @block.tensor
        def _(pe):
            def attention(lp, par, n0):
                w = wts[par]

                def scores(t, n, p):
                    pe.wait_ge(qkT_rdy, n * 4 + 4)
                    pe.wait_ge(kprev_rdy, n + 1)
                    for c in range(2):
                        pe.matmul(score[:, 8 * c:8 * c + 8, :], identb[:],
                                  maskb[:, bass.ds(t, 1), :].to_broadcast([P, 8, 2 * WIN]),
                                  start=True, stop=False, skip_group_check=True)
                    for wd in range(NWIN):
                        for hh in range(HEADS):
                            r = slice(DH * (hh % 2), DH * (hh % 2) + DH)
                            last = pe.matmul(score[WIN * wd:WIN * wd + WIN, slot(hh), :],
                                             qT[p][r, hh // 2, WIN * wd:WIN * wd + WIN],
                                             kT[p][r, hh // 2, WIN * wd:WIN * wd + 2 * WIN],
                                             start=False, stop=True, skip_group_check=True)
                    last.then_inc(s_done, 1)

                def project(n, p):
                    pe.wait_ge(hcur_rdy, n + 1)
                    pe.transpose(misc[0][:, 0:P], hcur[p][:], ident[:]).then_inc(xT_done, 1)
                    for j in range(6):
                        if j == 0:
                            pe.wait_ge(carry_rdy, n + 1)
                            pe.wait_ge(xs_rdy, n + 2)
                        if 2 <= j < 6:
                            pe.wait_ge(rope_rdy, n * 4 + j)
                        if j < 2:
                            pe.wait_ge(v_rdy, n * 2 + j + 1)
                        else:
                            pe.wait_ge(sq_rdy, n * 4 + j - 1)
                        pe.matmul(bank[j % 2][:], xs[p][:, 0:P], w[:, C_QKV + 512 * j:C_QKV + 512 * j + 512],
                                  start=True, stop=True).then_inc(proj_done, 1)

                def turn_probs(m):
                    pe.wait_ge(p_rdy, m + 1)
                    pe.sem_inc(tick["pe"], 1)
                    for hh in range(HEADS):
                        last = pe.transpose(score[:, 0:8, :].rearrange("p a b -> p (a b)")[:, WIN * hh:WIN * hh + WIN],
                                            pw[0:WIN, hh, 0:P], ident[0:WIN, 0:WIN])
                    last.then_inc(pT_done, 1)
                    for c in range(4):
                        if c >= 2:
                            pe.wait_ge(pT_rdy, m * 5 + c)
                        for k in range(4):
                            last = pe.transpose(tp[c % 2][:, P * k:P * k + P], pw[:, 4 * c + k, P:2 * P], ident[:])
                        last.then_inc(pT_done, 1)

                def values(m, p):
                    pe.wait_ge(vprev_rdy, m + 1)
                    pe.wait_ge(v_rdy, m * 2 + 4)
                    for c in range(4):
                        pe.wait_ge(pT_rdy, m * 5 + 2 + c)
                        if c == 0:
                            pe.wait_ge(h_rdy, m + 1)
                        if c >= 2:
                            pe.wait_ge(on_rdy, m * 4 + c - 1)
                        o = misc[(c + 1) % 2]
                        for k in range(4):
                            s = 4 * c + k
                            hh = 2 * (s % HP) + s // HP
                            pe.matmul(o[:, 65 * k:65 * k + 65], pT[:, s, :], v[p][:, hh, :],
                                      start=True, stop=False, skip_group_check=True)
                            last = pe.matmul(o[0:WIN, 65 * k:65 * k + 65], pTp[PADK:P, s, :], vprev[PADK:P, hh, :],
                                             start=False, stop=True, skip_group_check=True)
                        last.then_inc(pv_done, 1)

                def output(m):
                    for c in range(2):
                        pe.wait_ge(on_rdy, m * 4 + 3 + c)
                        for k in range(4):
                            last = pe.transpose(misc[(c + 1) % 2][:, P * k:P * k + P],
                                                on[:, 8 * c + 2 * k:8 * c + 2 * k + 2, :].rearrange("p a d -> p (a d)"),
                                                ident[:])
                        last.then_inc(oT_done, 1)
                    pe.wait_ge(oT_rdy, m * 2 + 2)
                    for k in range(HP):
                        last = pe.matmul(misc[1][:, 0:D], oT[:, k, :], w[:, C_WO + D * k:C_WO + D * k + D],
                                         start=(k == 0), stop=(k == HP - 1))
                    last.then_inc(y_done, 1)

                def turn_qk(n):
                    for c in range(4):
                        pe.wait_ge(qk_rdy, n * 4 + c + 1 + 4)
                        if c >= 2:
                            pe.wait_ge(qkT_rdy, n * 4 + c - 1)
                        for k in range(4):
                            last = pe.transpose(tp[c % 2][:, P * k:P * k + P], qk[:, c, P * k:P * k + P], ident[:])
                        last.then_inc(qkT_done, 1)

                def front(t, n, p):
                    project(n, p)
                    turn_qk(n)

                def back(t, m, p, front):
                    scores(t, m, p)
                    if front:
                        project(front[1], front[2])
                    turn_probs(m)
                    values(m, p)
                    output(m)
                    if front:
                        turn_qk(front[1])

                pe.wait_ge(w_ld[par], lp * 48 + 48)
                if par == 0:
                    pe.wait_ge(const_ld, 48)
                    pe.wait_ge(init, 1)
                by_tile(pe, front, back, n0)

            def geglu(lp, par, k0):
                w = wts[par]
                with pe.Fori(0, BATCH) as b:
                    for g in range(2):
                        k = k0 + b * 2 + g
                        pe.wait_ge(g_hgrp, k + 1)
                        for i in range(GT):
                            last = pe.transpose(bank[g][:, P * i:P * i + P], hgrp[:, i, :], ident[:])
                        last.then_inc(g_xT, 1)
                        pe.wait_ge(g_xs, k * 3 + 4)
                        for i in range(GT):
                            last = pe.transpose(tp[g][:, P * i:P * i + P], xs4[g][:, P * i:P * i + P], ident[:])
                        last.then_inc(g_back, 1)
                        pe.wait_ge(g_xn, k * 4 + 4)
                        for i in range(GT):
                            last = pe.transpose(bank[g][:, P * i:P * i + P], xn[:, i, :], ident[:])
                        last.then_inc(g_xnT, 1)
                        pe.wait_ge(g_xnT_rdy, k + 1)
                        wb = [misc[0], misc[1], tp[1 - g]]
                        for half in range(2):
                            for i, (c0, cn) in enumerate(FB):
                                if half == 0:
                                    pe.wait_ge(g_u, k * 3 + i + 1)
                                else:
                                    pe.wait_ge(g_gl, k * 3 + i + 1)
                                c = C_W1 + (DFF if half == 0 else 0) + c0
                                pe.matmul(wb[i][0:cn, :], w[:, c:c + cn], xnT[:], start=True, stop=True).then_inc(g_w1, 1)
                        pe.wait_ge(g_u, k * 3 + 6)
                        for i in range(GT):
                            y = bank[g][:, D * i:D * i + D]
                            pe.matmul(y, ones_row[:], b2row[par][:], start=True, stop=False, skip_group_check=True)
                            for f, (c0, cn) in enumerate(FB):
                                last = pe.matmul(y, u[0:cn, f, P * i:P * i + P], w[0:cn, C_W2 + D * f:C_W2 + D * f + D],
                                                 start=False, stop=(f == len(FB) - 1), skip_group_check=True)
                        last.then_inc(g_y, 1)

            by_layer(pe, attention, geglu)

        @block.scalar
        def _(act):
            def attention(lp, par, n0):
                def shift(t, n, p):
                    act.wait_ge(xs_rdy, n + 1)
                    act.sem_inc(tick["act"], 1)
                    act.activation(xs[p][DH:P, 0:1], xs[1 - p][DH:P, P:P + 1], ACT.Copy,
                                   scale=carried[DH:P, bass.ds(t, 1)]).then_inc(carry_rdy, 1)
                    act.wait_ge(xT_done, n + 1)
                    act.activation(xs[p][0:DH, 0:P], misc[0][0:DH, 0:P], ACT.Copy)
                    act.activation(xs[p][DH:P, 1:1 + P], misc[0][DH:P, 0:P], ACT.Copy).then_inc(xs_rdy, 1)

                def square(n, j):
                    act.wait_ge(proj_done, n * 6 + j + 1)
                    act.wait_ge(ss_rdy, n * 4 + j + 1)
                    act.activation(sq[:, j % 2, :], bank[j % 2][:], ACT.Square).then_inc(sq_rdy, 1)

                def keep_v(n, p, j):
                    act.wait_ge(proj_done, n * 6 + j + 1)
                    act.wait_ge(vprev_rdy, n)
                    act.activation(v[p][:, 8 * (j - 4):8 * (j - 4) + 8, 0:DH],
                                   bank[j % 2][:].rearrange("p (a d) -> p a d", d=DH), ACT.Copy).then_inc(v_rdy, 1)

                def exps(m, wd):
                    if wd == 0:
                        act.wait_ge(sd_rdy, m + 1)
                    r = slice(WIN * wd, WIN * wd + WIN)
                    e = act.activation(pw[r, :, PADK + WIN * wd:PADK + WIN * wd + 2 * WIN], sd[r, :, :], ACT.Exp)
                    if wd == NWIN - 1:
                        e.then_inc(p_rdy, 1)

                def keep_pT(m):
                    act.wait_ge(pT_done, m * 5 + 1)
                    act.wait_ge(pv_done, m * 4 + 1)
                    act.activation(pTp[PADK:P, :, :], score[PADK:P, 0:8, :].rearrange("p a (c w) -> p (a c) w", w=WIN),
                                   ACT.Copy).then_inc(pT_rdy, 1)
                    for c in range(4):
                        act.wait_ge(pT_done, m * 5 + 2 + c)
                        act.activation(pT[:, 4 * c:4 * c + 4, :], tp[c % 2][:].rearrange("p (a q) -> p a q", q=P),
                                       ACT.Copy).then_inc(pT_rdy, 1)

                def keep_oT(m):
                    for c in range(2):
                        act.wait_ge(oT_done, m * 2 + c + 1)
                        act.activation(oT[:, 4 * c:4 * c + 4, :], misc[(c + 1) % 2][:].rearrange("p (a q) -> p a q", q=P),
                                       ACT.Copy).then_inc(oT_rdy, 1)

                def keep_qkT(n, p):
                    for c in range(4):
                        act.wait_ge(qkT_done, n * 4 + c + 1)
                        src = tp[c % 2][:].rearrange("p (a q) -> p a q", q=P)
                        dst = qT[p][:, 4 * c:4 * c + 4, :] if c < 2 else kT[p][:, 4 * (c - 2):4 * (c - 2) + 4, WIN:WIN + P]
                        act.activation(dst, src, ACT.Copy).then_inc(qkT_rdy, 1)

                def front(t, n, p):
                    shift(t, n, p)
                    for j in range(4):
                        square(n, j)
                    keep_v(n, p, 4)
                    keep_v(n, p, 5)
                    keep_qkT(n, p)

                def back(t, m, p, front):
                    if front:
                        shift(*front)
                        square(front[1], 0)
                        square(front[1], 1)
                    exps(m, 0)
                    exps(m, 1)
                    if front:
                        square(front[1], 2)
                    exps(m, 2)
                    exps(m, 3)
                    if front:
                        square(front[1], 3)
                        keep_v(front[1], front[2], 4)
                        keep_v(front[1], front[2], 5)
                    keep_pT(m)
                    keep_oT(m)
                    if front:
                        keep_qkT(front[1], front[2])

                if par == 0:
                    act.wait_ge(const_ld, 48)
                    act.wait_ge(init, 1)
                by_tile(act, front, back, n0)

            def geglu(lp, par, k0):
                w = wts[par]
                act.wait_ge(w_ld[par], lp * 48 + 48)
                act.sem_inc(tick["act"], 1)
                with act.Fori(0, BATCH) as b:
                    for g in range(2):
                        k = k0 + b * 2 + g
                        act.wait_ge(g_xT, k + 1)
                        act.activation(xs4[g][0:DH, 0:GT * P], bank[g][0:DH, :], ACT.Copy).then_inc(g_xs, 1)
                        act.activation(xs4[g][DH:P, 1:1 + GT * P], bank[g][DH:P, :], ACT.Copy).then_inc(g_xs, 1)
                        if g == 0:
                            act.sem_inc(g_xs, 1)
                        else:
                            act.wait_ge(g_xs, k * 3 + 1)
                            act.sem_inc(tick["act"], 1)
                            act.activation(xs4[1][DH:P, 0:1], xs4[0][DH:P, GT * P:GT * P + 1], ACT.Copy).then_inc(g_xs, 1)
                        act.wait_ge(g_xnT, k + 1)
                        act.activation(xnT[:], bank[g][:], ACT.Identity, scale=w[:, C_LN:C_LN + 1],
                                       bias=w[:, C_LN + 1:C_LN + 2]).then_inc(g_xnT_rdy, 1)
                        wb = [misc[0], misc[1], tp[1 - g]]
                        for i, (c0, cn) in enumerate(FB):
                            act.wait_ge(g_w1, k * 6 + i + 1)
                            act.activation(gl[0:cn, i, :], wb[i][0:cn, :], ACT.Gelu,
                                           bias=w[0:cn, C_B1 + i:C_B1 + i + 1]).then_inc(g_gl, 1)

            by_layer(act, attention, geglu)

        @block.vector
        def _(dve):
            def attention(lp, par, n0):
                def rope(t, n, j):
                    src = bank[j % 2][:]
                    tb = 2 * (j // 2)
                    dve.wait_ge(qk_rdy, n * 4 + j + 1)
                    dve.wait_ge(sq_rdy, n * 4 + j + 1)
                    dve.tensor_reduce(ss[:, 8 * j:8 * j + 8], sq[:, j % 2, :].rearrange("p (a d) -> p a d", d=DH),
                                      AX, ALU.add).then_inc(ss_rdy, 1)
                    dve.tensor_tensor(rot_a[:, j, :].rearrange("p (a d) -> p a d", d=DH),
                                      src.rearrange("p (a d) -> p a d", d=DH),
                                      tab[:, tb, bass.ds(t, 1), :].to_broadcast([P, 8, DH]), ALU.mult)
                    swapped = src.rearrange("p (a e d) -> p a e d", a=8, e=2)[:, :, ::-1, :]
                    sins = tab[:, tb + 1, bass.ds(t, 1), :].rearrange("p a (e d) -> p a e d", e=2)
                    dve.tensor_tensor(rot_b[:, j, :].rearrange("p (a e d) -> p a e d", a=8, e=2), swapped,
                                      sins.to_broadcast([P, 8, 2, DH // 2]), ALU.mult).then_inc(rope_rdy, 1)

                def soft_shift(m):
                    dve.wait_ge(s_done, m + 1)
                    dve.tensor_reduce(mx[:], score[:], AX, ALU.max).then_inc(mx_rdy, 1)
                    dve.wait_ge(mx_rdy, m + 1)
                    dve.tensor_tensor(sd[:], score[:], mx[:].rearrange("p (a o) -> p a o", o=1).to_broadcast([P, HEADS, 2 * WIN]),
                                      ALU.subtract).then_inc(sd_rdy, 1)

                def normalise(m):
                    for c in range(4):
                        o = misc[(c + 1) % 2][:, 0:260].rearrange("p (a d) -> p a d", d=DH + 1)
                        dve.wait_ge(pv_done, m * 4 + c + 2)
                        dve.reciprocal(rsum[:, 4 * c:4 * c + 4], o[:, :, DH]).then_inc(rs_rdy, 1)
                        dve.wait_ge(rs_rdy, m * 4 + c + 1)
                        dve.tensor_tensor(on[:].rearrange("p (a e) d -> p a e d", e=2)[:, 4 * (c % 2):4 * (c % 2) + 4, c // 2, :],
                                          o[:, :, 0:DH],
                                          rsum[:, 4 * c:4 * c + 4].rearrange("p (a o) -> p a o", o=1).to_broadcast([P, 4, DH]),
                                          ALU.mult).then_inc(on_rdy, 1)

                def add_back(t, m):
                    dve.wait_ge(y_done, m + 1)
                    dve.tensor_tensor(h[:, bass.ds(t, 1), :].rearrange("p a d -> p (a d)"), misc[1][:, 0:D],
                                      h[:, bass.ds(t, 1), :].rearrange("p a d -> p (a d)"), ALU.add).then_inc(h_rdy, 1)

                def front(t, n, p):
                    for j in range(4):
                        rope(t, n, j)

                def back(t, m, p, front):
                    soft_shift(m)
                    if front:
                        for j in range(4):
                            rope(front[0], front[1], j)
                    normalise(m)
                    add_back(t, m)

                dve.wait_ge(tab_rdy, lp * 8 + par * 4 + 4)
                dve.sem_inc(tick["dve"], 1)
                by_tile(dve, front, back, n0)

            def geglu(lp, par, k0):
                w = wts[par]
                dve.wait_ge(w_ld[par], lp * 48 + 48)
                dve.sem_inc(tick["dve"], 1)
                with dve.Fori(0, BATCH) as b:
                    for g in range(2):
                        k = k0 + b * 2 + g
                        dve.wait_ge(g_back, k + 1)
                        for i in range(GT):
                            dve.bn_stats(st[:, i, :], tp[g][:, P * i:P * i + P]).then_inc(g_st, 1)
                        dve.wait_ge(g_st, k * 4 + 4)
                        dve.sem_inc(tick["dve"], 1)
                        for i in range(GT):
                            dve.bn_aggr(mv[:, i, :], st[:, i, :]).then_inc(g_mv, 1)
                        dve.wait_ge(g_rstd, k * RSQRT_STEPS + RSQRT_STEPS)
                        dve.sem_inc(tick["dve"], 1)
                        for i in range(GT):
                            dve.tensor_scalar(xn[:, i, :], tp[g][:, P * i:P * i + P], mv[:, i, 0:1], rstd[:, i:i + 1],
                                              ALU.subtract, ALU.mult).then_inc(g_xn, 1)
                        wb = [misc[0], misc[1], tp[1 - g]]
                        for i, (c0, cn) in enumerate(FB):
                            dve.wait_ge(g_w1, k * 6 + 3 + i + 1)
                            dve.sem_inc(tick["dve"], 1)
                            dve.scalar_tensor_tensor(u[0:cn, i, :], wb[i][0:cn, :], w[0:cn, C_B1 + 3 + i:C_B1 + 4 + i],
                                                     gl[0:cn, i, :], ALU.add, ALU.mult).then_inc(g_u, 1)
                        dve.wait_ge(g_y, k + 1)
                        hg = h[:, bass.ds(b * 8 + g * 4, GT), :].rearrange("p a d -> p (a d)")
                        dve.tensor_tensor(hg, bank[g][:], hg, ALU.add).then_inc(g_h, 1)
                dve.wait_ge(g_h, k0 + 4 + 1)
                dve.sem_inc(layer_done, 1)

            dve.memset(xs[1][:], 0.0)
            dve.memset(xs4[0][:], 0.0)
            dve.memset(ones_row[:], 1.0)
            for p in range(2):
                dve.memset(kT[p][:], 0.0)
                dve.memset(v[p][:], 1.0)
            dve.memset(vprev[:], 1.0)
            dve.memset(pw[:], 0.0).then_inc(xs_rdy, 1)
            dve.wait_ge(xs_rdy, 1)
            dve.sem_inc(init, 1)
            dve.sem_inc(layer_done, 2)
            dve.sem_inc(rope_rdy, 1)
            dve.sem_inc(ss_rdy, 2)
            dve.sem_inc(v_rdy, 2)
            dve.sem_inc(h_rdy, 1)
            dve.sem_inc(g_u, 3)
            dve.sem_inc(g_xs, 1)
            dve.sem_inc(g_h, 1)
            by_layer(dve, attention, geglu)

        @block.gpsimd
        def _(pool):
            def attention(lp, par, n0):
                def copy_in(t, n, p):
                    pool.wait_ge(xT_done, n)
                    pool.sem_inc(tick["pool"], 1)
                    pool.tensor_copy(hcur[p][:], h[:, bass.ds(t, 1), :].rearrange("p a d -> p (a d)")).then_inc(hcur_rdy, 1)

                def rope(n):
                    pool.wait_ge(ss_rdy, n * 4 + 6)
                    pool.sem_inc(tick["pool"], 1)
                    rsqrt(pool, rn[:], ss[:], rn_tmp[:], 1e-24, 0.0, rn_rdy, n * RSQRT_STEPS, tick["pool"])
                    for j in range(4):
                        pool.wait_ge(rope_rdy, n * 4 + j + 2)
                        pool.tensor_tensor(rot_a[:, j, :], rot_a[:, j, :], rot_b[:, j, :], ALU.add).then_inc(rot_sum, 1)
                    pool.wait_ge(qkT_rdy, n * 4)
                    pool.wait_ge(rn_rdy, n * RSQRT_STEPS + RSQRT_STEPS)
                    for j in range(4):
                        pool.wait_ge(rot_sum, n * 4 + j + 1)
                        pool.tensor_tensor(qk[:, j, :].rearrange("p (a d) -> p a d", d=DH),
                                           rot_a[:, j, :].rearrange("p (a d) -> p a d", d=DH),
                                           rn[:, 8 * j:8 * j + 8].rearrange("p (a o) -> p a o", o=1).to_broadcast([P, 8, DH]),
                                           ALU.mult).then_inc(qk_rdy, 1)

                def keys_before(t, n, p):
                    pool.wait_ge(qkT_rdy, n * 4)
                    pool.wait_ge(s_done, n)
                    pool.tensor_tensor(kT[p][:, :, 0:WIN], kT[1 - p][:, :, P:P + WIN],
                                       carried[:, bass.ds(t, 1)].rearrange("p (a o) -> p a o", o=1).to_broadcast([P, HP, WIN]),
                                       ALU.mult).then_inc(kprev_rdy, 1)

                def values_before(m, p):
                    pool.wait_ge(pv_done, m * 4 + 5)
                    pool.sem_inc(tick["pool"], 1)
                    pool.tensor_copy(vprev[:], v[p][:]).then_inc(vprev_rdy, 1)

                def front(t, n, p):
                    copy_in(t, n, p)
                    rope(n)
                    keys_before(t, n, p)

                def back(t, m, p, front):
                    if front:
                        copy_in(*front)
                        rope(front[1])
                        keys_before(*front)
                    values_before(m, p)

                pool.wait_ge(w_ld[par], lp * 48 + 48)
                pool.wait_ge(const_ld, 48)
                pool.wait_ge(rope_rdy, n0 * 4 + 1)
                pool.sem_inc(tick["pool"], 1)
                for a in range(4):
                    for b in range(BATCH):
                        last = pool.tensor_tensor(tab[:, a, TB * b:TB * b + TB, :], raw_tab[:, a, :, :],
                                                  scales[par][:, a:a + 1, :].to_broadcast([P, TB, DH]), ALU.mult)
                    last.then_inc(tab_rdy, 1)
                pool.wait_ge(g_h, k_of(lp, par) + 1)
                pool.sem_inc(tick["pool"], 1)
                by_tile(pool, front, back, n0)

            def k_of(lp, par):
                return lp * 8 + par * 4

            def geglu(lp, par, k0):
                pool.wait_ge(h_rdy, lp * 32 + par * 16 + 17)
                pool.sem_inc(tick["pool"], 1)
                with pool.Fori(0, BATCH) as b:
                    for g in range(2):
                        k = k0 + b * 2 + g
                        pool.wait_ge(g_xT, k)
                        pool.sem_inc(tick["pool"], 1)
                        pool.tensor_copy(hgrp[:], h[:, bass.ds(b * 8 + g * 4, GT), :]).then_inc(g_hgrp, 1)
                        pool.wait_ge(g_mv, k * 4 + 4)
                        pool.sem_inc(tick["pool"], 1)
                        rsqrt(pool, rstd[:], mv[:, :, 1], rstd_tmp[:], 0.0, 1e-5, g_rstd, k * RSQRT_STEPS, tick["pool"])

            pool.wait_ge(init, 1)
            pool.sem_inc(qk_rdy, 4)
            pool.sem_inc(pv_done, 1)
            pool.sem_inc(vprev_rdy, 1)
            by_layer(pool, attention, geglu)


def local_layer_constants():
    half = np.arange(0, DH, 2, dtype=np.float32)
    inv_freq = (np.float32(1.0) / np.float32(10000.0) ** (half / np.float32(DH))).astype(np.float32)
    pos = np.arange(SEQ, dtype=np.float32)
    freqs = np.concatenate([pos[:, None] * inv_freq[None, :]] * 2, -1)
    base = (half + np.float32(0.4 * DH)) / np.float32(1.4 * DH)
    power = (pos - SEQ // 2) / np.float32(WIN // 2)
    scale = np.concatenate([base[None, :] ** power[:, None]] * 2, -1).astype(np.float32)
    cos, sin = np.cos(freqs), np.sin(freqs)
    sign = np.where(np.arange(DH) < DH // 2, -1, 1).astype(np.float32)
    tabs = np.stack([cos * scale * 8.0, sin * sign * scale * 8.0, cos / scale, sin * sign / scale])
    tables = tabs.reshape(4, TB, P, DH).transpose(2, 0, 1, 3).astype(np.float32)
    i, j = np.arange(P)[:, None, None] % WIN, np.arange(2 * WIN)[None, None, :]
    out = (j < i) | (j > i + WIN)
    first = (np.arange(NT)[None, :, None] % TB == 0) & (np.arange(P)[:, None, None] < WIN) & (j < WIN)
    mask = np.where(out | first, np.float32(NEG), np.float32(0))
    carried = np.broadcast_to((np.arange(NT) % TB != 0).astype(np.float32), (P, NT))
    return np.ascontiguousarray(tables), mask, np.ascontiguousarray(carried)


def pack_local_weights(Wqkv, q_scale, k_scale, Wo, ln_g, ln_b, W1, b1, W2, b2):
    wts = np.zeros((DEPTH, P, NWC), np.float32)
    wts[:, :, C_QKV:C_WO] = Wqkv
    wts[:, :, C_WO:C_W1] = Wo.reshape(DEPTH, HP, P, D).transpose(0, 2, 1, 3).reshape(DEPTH, P, HP * D)
    wts[:, :, C_W1:C_W2] = W1
    for f, (c0, cn) in enumerate(FB):
        wts[:, 0:cn, C_W2 + D * f:C_W2 + D * f + D] = W2[:, c0:c0 + cn]
        wts[:, 0:cn, C_B1 + f] = b1[:, DFF + c0:DFF + c0 + cn]
        wts[:, 0:cn, C_B1 + 3 + f] = b1[:, c0:c0 + cn]
    wts[:, :, C_LN], wts[:, :, C_LN + 1] = ln_g, ln_b
    swap = lambda s: np.concatenate([s[:, DH // 2:], s[:, :DH // 2]], 1)
    scales = np.concatenate([q_scale, swap(q_scale), k_scale, swap(k_scale)], 1)
    return wts, np.ascontiguousarray(scales), np.ascontiguousarray(b2)

AH, AD = 16, D // 16
SPAN = 3 * P
AP_ = AH // 2


def windowed_attention(nc, x, xnT, ident, identb, dram):
    with ExitStack() as ctx:
        sb, ps, sem = buffers(nc, ctx)
        w = sb("a_w", [P, 4, D])
        bias = sb("a_bias", [P, 2])
        bias_q = sb("a_bias_q", [P, 1])
        row_b = sb("a_row_b", [1, 2, D])
        ones_row = sb("a_ones_row", [1, P])
        pairs = sb("a_pairs", [P, AP_])
        maskb = sb("a_mask", [P, NT, 2, P], BF16)
        qT = sb("a_qT", [P, NT * P])
        kT = sb("a_kT", [P, P + NT * P + P])
        v = sb("a_v", [P, NT + 2, AH, AD + 1])
        qz = sb("a_qz", [P, AP_, P])
        kwin = [sb(f"a_kwin{i}", [P, SPAN]) for i in range(2)]
        negmax = sb("a_negmax", [P, AP_, 2])
        pr = [sb(f"a_pr{i}", [P, 2, SPAN]) for i in range(2)]
        pT = [sb(f"a_pT{i}", [P, 2, SPAN]) for i in range(2)]
        rsum = sb("a_rsum", [P, AH])
        on = sb("a_on", [P, AH, AD])
        oT = sb("a_oT", [P, P])
        s_ps = [ps(f"a_s{i}", [P, 2, 512]) for i in range(2)]
        t_ps = ps("a_t", [P, 2, 512])
        o_ps = ps("a_o", [P, 512])
        y_ps = ps("a_y", [P, 512])

        (w_ld, init, bq_rdy, proj_done, proj_rdy, v_rdy, kwin_rdy, qz_rdy, s_done, mx_rdy, p_rdy, t_done, t_rdy, pv_done,
         o_done, rs_rdy, on_rdy, oT_done, oT_rdy, y_done, x_rdy) = (sem("a_" + s) for s in (
            "w_ld init bq_rdy proj_done proj_rdy v_rdy kwin_rdy qz_rdy s_done mx_rdy p_rdy t_done t_rdy pv_done "
            "o_done rs_rdy on_rdy oT_done oT_rdy y_done x_rdy").split())
        tick = {e: sem(f"a_tick_{e}") for e in ("pe", "act", "dve", "pool")}
        NC = NT * P // 512
        ACT_TURNS = (2, 6)
        block = ctx.enter_context(nc.Block())

        def by_tile(eng, tile, last):
            tile(0, 0, True)
            with eng.Fori(0, NT // 2 - 1) as j:
                tile(j * 2 + 1, 1, False)
                tile(j * 2 + 2, 0, False)
            tile(NT - 1, 1, False)
            last(NT - 1)

        @block.sync
        def _(sp):
            for dst, name in ((w, "a_w"), (bias, "a_bias"), (row_b, "a_row_b"), (pairs, "a_pairs"), (maskb, "a_mask")):
                sp.dma_start(dst[:], dram[name]).then_inc(w_ld, 16)

        @block.tensor
        def _(pe):
            pe.wait_ge(w_ld, 80)
            pe.wait_ge(init, 1)
            for a in range(2):
                for c in range(NC):
                    n = NC * a + c
                    if n >= 2:
                        pe.wait_ge(proj_rdy, n - 1)
                    pe.matmul(s_ps[n % 2][:, 0, :], w[:, a, :], xnT[:, 512 * c:512 * c + 512], start=True, stop=True)\
                      .then_inc(proj_done, 1)
            for t in range(NT):
                if t >= 2:
                    pe.wait_ge(v_rdy, t - 1)
                else:
                    pe.wait_ge(proj_rdy, 2 * NC - 1 + t)
                pe.matmul(s_ps[t % 2][:, 0, 0:D], ones_row[:], row_b[:, 0, :], start=True, stop=False)
                pe.matmul(s_ps[t % 2][:, 0, 0:D], xnT[:, P * t:P * t + P], w[:, 2, :], start=False, stop=True)\
                  .then_inc(proj_done, 1)
            pe.wait_ge(v_rdy, NT)

            def scores(t, p, par):
                q = t * AP_ + p
                pe.wait_ge(p_rdy, q - 2 + 3)
                pe.wait_ge(qz_rdy, q + 1)
                pe.sem_inc(tick["pe"], 1)
                for e in range(2):
                    r = slice(64 * e, 64 * e + 64)
                    pe.matmul(s_ps[p % 2][:, e, 0:SPAN], qz[r, p, :], kwin[par][r, :], start=True, stop=False,
                              skip_group_check=True)
                for e in range(2):
                    s = s_ps[p % 2][:, e, 0:SPAN].rearrange("q (a k) -> q a k", a=3)[:, 0:3:2, :]
                    mm = pe.matmul(s, identb[:], maskb[:, bass.ds(t, 1), :, :].rearrange("q o a k -> q (o a) k"),
                                   start=False, stop=True, skip_group_check=True)
                mm.then_inc(s_done, 1)

            def turn(t, p):
                q = t * AP_ + p
                pe.wait_ge(t_rdy, q + 1)
                pe.wait_ge(p_rdy, q + 2)
                for e in range(2):
                    for a in range(3):
                        mm = pe.transpose(t_ps[:, e, P * a:P * a + P], pr[p % 2][:, e, P * a:P * a + P], ident[:])
                mm.then_inc(t_done, 1)

            def values(t, p):
                q = t * AP_ + p
                pe.wait_ge(t_rdy, q + 2)
                if p == 0:
                    pe.wait_ge(on_rdy, t + 1)
                for e in range(2):
                    h = p + 8 * e
                    for a in range(3):
                        mm = pe.matmul(o_ps[:, (AD + 1) * h:(AD + 1) * h + AD + 1], pT[p % 2][:, e, P * a:P * a + P],
                                       v[:, bass.ds(t + a, 1), h, :].rearrange("k o d -> k (o d)"), start=(a == 0), stop=(a == 2),
                                       skip_group_check=True)
                mm.then_inc(pv_done, 1)

            def turn_out(t):
                pe.wait_ge(on_rdy, t + 2)
                pe.wait_ge(x_rdy, t + 1)
                pe.transpose(y_ps[:, 0:P], on[:].rearrange("q h d -> q (h d)"), ident[:]).then_inc(oT_done, 1)

            def project_out(t):
                pe.wait_ge(oT_rdy, t + 1)
                pe.matmul(y_ps[:, P:P + D], ones_row[:], row_b[:, 1, :], start=True, stop=False, skip_group_check=True)
                pe.matmul(y_ps[:, P:P + D], oT[:], w[:, 3, :], start=False, stop=True, skip_group_check=True).then_inc(y_done, 1)

            def tile(t, par, first):
                pe.wait_ge(kwin_rdy, t + 1)
                pe.sem_inc(tick["pe"], 1)
                for p in range(AP_ + 2):
                    if p < AP_:
                        scores(t, p, par)
                    if 1 <= p <= AP_:
                        turn(t, p - 1)
                    if p >= 2:
                        values(t, p - 2)
                    if p == 3 and not first:
                        turn_out(t - 1)
                    if p == 5 and not first:
                        project_out(t - 1)

            def last(t):
                turn_out(t)
                project_out(t)

            by_tile(pe, tile, last)

        @block.scalar
        def _(act):
            act.wait_ge(bq_rdy, 1)
            for a in range(2):
                for c in range(NC):
                    n = NC * a + c
                    act.wait_ge(proj_done, n + 1)
                    dst = qT[:, 512 * c:512 * c + 512] if a == 0 else kT[:, P + 512 * c:P + 512 * c + 512]
                    act.activation(dst, s_ps[n % 2][:, 0, :], ACT.Identity, bias=bias_q[:] if a == 0 else bias[:, 1:2],
                                   scale=float(AD) ** -0.5 if a == 0 else 1.0).then_inc(proj_rdy, 1)
            for t in range(NT):
                act.wait_ge(proj_done, 2 * NC + t + 1)
                act.activation(v[:, t + 1, :, 0:AD], s_ps[t % 2][:, 0, 0:D].rearrange("k (h d) -> k h d", h=AH), ACT.Copy)\
                   .then_inc(v_rdy, 1)

            def weights(t, p):
                q = t * AP_ + p
                act.wait_ge(mx_rdy, q + 1)
                for e in range(2):
                    ins = act.activation(pr[p % 2][:, e, :], s_ps[p % 2][:, e, 0:SPAN], ACT.Exp, bias=negmax[:, p, e:e + 1])
                ins.then_inc(p_rdy, 1)

            def keep_turned(t, p):
                q = t * AP_ + p
                act.wait_ge(t_done, q + 1)
                act.activation(pT[p % 2][:], t_ps[:, :, 0:SPAN], ACT.Copy).then_inc(t_rdy, 1)

            def tile(t, par, first):
                for p in range(AP_ + 1):
                    if p < AP_:
                        weights(t, p)
                    if p >= 1 and (p - 1) in ACT_TURNS:
                        keep_turned(t, p - 1)
                    if p == 4 and not first:
                        keep_out(t - 1)

            def keep_out(t):
                act.wait_ge(oT_done, t + 1)
                act.activation(oT[:], y_ps[:, 0:P], ACT.Copy).then_inc(oT_rdy, 1)

            by_tile(act, tile, keep_out)

        @block.vector
        def _(dve):
            dve.memset(ones_row[:], 1.0)
            dve.memset(kT[:, 0:P], 0.0)
            dve.memset(kT[:, P + NT * P:], 0.0)
            dve.memset(v[:], 1.0)
            dve.memset(kwin[0][:], 0.0).then_inc(init, 1)
            for s in (p_rdy, t_rdy, on_rdy, x_rdy):
                dve.sem_inc(s, 1)
            dve.wait_ge(w_ld, 80)
            dve.tensor_scalar(bias_q[:], bias[:, 0:1], float(AD) ** -0.5, None, ALU.mult).then_inc(bq_rdy, 1)

            def maxima(t, p):
                q = t * AP_ + p
                dve.wait_ge(s_done, q + 1)
                dve.tensor_reduce(negmax[:, p, :], s_ps[p % 2][:, :, 0:SPAN], AX, ALU.max, negate=True).then_inc(mx_rdy, 1)

            def keep_turned(t, p):
                q = t * AP_ + p
                dve.wait_ge(t_done, q + 1)
                dve.tensor_copy(pT[p % 2][:], t_ps[:, :, 0:SPAN]).then_inc(t_rdy, 1)

            def outputs(t):
                dve.wait_ge(pv_done, t * AP_ + AP_)
                o = o_ps[:, 0:AH * (AD + 1)].rearrange("q (h d) -> q h d", h=AH)
                dve.reciprocal(rsum[:], o[:, :, AD]).then_inc(rs_rdy, 1)
                dve.wait_ge(rs_rdy, t + 1)
                dve.tensor_tensor(on[:], o[:, :, 0:AD], rsum[:].rearrange("q (h o) -> q h o", o=1).to_broadcast([P, AH, AD]),
                                  ALU.mult).then_inc(on_rdy, 1)

            def add(t):
                dve.wait_ge(y_done, t + 1)
                xt = x[:, bass.ds(t, 1), :].rearrange("q a d -> q (a d)")
                dve.tensor_tensor(xt, xt, y_ps[:, P:P + D], ALU.add).then_inc(x_rdy, 1)

            def tile(t, par, first):
                for p in range(AP_ + 1):
                    if p < AP_:
                        maxima(t, p)
                    if p == 2 and not first:
                        outputs(t - 1)
                    if p >= 1 and (p - 1) not in ACT_TURNS:
                        keep_turned(t, p - 1)
                    if p == 6 and not first:
                        add(t - 1)

            def last(t):
                outputs(t)
                add(t)
                dve.wait_ge(x_rdy, NT + 1)

            by_tile(dve, tile, last)

        @block.gpsimd
        def _(pool):
            pool.wait_ge(w_ld, 80)
            pool.wait_ge(proj_rdy, 2 * NC)
            pool.wait_ge(init, 1)

            def tile(t, par, first):
                if not first:
                    pool.wait_ge(s_done, t * AP_ - AP_)
                    pool.sem_inc(tick["pool"], 1)
                pool.tensor_copy(kwin[par][:], kT[:, bass.ds(t * P, SPAN)]).then_inc(kwin_rdy, 1)
                for p in range(AP_):
                    if not first:
                        pool.wait_ge(s_done, t * AP_ + p - AP_ + 1)
                        pool.sem_inc(tick["pool"], 1)
                    pool.tensor_tensor(qz[:, p, :], qT[:, bass.ds(t * P, P)], pairs[:, p:p + 1].to_broadcast([P, P]),
                                       ALU.mult).then_inc(qz_rdy, 1)

            by_tile(pool, tile, lambda t: None)


def attention_constants():
    i, j = np.arange(P)[:, None], np.arange(P)[None, :]
    before, behind = j < i, j > i
    never = np.ones((P, P), bool)
    tiles = [np.stack([never if t % TB == 0 else before, never if t % TB == TB - 1 else behind], 1) for t in range(NT)]
    mask = np.where(np.stack(tiles, 1), np.float32(NEG), np.float32(0))
    pairs = (np.arange(P)[:, None] // AD % AP_ == np.arange(AP_)[None, :]).astype(np.float32)
    return mask, pairs


NCOL, NNEU = 16, 32
GATE_H = D // 2
CB = NCOL * NNEU // P


def column_mixture(nc, x, xn, xnT, ident, dram):
    with ExitStack() as ctx:
        sb, ps, sem = buffers(nc, ctx)
        w = sb("m_w", [P, CB * P])
        pw = sb("m_pw", [P, CB, D])
        gw1 = sb("m_gw1", [P, GATE_H])
        gw2 = sb("m_gw2", [GATE_H, NCOL])
        bcol = sb("m_bcol", [P, CB + 1])
        rows = sb("m_rows", [1, NCOL + D])
        lng = sb("m_lng", [P, 2, D])
        emb = sb("m_emb", [NCOL, D])
        spread = sb("m_spread", [NCOL, CB * P])
        order = sb("m_order", [P, NCOL])
        ones_row = sb("m_ones_row", [1, P])
        embT = sb("m_embT", [P, NCOL])
        esq = sb("m_esq", [NCOL, D])
        ess, ers, etm = (sb("m_" + n, [NCOL, 1]) for n in ("ess", "ers", "etm"))
        xsq = sb("m_xsq", [P, NT, D])
        xss, xrs, xtm = (sb("m_" + n, [P, NT]) for n in ("xss", "xrs", "xtm"))
        hT = sb("m_hT", [GATE_H, NT * P])
        cT = sb("m_cT", [P, CB, NT * P])
        sg, lg, ex, ca = (sb("m_" + n, [P, NT, NCOL]) for n in ("sg", "lg", "ex", "ca"))
        best, tot, top = (sb("m_" + n, [P, NT]) for n in ("best", "tot", "top"))
        wT = sb("m_wT", [NCOL, NT * P])
        y = xsq
        st = sb("m_st", [P, NT, 6])
        mv = sb("m_mv", [P, NT, 2])
        rstd, rtm = (sb("m_" + n, [P, NT]) for n in ("rstd", "rtm"))
        gp = [ps(f"m_gp{i}", [P, 512]) for i in range(4)]
        sim = ps("m_sim", [P, NT, NCOL])
        gat = ps("m_gat", [P, NT, NCOL])
        yp = [ps(f"m_yp{i}", [P, 512]) for i in range(2)]
        (w_ld, emb_step, ess_rdy, ers_step, embT_done, embT_rdy, xss_rdy, xrs_step, g_done, g_rdy, sim_done, gat_done, step, act_step,
         wT_done, wT_rdy, sp_done, comb_rdy, y_done, y_rdy, st_rdy, mv_rdy, rs_step, out_step, init, tick, ptick) = (sem("m_" + s) for s in (
            "w_ld emb_step ess_rdy ers_step embT_done embT_rdy xss_rdy xrs_step g_done g_rdy sim_done gat_done step act_step "
            "wT_done wT_rdy sp_done comb_rdy y_done y_rdy st_rdy mv_rdy rs_step out_step init tick ptick").split())
        NG = NT * P // 512
        NGELU = NG * (1 + CB)
        MIX_EX, MIX_STEPS = 7, 15
        loads = ((w[:], "m_w"), (pw[:], "m_pw"), (gw1[:], "m_gw1"), (gw2[:], "m_gw2"), (bcol[:], "m_bcol"), (rows[:], "m_rows"),
                 (emb[:], "m_emb"), (spread[:], "m_spread"))
        wide = ((lng[:].rearrange("p a d -> p (a d)"), "m_lng", 2 * D), (order[:], "m_order", NCOL))
        LOADED = 16 * (len(loads) + len(wide))
        block = ctx.enter_context(nc.Block())

        def over(small, n):
            return small.rearrange("p (t o) -> p t o", o=1).to_broadcast([P, NT, n])

        @block.sync
        def _(sp):
            for dst, name in loads:
                sp.dma_start(dst, dram[name]).then_inc(w_ld, 16)
            for dst, name, n in wide:
                sp.dma_start(dst, dram[name].broadcast_to([P, n])).then_inc(w_ld, 16)

        @block.tensor
        def _(pe):
            pe.wait_ge(w_ld, LOADED)
            pe.wait_ge(init, 1)
            for g in range(NG):
                for c in range(1 + CB):
                    n = g * (1 + CB) + c
                    if n >= 4:
                        pe.wait_ge(g_rdy, n - 3)
                    lhs, m = (gw1[:], GATE_H) if c == 0 else (w[:, P * (c - 1):P * c], P)
                    pe.matmul(gp[n % 4][0:m, :], lhs, xnT[:, 512 * g:512 * g + 512], start=True, stop=True).then_inc(g_done, 1)
            pe.wait_ge(ers_step, RSQRT_STEPS + 1)
            pe.transpose(yp[0][:, 0:NCOL], emb[:], ident[0:NCOL, 0:NCOL]).then_inc(embT_done, 1)
            pe.wait_ge(embT_rdy, 1)
            for t in range(NT):
                mm = pe.matmul(sim[:, t, :], xnT[:, P * t:P * t + P], embT[:], start=True, stop=True, skip_group_check=True)
            mm.then_inc(sim_done, 1)
            pe.wait_ge(g_rdy, NGELU)
            for t in range(NT):
                pe.matmul(gat[:, t, :], ones_row[:], rows[:, 0:NCOL], start=True, stop=False, skip_group_check=True)
                mm = pe.matmul(gat[:, t, :], hT[:, P * t:P * t + P], gw2[:], start=False, stop=True, skip_group_check=True)
            mm.then_inc(gat_done, 1)
            pe.wait_ge(step, MIX_STEPS)
            for g in range(NG):
                for k in range(4):
                    t = 4 * g + k
                    mm = pe.transpose(gp[g][0:NCOL, P * k:P * k + P], ca[:, t, :], ident[:])
                mm.then_inc(wT_done, 1)
            for g in range(NG):
                pe.wait_ge(wT_rdy, NG)
                for c in range(CB):
                    n = g * CB + c
                    if n >= 4:
                        pe.wait_ge(comb_rdy, n - 3)
                    pe.matmul(gp[n % 4][:], spread[:, P * c:P * c + P], wT[:, 512 * g:512 * g + 512], start=True, stop=True)\
                      .then_inc(sp_done, 1)
            for g in range(NG):
                pe.wait_ge(comb_rdy, CB * (g + 1))
                if g >= 2:
                    pe.wait_ge(y_rdy, g - 1)
                for k in range(4):
                    t = 4 * g + k
                    yt = yp[g % 2][:, D * k:D * k + D]
                    pe.matmul(yt, ones_row[:], rows[:, NCOL:], start=True, stop=False, skip_group_check=True)
                    for c in range(CB):
                        mm = pe.matmul(yt, cT[:, c, P * t:P * t + P], pw[:, c, :], start=False, stop=(c == CB - 1),
                                       skip_group_check=True)
                mm.then_inc(y_done, 1)

        @block.scalar
        def _(act):
            act.wait_ge(w_ld, LOADED)
            for g in range(NG):
                for c in range(1 + CB):
                    n = g * (1 + CB) + c
                    act.wait_ge(g_done, n + 1)
                    if c == 0:
                        ins = act.activation(hT[:, 512 * g:512 * g + 512], gp[n % 4][0:GATE_H, :], ACT.Gelu,
                                             bias=bcol[0:GATE_H, CB:CB + 1])
                    else:
                        ins = act.activation(cT[:, c - 1, 512 * g:512 * g + 512], gp[n % 4][:], ACT.Gelu, bias=bcol[:, c - 1:c])
                    ins.then_inc(g_rdy, 1)
            act.wait_ge(embT_done, 1)
            act.activation(embT[:], yp[0][:, 0:NCOL], ACT.Copy).then_inc(embT_rdy, 1)
            act.wait_ge(step, 2)
            act.activation(sg[:], sg[:], ACT.Exp, scale=-1.0).then_inc(act_step, 1)
            act.wait_ge(step, MIX_EX)
            act.activation(ex[:], ex[:], ACT.Exp).then_inc(act_step, 1)
            for g in range(NG):
                act.wait_ge(wT_done, g + 1)
                act.activation(wT[:, 512 * g:512 * g + 512], gp[g][0:NCOL, :], ACT.Copy).then_inc(wT_rdy, 1)

        @block.vector
        def _(dve):
            dve.memset(ones_row[:], 1.0).then_inc(init, 1)
            dve.tensor_tensor(xsq[:], xn[:], xn[:], ALU.mult).then_inc(xss_rdy, 1)
            dve.wait_ge(w_ld, LOADED)
            dve.tensor_tensor(esq[:], emb[:], emb[:], ALU.mult).then_inc(emb_step, 1)
            dve.wait_ge(emb_step, 1)
            dve.tensor_reduce(ess[:], esq[:], AX, ALU.add).then_inc(ess_rdy, 1)
            dve.wait_ge(xss_rdy, 1)
            dve.tensor_reduce(xss[:], xsq[:], AX, ALU.add).then_inc(xss_rdy, 1)
            dve.wait_ge(ers_step, RSQRT_STEPS)
            dve.tensor_scalar(emb[:], emb[:], ers[:], None, ALU.mult).then_inc(ers_step, 1)

            steps = 0

            def link(ins):
                nonlocal steps
                steps += 1
                ins.then_inc(step, 1)
                dve.wait_ge(step, steps)

            dve.wait_ge(sim_done, 1)
            dve.wait_ge(xrs_step, RSQRT_STEPS)
            link(dve.tensor_tensor(lg[:], sim[:], over(xrs[:], NCOL), ALU.mult))
            dve.wait_ge(gat_done, 1)
            link(dve.tensor_scalar(sg[:], gat[:], -EXP_MAX, None, ALU.max))
            dve.wait_ge(act_step, 1)
            link(dve.tensor_scalar(sg[:], sg[:], 1.0, None, ALU.add))
            link(dve.reciprocal(sg[:], sg[:]))
            link(dve.tensor_tensor(lg[:], lg[:], sg[:], ALU.add))
            link(dve.tensor_reduce(best[:], lg[:], AX, ALU.max))
            link(dve.tensor_tensor(ex[:], lg[:], over(best[:], NCOL), ALU.subtract))
            assert steps == MIX_EX
            link(dve.tensor_tensor(ca[:], lg[:], over(best[:], NCOL), ALU.is_equal))
            link(dve.tensor_tensor(ca[:], ca[:], order[:].rearrange("p (o c) -> p o c", o=1).to_broadcast([P, NT, NCOL]), ALU.mult))
            link(dve.tensor_reduce(top[:], ca[:], AX, ALU.max))
            link(dve.tensor_tensor(ca[:], ca[:], over(top[:], NCOL), ALU.is_equal))
            dve.wait_ge(act_step, 2)
            link(dve.tensor_reduce(tot[:], ex[:], AX, ALU.add))
            link(dve.reciprocal(tot[:], tot[:]))
            link(dve.tensor_tensor(ex[:], ex[:], over(tot[:], NCOL), ALU.mult))
            assert steps == MIX_STEPS - 1
            link(dve.tensor_tensor(ca[:], ca[:], ex[:], ALU.mult))
            for g in range(NG):
                for c in range(CB):
                    n = g * CB + c
                    dve.wait_ge(sp_done, n + 1)
                    part = cT[:, c, 512 * g:512 * g + 512]
                    dve.tensor_tensor(part, part, gp[n % 4][:], ALU.mult).then_inc(comb_rdy, 1)
            for g in range(NG):
                s = slice(4 * g, 4 * g + 4)
                dve.wait_ge(y_done, g + 1)
                dve.tensor_tensor(y[:, s, :], yp[g % 2][:].rearrange("p (t d) -> p t d", d=D), xn[:, s, :], ALU.add).then_inc(y_rdy, 1)
            for t in range(NT):
                dve.wait_ge(y_rdy, t // 4 + 1)
                dve.bn_stats(st[:, t, :], y[:, t, :]).then_inc(st_rdy, 1)
            dve.wait_ge(st_rdy, NT)
            for t in range(NT):
                dve.bn_aggr(mv[:, t, :], st[:, t, :]).then_inc(mv_rdy, 1)
            dve.wait_ge(mv_rdy, NT)
            dve.tensor_tensor(y[:], y[:], mv[:, :, 0:1].to_broadcast([P, NT, D]), ALU.subtract).then_inc(out_step, 1)
            dve.wait_ge(rs_step, RSQRT_STEPS)
            dve.wait_ge(out_step, 1)
            dve.tensor_tensor(y[:], y[:], over(rstd[:], D), ALU.mult).then_inc(out_step, 1)
            dve.wait_ge(out_step, 2)
            dve.tensor_tensor(y[:], y[:], lng[:, 0:1, :].to_broadcast([P, NT, D]), ALU.mult).then_inc(out_step, 1)
            dve.tensor_tensor(x[:], x[:], lng[:, 1:2, :].to_broadcast([P, NT, D]), ALU.add).then_inc(out_step, 1)
            dve.wait_ge(out_step, 4)
            dve.tensor_tensor(x[:], x[:], y[:], ALU.add).then_inc(out_step, 1)
            dve.wait_ge(out_step, 5)

        @block.gpsimd
        def _(pool):
            pool.wait_ge(ess_rdy, 1)
            rsqrt(pool, ers[:], ess[:], etm[:], 1e-24, 0.0, ers_step, 0, ptick)
            pool.wait_ge(ers_step, RSQRT_STEPS)
            pool.wait_ge(xss_rdy, 2)
            rsqrt(pool, xrs[:], xss[:], xtm[:], 1e-24, 0.0, xrs_step, 0, ptick)
            pool.wait_ge(xrs_step, RSQRT_STEPS)
            pool.wait_ge(mv_rdy, NT)
            rsqrt(pool, rstd[:], mv[:, :, 1], rtm[:], 0.0, 1e-5, rs_step, 0, ptick)


def pack_mixture_weights(W_cols, b_cols, gate_b1, gate_b2, proj_w, proj_b, ln_g, ln_b):
    w = np.ascontiguousarray(W_cols.transpose(1, 0, 2).reshape(D, NCOL * NNEU))
    pw = np.ascontiguousarray(proj_w.reshape(CB, P, D).transpose(1, 0, 2))
    bcol = np.zeros((P, CB + 1), np.float32)
    bcol[:, 0:CB] = b_cols.reshape(CB, P).T
    bcol[0:GATE_H, CB] = gate_b1
    return w, pw, bcol, np.concatenate([gate_b2, proj_b])[None], np.concatenate([ln_g, ln_b])[None]


def mixture_constants():
    spread = (np.arange(CB * P)[None, :] // NNEU == np.arange(NCOL)[:, None]).astype(np.float32)
    return spread, np.arange(NCOL, 0, -1, dtype=np.float32)[None]

def program(nc, dram):
    with ExitStack() as ctx:
        sb, ps, sem = buffers(nc, ctx)
        x = sb("x", [P, NT, D])
        xn = sb("xn", [P, NT, D])
        ident = sb("ident", [P, P])
        identb = sb("identb", [P, P], BF16)
        loaded, stored = sem("loaded"), sem("stored")
        with nc.Block() as block:
            @block.sync
            def _(sp):
                for dst, src in ((x[:], dram["x"].rearrange("(t p) d -> p t d", p=P)), (ident[:], dram["ident"]),
                                 (identb[:], dram["identb"])):
                    sp.dma_start(dst, src).then_inc(loaded, 16)
                sp.wait_ge(loaded, 48)
        gated_delta(nc, x, xn, ident, identb, dram)
        local_layers(nc, xn, ident, identb, dram)
        with ExitStack() as second:
            xnT = second.enter_context(nc.sbuf_tensor("xnT2", [P, NT * P], F32))
            normalise(nc, x, xn, lambda t, n: xnT[:, P * t:P * (t + n)], ident, "n1", add=xn)
            windowed_attention(nc, x, xnT, ident, identb, dram)
            column_mixture(nc, x, xn, xnT, ident, dram)
        with nc.Block() as block:
            @block.sync
            def _(sp):
                sp.dma_start(dram["out"].rearrange("(t p) d -> p t d", p=P), x[:]).then_inc(stored, 16)
                sp.wait_ge(stored, 16)


def kernel(L0_attn_hidden_states, L0_attn_q_w, L0_attn_k_w, L0_attn_v_w, L0_attn_a_w, L0_attn_b_w, L0_attn_g_w, L0_attn_o_w,
           L0_attn_conv_q_w, L0_attn_conv_k_w, L0_attn_conv_v_w, L0_attn_A_log, L0_attn_dt_bias, L0_attn_norm_weight,
           L0_ffn_Wqkv, L0_ffn_q_scale, L0_ffn_k_scale, L0_ffn_Wo, L0_ffn_ln_g, L0_ffn_ln_b, L0_ffn_W1, L0_ffn_b1, L0_ffn_W2,
           L0_ffn_b2, L1_attn_Wq, L1_attn_bq, L1_attn_Wk, L1_attn_bk, L1_attn_Wv, L1_attn_bv, L1_attn_Wo, L1_attn_bo,
           L1_ffn_col_emb, L1_ffn_gate_w1, L1_ffn_gate_b1, L1_ffn_gate_w2, L1_ffn_gate_b2, L1_ffn_W_cols, L1_ffn_b_cols,
           L1_ffn_proj_w, L1_ffn_proj_b, L1_ffn_ln_g, L1_ffn_ln_b):
    import concourse.bacc as bacc
    from concourse.bass_utils import run_bass_kernel_spmd
    import ml_dtypes
    A = np.ascontiguousarray
    bf16 = ml_dtypes.bfloat16
    w_qkv, w_abg, w_conv, wo = pack_delta_weights(*[A(a) for a in (
        L0_attn_q_w, L0_attn_k_w, L0_attn_v_w, L0_attn_a_w, L0_attn_b_w, L0_attn_g_w, L0_attn_o_w,
        L0_attn_conv_q_w, L0_attn_conv_k_w, L0_attn_conv_v_w)])
    tri, causal, blocks = delta_constants()
    l_wts, l_scales, l_b2 = pack_local_weights(*[A(a) for a in (
        L0_ffn_Wqkv, L0_ffn_q_scale, L0_ffn_k_scale, L0_ffn_Wo, L0_ffn_ln_g, L0_ffn_ln_b, L0_ffn_W1, L0_ffn_b1, L0_ffn_W2,
        L0_ffn_b2)])
    l_tables, l_mask, l_carried = local_layer_constants()
    a_mask, a_pairs = attention_constants()
    m_w, m_pw, m_bcol, m_rows, m_lng = pack_mixture_weights(*[A(a) for a in (
        L1_ffn_W_cols, L1_ffn_b_cols, L1_ffn_gate_b1, L1_ffn_gate_b2, L1_ffn_proj_w, L1_ffn_proj_b, L1_ffn_ln_g, L1_ffn_ln_b)])
    m_spread, m_order = mixture_constants()
    arrays = {"x": A(L0_attn_hidden_states).reshape(-1, D), "ident": np.eye(P, dtype=np.float32), "identb": np.eye(P, dtype=bf16),
              "d_w_qkv": w_qkv, "d_w_abg": w_abg, "d_w_conv": w_conv, "d_wo": wo, "d_dt_bias": A(L0_attn_dt_bias)[None],
              "d_a_log": A(L0_attn_A_log)[None], "d_nw": A(L0_attn_norm_weight)[None], "d_tri": tri,
              "d_causal": causal.astype(bf16), "d_blocks": blocks.astype(bf16),
              "l_wts": l_wts, "l_scales": l_scales, "l_b2": l_b2, "l_tables": l_tables, "l_mask": A(l_mask).astype(bf16),
              "l_carried": l_carried,
              "a_w": A(np.stack([A(a) for a in (L1_attn_Wq, L1_attn_Wk, L1_attn_Wv, L1_attn_Wo)], 1)),
              "a_bias": A(np.stack([A(L1_attn_bq), A(L1_attn_bk)], 1)),
              "a_row_b": A(np.stack([A(L1_attn_bv), A(L1_attn_bo)])[None]), "a_pairs": a_pairs, "a_mask": a_mask.astype(bf16),
              "m_w": m_w, "m_pw": m_pw, "m_gw1": A(L1_ffn_gate_w1), "m_gw2": A(L1_ffn_gate_w2), "m_bcol": m_bcol,
              "m_rows": m_rows, "m_emb": A(L1_ffn_col_emb), "m_spread": m_spread, "m_lng": m_lng, "m_order": m_order}
    nc = bacc.Bacc("TRN2", target_bir_lowering=False, num_devices=1)
    dram = {k: nc.dram_tensor("in_" + k, a.shape, mybir.dt.from_np(a.dtype), kind="ExternalInput").ap() for k, a in arrays.items()}
    dram["out"] = nc.dram_tensor("result", (BATCH * SEQ, D), F32, kind="ExternalOutput").ap()
    program(nc, dram)
    r = run_bass_kernel_spmd(nc, [{"in_" + k: a for k, a in arrays.items()}], core_ids=[0])
    return r.results[0]["result"].reshape(BATCH, SEQ, D)
```

```python
from contextlib import ExitStack

import numpy as np

import concourse.bass as bass
from concourse import mybir

F32 = mybir.dt.float32
BF16 = mybir.dt.bfloat16
I32 = mybir.dt.int32
ALU = mybir.AluOpType
ACT = mybir.ActivationFunctionType
AX = mybir.AxisListType.X

P = 128
BATCH, SEQ, D = 2, 1024, 128
NT = BATCH * SEQ // P
TB = SEQ // P
NEG = -1e30
EXP_MAX = 87.0


def buffers(nc, ctx):
    taken = []

    def sb(name, shape, dt=F32):
        return ctx.enter_context(nc.sbuf_tensor(name, shape, dt))

    def ps(name, shape, dt=F32):
        return ctx.enter_context(nc.psum_tensor(name, shape, dt))

    def sem(name):
        taken.append(nc.alloc_semaphore(name))
        return taken[-1]

    def clear():
        if taken:
            nc.clear_and_free_semaphores(taken)
            nc.all_engine_barrier()

    ctx.callback(clear)
    return sb, ps, sem


RSQRT_STEPS = 15


def rsqrt(eng, y, x, tmp, low, shift, done, n, tick):
    def step(ins, k):
        ins.then_inc(done, 1)
        eng.wait_ge(done, n + k)
        eng.sem_inc(tick, 1)

    step(eng.tensor_scalar(x, x, shift, low, ALU.add, ALU.max), 1)
    step(eng.tensor_scalar(y.bitcast(I32), x.bitcast(I32), -0.5, float(0x5F3759DF), ALU.mult, ALU.add), 2)
    step(eng.tensor_scalar(x, x, -0.5, None, ALU.mult), 3)
    for i in range(3):
        step(eng.tensor_tensor(tmp, y, y, ALU.mult), 4 * i + 4)
        step(eng.tensor_tensor(tmp, tmp, x, ALU.mult), 4 * i + 5)
        step(eng.tensor_scalar(tmp, tmp, 1.5, None, ALU.add), 4 * i + 6)
        last = eng.tensor_tensor(y, tmp, y, ALU.mult)
        if i < 2:
            step(last, 4 * i + 7)
    last.then_inc(done, 1)

def normalise(nc, x, xn, xnT, ident, tag, add=None):
    GT = 4
    with ExitStack() as ctx:
        sb, ps, sem = buffers(nc, ctx)
        st = sb(tag + "_st", [P, NT, 6])
        mv = sb(tag + "_mv", [P, NT, 2])
        rstd = sb(tag + "_rstd", [P, NT])
        tmp = sb(tag + "_tmp", [P, NT])
        tp = [ps(f"{tag}_tp{i}", [P, GT, P]) for i in range(2)]
        sum_rdy, st_rdy, mv_rdy, rs_rdy, centred, xn_rdy, tp_done, xnT_rdy, tick = (sem(f"{tag}_{s}") for s in (
            "sum_rdy", "st_rdy", "mv_rdy", "rs_rdy", "centred", "xn_rdy", "tp_done", "xnT_rdy", "tick"))
        block = ctx.enter_context(nc.Block())

        @block.vector
        def _(dve):
            if add is not None:
                dve.tensor_tensor(x[:], x[:], add[:], ALU.add).then_inc(sum_rdy, 1)
                dve.wait_ge(sum_rdy, 1)
            for t in range(NT):
                dve.bn_stats(st[:, t, :], x[:, t, :]).then_inc(st_rdy, 1)
            dve.wait_ge(st_rdy, NT)
            for t in range(NT):
                dve.bn_aggr(mv[:, t, :], st[:, t, :]).then_inc(mv_rdy, 1)
            dve.wait_ge(mv_rdy, NT)
            for g in range(NT // GT):
                s = slice(GT * g, GT * g + GT)
                dve.tensor_tensor(xn[:, s, :], x[:, s, :], mv[:, s, 0:1].to_broadcast([P, GT, D]), ALU.subtract).then_inc(centred, 1)
            dve.wait_ge(rs_rdy, RSQRT_STEPS)
            for g in range(NT // GT):
                s = slice(GT * g, GT * g + GT)
                dve.wait_ge(centred, g + 1)
                dve.tensor_tensor(xn[:, s, :], xn[:, s, :],
                                  rstd[:, s].rearrange("p (t o) -> p t o", o=1).to_broadcast([P, GT, D]), ALU.mult).then_inc(xn_rdy, 1)

        @block.gpsimd
        def _(pool):
            pool.wait_ge(mv_rdy, NT)
            rsqrt(pool, rstd[:], mv[:, :, 1], tmp[:], 0.0, 1e-5, rs_rdy, 0, tick)

        @block.tensor
        def _(pe):
            for g in range(NT // GT):
                pe.wait_ge(xn_rdy, g + 1)
                if g >= 2:
                    pe.wait_ge(xnT_rdy, g - 1)
                for k in range(GT):
                    mm = pe.transpose(tp[g % 2][:, k, :], xn[:, GT * g + k, :], ident[:])
                mm.then_inc(tp_done, 1)

        @block.scalar
        def _(act):
            for g in range(NT // GT):
                act.wait_ge(tp_done, g + 1)
                act.activation(xnT(GT * g, GT), tp[g % 2][:].rearrange("p t q -> p (t q)"), ACT.Copy).then_inc(xnT_rdy, 1)
            act.wait_ge(xnT_rdy, NT // GT)


def gated_delta(nc, x, xn, ident, identb, dram):
    with ExitStack() as ctx:
        sb, ps, sem = buffers(nc, ctx)
        qT = sb("qT", [P, GH, BATCH * SEQ])
        kT = sb("kT", [P, GH, BATCH * SEQ])
        vT = sb("vT", [P, len(VB), BATCH * SEQ])
        gate = sb("gate", [P, NT, VD])
        beta = sb("beta", [P, NT, GH])
        logdecay = sb("logdecay", [P, NT, GH])
        decay = sb("decay", [P, 3, NT, GH])
        rinv = sb("rinv", [P, 2 * GH, NT])
        cleared = sem("cleared")
        with ExitStack() as first:
            xnT = first.enter_context(nc.sbuf_tensor("xnT", [P, BATCH, KCONV - 1 + SEQ], F32))
            with nc.Block() as block:
                @block.vector
                def _(dve):
                    dve.memset(xnT[:, :, 0:KCONV - 1], 0.0)
                    dve.memset(vT[:], 0.0).then_inc(cleared, 1)
                    dve.wait_ge(cleared, 1)
            normalise(nc, x, xn, lambda t, n: xnT[:, t // TB, KCONV - 1 + P * (t % TB):KCONV - 1 + P * (t % TB + n)], ident, "n0")
            delta_inputs(nc, xnT, qT, kT, vT, gate, (beta, logdecay), rinv, decay, dram)
        delta_chunks(nc, x[:].rearrange("p t d -> p (t d)"), ident, identb, qT, kT, vT, gate, beta, logdecay, rinv, decay, dram)
        delta_outputs(nc, x, ident, gate, dram)

GH, HK, HV, KCONV = 6, 128, 32, 4
KD, VD = GH * HK, GH * HV
VB = [(0, 128), (128, VD - 128)]
NBLK = 2 * GH + len(VB)
LEVELS = 7
SMALL = NT * GH
SERIES = range(15, 1, -2)
GATE_G = 13 + len(SERIES)


def delta_inputs(nc, xnT, qT, kT, vT, gate, beta, rinv, decay, dram):
    beta, logdecay = beta
    with ExitStack() as ctx:
        sb, ps, sem = buffers(nc, ctx)
        w_qkv = sb("d_w_qkv", [P, 2 * KD + VD])
        w_abg = sb("d_w_abg", [P, 2 * GH + VD])
        w_conv = sb("d_w_conv", [P, NBLK, KCONV])
        dt_bias = sb("d_dt_bias", [P, GH])
        a_log = sb("d_a_log", [P, GH])
        tri = sb("d_tri", [P, 3, P])
        raw = [sb(f"d_raw{i}", [P, KCONV - 1 + SEQ]) for i in range(2)]
        conv = [sb(f"d_conv{i}", [P, SEQ]) for i in range(2)]
        sqd = [sb(f"d_sqd{i}", [P, SEQ]) for i in range(2)]
        rs_tmp = sb("d_rs_tmp", [P, 2 * GH * NT])
        zab = sb("d_zab", [P, NT, 2 * GH])
        za = sb("d_za", [P, NT, GH])
        e1 = sb("d_e1", [P, NT, GH])
        s1 = sb("d_s1", [P, NT, GH])
        s2 = sb("d_s2", [P, NT, GH])
        pl = sb("d_pl", [P, NT, GH])
        ssq = sb("d_ssq", [P, 2 * GH * NT])

        proj = [ps(f"d_proj{i}", [P, SEQ]) for i in range(2)]
        norms = ps("d_norms", [P, 512])
        zp = [ps(f"d_zp{i}", [P, 512]) for i in range(2)]
        sums = ps("d_sums", [P, 512])

        w_ld = sem("d_w_ld")
        init = sem("d_init")
        proj_done = sem("d_proj_done")
        raw_rdy = sem("d_raw_rdy")
        conv_rdy = sem("d_conv_rdy")
        tap_rdy = sem("d_tap_rdy")
        silu_rdy = sem("d_silu_rdy")
        sqd_rdy = sem("d_sqd_rdy")
        norm_done = sem("d_norm_done")
        z_done = sem("d_z_done")
        z_rdy = sem("d_z_rdy")
        gate_step = sem("d_gate_step")
        act_step = sem("d_act_step")
        ssq_rdy = sem("d_ssq_rdy")
        rinv_step = sem("d_rinv_step")
        rinv_rdy = sem("d_rinv_rdy")
        sums_done = sem("d_sums_done")
        tick = {e: sem(f"d_tick_{e}") for e in ("pe", "act", "dve", "pool")}

        def rows(f):
            return P if f < 2 * GH else VB[f - 2 * GH][1]

        def convolved(f, b):
            if f < GH:
                return qT[:, f, bass.ds(b * SEQ, SEQ)]
            if f < 2 * GH:
                return kT[:, f - GH, bass.ds(b * SEQ, SEQ)]
            return vT[0:rows(f), f - 2 * GH, bass.ds(b * SEQ, SEQ)]

        block = ctx.enter_context(nc.Block())

        @block.sync
        def _(sp):
            for dst, src in ((w_qkv[:], dram["d_w_qkv"]), (w_abg[:], dram["d_w_abg"]), (w_conv[:], dram["d_w_conv"]),
                             (dt_bias[:], dram["d_dt_bias"].broadcast_to([P, GH])),
                             (a_log[:], dram["d_a_log"].broadcast_to([P, GH])), (tri[:], dram["d_tri"])):
                sp.dma_start(dst, src).then_inc(w_ld, 16)

        @block.tensor
        def _(pe):
            pe.wait_ge(w_ld, 96)
            pe.wait_ge(init, 1)
            with pe.Fori(0, BATCH) as b:
                for f in range(NBLK):
                    i = b * NBLK + f
                    m = rows(f)
                    pe.wait_ge(raw_rdy, i + 1)
                    pe.sem_inc(tick["pe"], 1)
                    for c in range(SEQ // 512):
                        mm = pe.matmul(proj[f % 2][0:m, 512 * c:512 * c + 512], w_qkv[:, P * f:P * f + m],
                                       xnT[:, bass.ds(b, 1), KCONV - 1 + 512 * c:KCONV - 1 + 512 * c + 512],
                                       start=True, stop=True)
                    mm.then_inc(proj_done, 1)
                    if f >= 2:
                        pe.wait_ge(sqd_rdy, b * 2 * GH + f - 1)
                        for k in range(TB):
                            mm = pe.matmul(norms[:, bass.ds(b * TB + (f - 2) * NT + k, 1)],
                                           sqd[f % 2][:, P * k:P * k + P], tri[:, 2, 0:1], start=True, stop=True,
                                           skip_group_check=True)
                        mm.then_inc(norm_done, 1)
            for t in range(NT):
                b, k = t // TB, t % TB
                if t >= 2:
                    pe.wait_ge(z_rdy, t - 1)
                pe.matmul(zp[t % 2][:, 0:2 * GH + VD], xnT[:, b, KCONV - 1 + P * k:KCONV - 1 + P * k + P], w_abg[:],
                          start=True, stop=True).then_inc(z_done, 1)
            pe.wait_ge(gate_step, GATE_G)
            for a in range(3):
                mm = pe.matmul(sums[:, SMALL * a:SMALL * a + SMALL], tri[:, a, :], logdecay[:].rearrange("p t h -> p (t h)"),
                               start=True, stop=True, skip_group_check=True)
            mm.then_inc(sums_done, 1)

        @block.scalar
        def _(act):
            act.wait_ge(init, 1)
            with act.Fori(0, BATCH) as b:
                def keep_raw(f):
                    i = b * NBLK + f
                    m = rows(f)
                    act.wait_ge(proj_done, i + 1)
                    act.wait_ge(conv_rdy, i + 1)
                    act.activation(raw[f % 2][0:m, KCONV - 1:], proj[f % 2][0:m, :], ACT.Copy).then_inc(raw_rdy, 1)

                keep_raw(0)
                for f in range(NBLK):
                    i = b * NBLK + f
                    m = rows(f)
                    if f + 1 < NBLK:
                        keep_raw(f + 1)
                    act.wait_ge(conv_rdy, i + 3)
                    act.sem_inc(tick["act"], 1)
                    act.activation(convolved(f, b), conv[f % 2][0:m, :], ACT.Silu).then_inc(silu_rdy, 1)
                    if f < 2 * GH:
                        act.wait_ge(silu_rdy, i + 3)
                        act.wait_ge(norm_done, b * 2 * GH + f + 1)
                        act.sem_inc(tick["act"], 1)
                        act.activation(sqd[f % 2][:], convolved(f, b), ACT.Square).then_inc(sqd_rdy, 1)
            for t in range(NT):
                act.wait_ge(z_done, t + 1)
                act.activation(gate[:, t, :], zp[t % 2][:, 2 * GH:2 * GH + VD], ACT.Silu)
                act.activation(zab[:, t, :], zp[t % 2][:, 0:2 * GH], ACT.Copy).then_inc(z_rdy, 1)
            act.wait_ge(z_rdy, NT)
            act.wait_ge(gate_step, 1)
            act.activation(beta[:], beta[:], ACT.Exp, scale=-1.0).then_inc(act_step, 1)
            act.activation(a_log[:], a_log[:], ACT.Exp).then_inc(act_step, 1)
            act.wait_ge(gate_step, 3)
            act.activation(e1[:], s1[:], ACT.Exp, scale=-1.0).then_inc(act_step, 1)
            act.wait_ge(sums_done, 1)
            act.activation(decay[:].rearrange("p a t h -> p (a t h)"), sums[:, 0:3 * SMALL], ACT.Exp).then_inc(act_step, 1)
            act.wait_ge(act_step, 4)

        @block.vector
        def _(dve):
            for i in range(2):
                dve.memset(raw[i][:, 0:KCONV - 1], 0.0).then_inc(init, 1) if i else dve.memset(raw[i][:, 0:KCONV - 1], 0.0)
            dve.sem_inc(raw_rdy, 2)
            dve.sem_inc(conv_rdy, 2)
            dve.sem_inc(silu_rdy, 2)
            dve.sem_inc(norm_done, 2)
            dve.wait_ge(w_ld, 96)
            with dve.Fori(0, BATCH) as b:
                for f in range(NBLK):
                    i = b * NBLK + f
                    m = rows(f)
                    x, y = raw[f % 2], conv[f % 2][0:m, :]
                    dve.wait_ge(raw_rdy, i + 3)
                    dve.wait_ge(silu_rdy, i + 1)
                    dve.tensor_scalar(y, x[0:m, 0:SEQ], w_conv[0:m, f, 0:1], None, ALU.mult).then_inc(tap_rdy, 1)
                    for j in range(1, KCONV):
                        dve.wait_ge(tap_rdy, i * (KCONV - 1) + j)
                        dve.sem_inc(tick["dve"], 1)
                        dve.scalar_tensor_tensor(y, x[0:m, j:j + SEQ], w_conv[0:m, f, j:j + 1], y, ALU.mult, ALU.add)\
                           .then_inc(tap_rdy if j < KCONV - 1 else conv_rdy, 1)
            dve.wait_ge(norm_done, 2 * 2 * GH + 2)
            dve.tensor_copy(ssq[:], norms[:, 0:2 * GH * NT]).then_inc(ssq_rdy, 1)

            steps = 0

            def step(ins):
                nonlocal steps
                steps += 1
                ins.then_inc(gate_step, 1)
                dve.wait_ge(gate_step, steps)

            def over(row):
                return row[:].rearrange("p (o h) -> p o h", o=1).to_broadcast([P, NT, GH])

            dve.wait_ge(z_rdy, NT)
            step(dve.tensor_scalar(beta[:], zab[:, :, GH:2 * GH], -EXP_MAX, None, ALU.max))
            step(dve.tensor_tensor(za[:], zab[:, :, 0:GH], over(dt_bias), ALU.add))
            step(dve.scalar_tensor_tensor(s1[:], za[:], -1.0, za[:], ALU.mult, ALU.max))
            dve.wait_ge(act_step, 3)
            step(dve.tensor_scalar(s2[:], e1[:], 2.0, None, ALU.add))
            step(dve.reciprocal(s2[:], s2[:]))
            step(dve.tensor_tensor(s1[:], e1[:], s2[:], ALU.mult))
            step(dve.tensor_tensor(s2[:], s1[:], s1[:], ALU.mult))
            step(dve.tensor_scalar(pl[:], s2[:], 1.0 / 17, None, ALU.mult))
            for k in SERIES:
                step(dve.scalar_tensor_tensor(pl[:], pl[:], 1.0 / k, s2[:], ALU.add, ALU.mult))
            step(dve.scalar_tensor_tensor(pl[:], pl[:], 1.0, s1[:], ALU.add, ALU.mult))
            step(dve.tensor_scalar(za[:], za[:], 0.0, None, ALU.max))
            step(dve.scalar_tensor_tensor(pl[:], pl[:], 2.0, za[:], ALU.mult, ALU.add))
            step(dve.scalar_tensor_tensor(logdecay[:], pl[:], -1.0, over(a_log), ALU.mult, ALU.mult))
            assert steps == GATE_G - 1
            step(dve.tensor_scalar(logdecay[:], logdecay[:], NEG, None, ALU.max))
            step(dve.tensor_scalar(beta[:], beta[:], 1.0, None, ALU.add))
            step(dve.reciprocal(beta[:], beta[:]))

        @block.gpsimd
        def _(pool):
            pool.wait_ge(ssq_rdy, 1)
            flat = rinv[:].rearrange("p f t -> p (f t)")
            rsqrt(pool, flat, ssq[:], rs_tmp[:], 0.0, 1e-6, rinv_step, 0, tick["pool"])
            pool.wait_ge(rinv_step, RSQRT_STEPS)
            pool.tensor_scalar(rinv[:, 0:GH, :], rinv[:, 0:GH, :], float(HK) ** -0.5, None, ALU.mult).then_inc(rinv_rdy, 1)
            pool.wait_ge(rinv_rdy, 1)


def delta_chunks(nc, spare, ident, identb, qT, kT, vT, gate, beta, logdecay, rinv, decay, dram):
    with ExitStack() as ctx:
        sb, ps, sem = buffers(nc, ctx)
        tri = sb("c_tri", [P, 3, P])
        causal = sb("c_causal", [P, P], BF16)
        blocks = sb("c_blocks", [P, LEVELS, P], BF16)
        two = range(BATCH)

        def each(name, shape, dt=F32):
            return [sb(f"c_{name}{b}", shape, dt) for b in two]

        kt_in = each("kt_in", [P, GH, P])
        kq = each("kq", [P, GH, 2, P])
        vt_in = each("vt_in", [P, 2, P])
        kn = each("kn", [P, GH, P])
        kb = each("kb", [P, GH, P])
        m1 = each("m1", [P, GH, P])
        atm1 = each("atm1", [P, GH, P])
        gt = each("gt", [P, GH, P])
        at = each("at", [P, GH, P])
        mt = [spare[:, GH * P * b:GH * P * (b + 1)].rearrange("p (h t) -> p h t", h=GH) for b in two]
        bv = [spare[:, 2 * GH * P + VD * b:2 * GH * P + VD * (b + 1)].rearrange("p (h v) -> p h v", h=GH) for b in two]
        rhs = each("rhs", [P, GH, HV])
        upd = each("upd", [P, GH, HV])
        state = each("state", [P, GH, HV])
        knT, u, inv, invT, out = kt_in, kb, kt_in, gt, bv
        atm = [m1, atm1]

        g0 = [ps(f"c_g0{b}", [P, 1024]) for b in two]
        g1 = [ps(f"c_g1{b}", [P, 1024]) for b in two]

        def heads(buf):
            return buf[:, 0:GH * P].rearrange("p (h t) -> p h t", h=GH)

        def sems(name):
            return [sem(f"c_{name}{b}") for b in two]

        const_ld = sem("c_const_ld")
        init = sem("c_init")
        tile_in, turned, kn_rdy, m1_rdy, kb_rdy, kdec_rdy = (sems(x) for x in
            ("tile_in", "turned", "kn_rdy", "m1_rdy", "kb_rdy", "kdec_rdy"))
        kT_done, kT_rdy, gam_done, gt_rdy, kk_done, qk_done = (sems(x) for x in
            ("kT_done", "kT_rdy", "gam_done", "gt_rdy", "kk_done", "qk_done"))
        at_rdy, mt_rdy, atm_rdy, tt0_rdy, t0_done, t0_rdy = (sems(x) for x in
            ("at_rdy", "mt_rdy", "atm_rdy", "tt0_rdy", "t0_done", "t0_rdy"))
        u_done, u_rdy, w_done, t_rdy, tt_done, tt_rdy, ttf_rdy = (sems(x) for x in
            ("u_done", "u_rdy", "w_done", "t_rdy", "tt_done", "tt_rdy", "ttf_rdy"))
        po_done, rhs_step, d_done, d_rdy, od_done, s_step, s_rdy, o_step, out_rdy = (sems(x) for x in
            ("po_done", "rhs_step", "d_done", "d_rdy", "od_done", "s_step", "s_rdy", "o_step", "out_rdy"))
        tick = {e: sem(f"c_tick_{e}") for e in ("pe", "act", "dve", "pool")}
        LV = LEVELS - 1
        block = ctx.enter_context(nc.Block())

        @block.sync
        def _(sp):
            sp.dma_start(tri[:], dram["d_tri"]).then_inc(const_ld, 16)
            sp.dma_start(causal[:], dram["d_causal"]).then_inc(const_ld, 16)
            sp.dma_start(blocks[:], dram["d_blocks"]).then_inc(const_ld, 16)

        @block.tensor
        def _(pe):
            pe.wait_ge(const_ld, 48)
            pe.wait_ge(init, 1)
            with pe.Fori(0, TB) as i:
                for b in two:
                    pe.wait_ge(tile_in[b], i + 1)
                    pe.wait_ge(out_rdy[b], i + 1)
                    for h in range(GH):
                        pe.transpose(heads(g0[b])[:, h, :], kt_in[b][:, h, :], ident[:])
                    for c, (c0, cn) in enumerate(VB):
                        mm = pe.transpose(g1[b][:, c0:c0 + cn], vt_in[b][0:cn, c, :], ident[0:cn, 0:cn])
                    mm.then_inc(turned[b], 1)
                for b in two:
                    pe.wait_ge(kn_rdy[b], i + 1)
                    for h in range(GH):
                        mm = pe.transpose(heads(g0[b])[:, h, :], kn[b][:, h, :], ident[:])
                    mm.then_inc(kT_done[b], 1)
                    pe.wait_ge(kb_rdy[b], i + 1)
                    for h in range(GH):
                        mm = pe.transpose(heads(g1[b])[:, h, :], kb[b][:, h, :], ident[:])
                    mm.then_inc(kT_done[b], 1)
                for b in two:
                    pe.wait_ge(kT_rdy[b], i * 2 + 1)
                    pe.wait_ge(m1_rdy[b], i + 1)
                    for h0, hn in ((0, 4), (4, 2)):
                        pe.matmul(heads(g0[b])[:, h0:h0 + hn, :], identb[:],
                                  causal[:].rearrange("p (o t) -> p o t", o=1).to_broadcast([P, hn, P]),
                                  start=True, stop=False, skip_group_check=True)
                        for h in range(h0, h0 + hn):
                            mm = pe.matmul(heads(g0[b])[:, h, :], m1[b][:, h, :], tri[:, 0, :], start=False, stop=True,
                                           skip_group_check=True)
                    mm.then_inc(gam_done[b], 1)
                for b in two:
                    pe.wait_ge(kT_rdy[b], i * 2 + 2)
                    for h in range(GH):
                        mm = pe.matmul(heads(g1[b])[:, h, :], knT[b][:, h, :], kq[b][:, h, 0, :], start=True, stop=True,
                                       skip_group_check=True)
                    mm.then_inc(kk_done[b], 1)
                    pe.wait_ge(gt_rdy[b], i + 1)
                    for h in range(GH):
                        mm = pe.matmul(heads(g0[b])[:, h, :], knT[b][:, h, :], kq[b][:, h, 1, :], start=True, stop=True,
                                       skip_group_check=True)
                    mm.then_inc(qk_done[b], 1)
                for b in two:
                    pe.wait_ge(tt0_rdy[b], i + 1)
                    for h in range(GH):
                        mm = pe.transpose(heads(g1[b])[:, h, :], invT[b][:, h, :], ident[:])
                    mm.then_inc(t0_done[b], 1)
                for l in range(1, LEVELS):
                    for b in two:
                        pe.wait_ge(atm_rdy[b], i * LEVELS + l + 1)
                        if l == 1:
                            pe.wait_ge(t0_rdy[b], i + 1)
                            pe.wait_ge(mt_rdy[b], i + 1)
                        else:
                            pe.wait_ge(t_rdy[b], i * (LV - 1) + l - 1)
                            pe.wait_ge(tt_rdy[b], i * (LV - 1) + l - 1)
                        for h in range(GH):
                            mm = pe.matmul(heads(g0[b])[:, h, :], atm[l % 2][b][:, h, :], inv[b][:, h, :], start=True,
                                           stop=True, skip_group_check=True)
                        mm.then_inc(u_done[b], 1)
                    for b in two:
                        pe.wait_ge(u_rdy[b], i * LV + l)
                        for h in range(GH):
                            if l < LV:
                                mm = pe.matmul(heads(g1[b])[:, h, :], invT[b][:, h, :], u[b][:, h, :], start=True,
                                               stop=True, skip_group_check=True)
                            else:
                                mm = pe.matmul(heads(g1[b])[:, h, :], u[b][:, h, :], invT[b][:, h, :], start=True,
                                               stop=True, skip_group_check=True)
                        mm.then_inc(w_done[b], 1)
                    if l < LV:
                        for b in two:
                            pe.wait_ge(t_rdy[b], i * (LV - 1) + l)
                            for h in range(GH):
                                mm = pe.transpose(heads(g0[b])[:, h, :], inv[b][:, h, :], ident[:])
                            mm.then_inc(tt_done[b], 1)
                for b in two:
                    pe.wait_ge(ttf_rdy[b], i + 1)
                    pe.wait_ge(s_rdy[b], i + 1)
                    for a in range(2):
                        for h in range(GH):
                            mm = pe.matmul(g1[b][:, VD * a + HV * h:VD * a + HV * h + HV], kq[b][:, h, a, :],
                                           state[b][:, h, :], start=True, stop=True, skip_group_check=True)
                    mm.then_inc(po_done[b], 1)
                for b in two:
                    pe.wait_ge(rhs_step[b], i * 2 + 2)
                    for h in range(GH):
                        mm = pe.matmul(g0[b][:, HV * h:HV * h + HV], invT[b][:, h, :], rhs[b][:, h, :], start=True,
                                       stop=True, skip_group_check=True)
                    mm.then_inc(d_done[b], 1)
                for b in two:
                    pe.wait_ge(d_rdy[b], i + 1)
                    pe.wait_ge(kdec_rdy[b], i + 1)
                    for h in range(GH):
                        pe.matmul(g0[b][:, 512 + HV * h:512 + HV * h + HV], mt[b][:, h, :], upd[b][:, h, :], start=True,
                                  stop=True, skip_group_check=True)
                    for h in range(GH):
                        mm = pe.matmul(g0[b][:, 512 + VD + HV * h:512 + VD + HV * h + HV], kn[b][:, h, :],
                                       upd[b][:, h, :], start=True, stop=True, skip_group_check=True)
                    mm.then_inc(od_done[b], 1)

        @block.scalar
        def _(act):
            def keep(dst, src, done, value, rdy, func=ACT.Copy):
                act.wait_ge(done, value)
                act.activation(dst, src, func).then_inc(rdy, 1)

            with act.Fori(0, TB) as i:
                for b in two:
                    keep(knT[b][:], heads(g0[b]), kT_done[b], i * 2 + 1, kT_rdy[b])
                    keep(kq[b][:, :, 0, :], heads(g1[b]), kT_done[b], i * 2 + 2, kT_rdy[b])
                for b in two:
                    keep(gt[b][:], heads(g0[b]), gam_done[b], i + 1, gt_rdy[b], ACT.Exp)
                for b in two:
                    keep(inv[b][:], heads(g1[b]), t0_done[b], i + 1, t0_rdy[b])
                for l in range(1, LEVELS):
                    for b in two:
                        keep(u[b][:], heads(g0[b]), u_done[b], i * LV + l + 1, u_rdy[b])
                    if l < LV:
                        for b in two:
                            keep(invT[b][:], heads(g0[b]), tt_done[b], i * (LV - 1) + l, tt_rdy[b])
                for b in two:
                    keep(upd[b][:].rearrange("p h v -> p (h v)"), g0[b][:, 0:VD], d_done[b], i + 1, d_rdy[b])

        @block.vector
        def _(dve):
            def across(small, n):
                return small.rearrange("p (h o) -> p h o", o=1).to_broadcast([P, GH, n])

            for b in two:
                mm = dve.memset(state[b][:], 0.0)
            mm.then_inc(init, 1)
            for b in two:
                dve.sem_inc(s_rdy[b], 1)
                dve.sem_inc(out_rdy[b], 1)
                dve.sem_inc(u_done[b], 1)
            dve.wait_ge(const_ld, 48)
            with dve.Fori(0, TB) as i:
                for b in two:
                    t0 = i * P + b * SEQ
                    dve.tensor_copy(kq[b][:, :, 1, :], qT[:, :, bass.ds(t0, P)])
                    dve.tensor_copy(vt_in[b][:], vT[:, :, bass.ds(t0, P)])
                    dve.tensor_copy(kt_in[b][:], kT[:, :, bass.ds(t0, P)]).then_inc(tile_in[b], 1)
                for b in two:
                    t = i + b * TB
                    small = lambda x: x.rearrange("p a h -> p (a h)")
                    dve.wait_ge(turned[b], i + 1)
                    dve.tensor_tensor(bv[b], g1[b][:, 0:VD].rearrange("p (h v) -> p h v", h=GH),
                                      across(small(beta[:, bass.ds(t, 1), :]), HV), ALU.mult)
                    dve.tensor_tensor(kn[b][:], heads(g0[b]),
                                      across(rinv[:, GH:2 * GH, bass.ds(t, 1)].rearrange("p h a -> p (h a)"), P),
                                      ALU.mult).then_inc(kn_rdy[b], 1)
                for b in two:
                    dve.wait_ge(gt_rdy[b], i + 1)
                    dve.wait_ge(kk_done[b], i + 1)
                    dve.tensor_tensor(at[b][:], heads(g1[b]), gt[b][:], ALU.mult).then_inc(at_rdy[b], 1)
                    dve.wait_ge(qk_done[b], i + 1)
                    dve.tensor_tensor(mt[b], heads(g0[b]), gt[b][:], ALU.mult).then_inc(mt_rdy[b], 1)
                for b in two:
                    dve.wait_ge(mt_rdy[b], i + 1)
                    dve.wait_ge(atm_rdy[b], i * LEVELS + 1)
                    dve.tensor_tensor(invT[b][:], ident[:].rearrange("p (o t) -> p o t", o=1).to_broadcast([P, GH, P]),
                                      atm[0][b][:], ALU.subtract).then_inc(tt0_rdy[b], 1)
                for l in range(1, LV):
                    for b in two:
                        dve.wait_ge(w_done[b], i * LV + l)
                        dve.tensor_tensor(inv[b][:], inv[b][:], heads(g1[b]), ALU.subtract).then_inc(t_rdy[b], 1)
                for b in two:
                    dve.wait_ge(w_done[b], i * LV + LV)
                    dve.tensor_tensor(invT[b][:], invT[b][:], heads(g1[b]), ALU.subtract).then_inc(ttf_rdy[b], 1)
                small = lambda x: x.rearrange("p a h -> p (a h)")
                for b in two:
                    t = i + b * TB
                    upto = across(small(decay[:, 0, bass.ds(t, 1), :]), HV)
                    whole = across(small(decay[:, 2, bass.ds(t, 1), :]), HV)
                    po = g1[b][:, 0:2 * VD].rearrange("p (a h v) -> p a h v", a=2, h=GH)
                    dve.wait_ge(po_done[b], i + 1)
                    dve.tensor_tensor(rhs[b][:], po[:, 0], upto, ALU.mult).then_inc(rhs_step[b], 1)
                    dve.wait_ge(rhs_step[b], i * 2 + 1)
                    dve.tensor_tensor(rhs[b][:], bv[b], rhs[b][:], ALU.subtract).then_inc(rhs_step[b], 1)
                    dve.tensor_tensor(state[b][:], state[b][:], whole, ALU.mult).then_inc(s_step[b], 1)
                    dve.wait_ge(rhs_step[b], i * 2 + 2)
                    dve.tensor_tensor(out[b], po[:, 1], upto, ALU.mult).then_inc(o_step[b], 1)
                for b in two:
                    t = i + b * TB
                    od = g0[b][:, 512:512 + 2 * VD].rearrange("p (a h v) -> p a h v", a=2, h=GH)
                    dve.wait_ge(od_done[b], i + 1)
                    dve.wait_ge(s_step[b], i + 1)
                    dve.tensor_tensor(state[b][:], state[b][:], od[:, 1], ALU.add).then_inc(s_rdy[b], 1)
                    dve.wait_ge(o_step[b], i * 3 + 1)
                    dve.tensor_tensor(out[b], out[b], od[:, 0], ALU.add).then_inc(o_step[b], 1)
                    dve.wait_ge(o_step[b], i * 3 + 2)
                    dve.tensor_tensor(out[b], out[b],
                                      across(rinv[:, 0:GH, bass.ds(t, 1)].rearrange("p h a -> p (h a)"), HV),
                                      ALU.mult).then_inc(o_step[b], 1)
                    dve.wait_ge(o_step[b], i * 3 + 3)
                    gt_tile = gate[:, bass.ds(t, 1), :].rearrange("p a f -> p (a f)")
                    dve.tensor_tensor(gt_tile, out[b].rearrange("p h v -> p (h v)"), gt_tile, ALU.mult)\
                       .then_inc(out_rdy[b], 1)
            for b in two:
                dve.wait_ge(out_rdy[b], TB + 1)

        @block.gpsimd
        def _(pool):
            def across(small):
                return small.rearrange("p a h -> p (a h)").rearrange("p (h o) -> p h o", o=1).to_broadcast([P, GH, P])

            def over(mask):
                return mask.rearrange("p (o t) -> p o t", o=1).to_broadcast([P, GH, P])

            pool.wait_ge(const_ld, 48)
            with pool.Fori(0, TB) as i:
                for b in two:
                    t = i + b * TB
                    pool.wait_ge(u_done[b], i * LV + 1)
                    pool.sem_inc(tick["pool"], 1)
                    pool.tensor_tensor(m1[b][:], over(tri[:, 1, :]), across(logdecay[:, bass.ds(t, 1), :]),
                                       ALU.mult).then_inc(m1_rdy[b], 1)
                for b in two:
                    t = i + b * TB
                    pool.wait_ge(kn_rdy[b], i + 1)
                    pool.sem_inc(tick["pool"], 1)
                    pool.tensor_tensor(kb[b][:], kn[b][:], across(beta[:, bass.ds(t, 1), :]), ALU.mult).then_inc(kb_rdy[b], 1)
                for b in two:
                    t = i + b * TB
                    pool.wait_ge(kT_done[b], i * 2 + 1)
                    pool.wait_ge(kb_rdy[b], i + 1)
                    pool.sem_inc(tick["pool"], 1)
                    pool.tensor_tensor(kn[b][:], kn[b][:], across(decay[:, 1, bass.ds(t, 1), :]), ALU.mult)\
                        .then_inc(kdec_rdy[b], 1)
                for l in range(LEVELS):
                    for b in two:
                        if l == 0:
                            pool.wait_ge(at_rdy[b], i + 1)
                        elif l == 2:
                            pool.wait_ge(tt0_rdy[b], i + 1)
                        elif l > 2:
                            pool.wait_ge(u_done[b], i * LV + l - 1)
                        pool.tensor_tensor(atm[l % 2][b][:], at[b][:], over(blocks[:, l, :]), ALU.mult)\
                            .then_inc(atm_rdy[b], 1)


def delta_outputs(nc, x, ident, og, dram):
    with ExitStack() as ctx:
        sb, ps, sem = buffers(nc, ctx)
        nw = sb("o_nw", [P, VD])
        wo = sb("o_wo", [P, len(VB), D])
        sq = [sb(f"o_sq{i}", [P, VD]) for i in range(2)]
        ms = sb("o_ms", [P, NT])
        rstd = sb("o_rstd", [P, NT])
        tmp = sb("o_tmp", [P, NT])
        on = [sb(f"o_on{i}", [P, VD]) for i in range(2)]
        oT = [sb(f"o_oT{i}", [P, len(VB), P]) for i in range(2)]
        tp = [ps(f"o_tp{i}", [P, 512]) for i in range(2)]
        yp = [ps(f"o_yp{i}", [P, 512]) for i in range(2)]
        x_ld, w_ld, ms_rdy, rs_rdy, on_rdy, tp_done, oT_rdy, y_done, x_rdy, tick = (sem("o_" + s) for s in (
            "x_ld", "w_ld", "ms_rdy", "rs_rdy", "on_rdy", "tp_done", "oT_rdy", "y_done", "x_rdy", "tick"))
        block = ctx.enter_context(nc.Block())

        @block.sync
        def _(sp):
            sp.dma_start(nw[:], dram["d_nw"].broadcast_to([P, VD])).then_inc(w_ld, 16)
            sp.dma_start(wo[:], dram["d_wo"]).then_inc(w_ld, 16)

        @block.scalar
        def _(act):
            act.dma_start(x[:], dram["x"].rearrange("(t p) d -> p t d", p=P)).then_inc(x_ld, 16)
            for t in range(NT):
                if t >= 2:
                    act.wait_ge(ms_rdy, t - 1)
                act.activation(sq[t % 2][:], og[:, t, :], ACT.Square, scale=float(VD) ** -0.5, accum_out=ms[:, t:t + 1]).then_inc(ms_rdy, 1)
            for t in range(NT):
                act.wait_ge(tp_done, t + 1)
                for c, (c0, cn) in enumerate(VB):
                    last = act.activation(oT[t % 2][0:cn, c, :], tp[t % 2][0:cn, P * c:P * c + P], ACT.Copy)
                last.then_inc(oT_rdy, 1)

        @block.gpsimd
        def _(pool):
            pool.wait_ge(ms_rdy, NT)
            rsqrt(pool, rstd[:], ms[:], tmp[:], 0.0, 1e-5, rs_rdy, 0, tick)

        @block.vector
        def _(dve):
            dve.wait_ge(w_ld, 32)
            dve.wait_ge(rs_rdy, RSQRT_STEPS)
            dve.wait_ge(x_ld, 16)
            for t in range(NT):
                if t >= 2:
                    dve.wait_ge(tp_done, t - 1)
                dve.scalar_tensor_tensor(on[t % 2][:], og[:, t, :], rstd[:, t:t + 1], nw[:], ALU.mult, ALU.mult).then_inc(on_rdy, 1)
                if t >= 1:
                    dve.wait_ge(y_done, t)
                    dve.tensor_tensor(x[:, t - 1, :], x[:, t - 1, :], yp[(t - 1) % 2][:, 0:D], ALU.add).then_inc(x_rdy, 1)
            dve.wait_ge(y_done, NT)
            dve.tensor_tensor(x[:, NT - 1, :], x[:, NT - 1, :], yp[(NT - 1) % 2][:, 0:D], ALU.add).then_inc(x_rdy, 1)
            dve.wait_ge(x_rdy, NT)

        @block.tensor
        def _(pe):
            pe.wait_ge(w_ld, 32)
            for t in range(NT):
                pe.wait_ge(on_rdy, t + 1)
                if t >= 2:
                    pe.wait_ge(oT_rdy, t - 1)
                for c, (c0, cn) in enumerate(VB):
                    mm = pe.transpose(tp[t % 2][0:cn, P * c:P * c + P], on[t % 2][:, c0:c0 + cn], ident[:])
                mm.then_inc(tp_done, 1)
                pe.wait_ge(oT_rdy, t + 1)
                if t >= 2:
                    pe.wait_ge(x_rdy, t - 1)
                for c, (c0, cn) in enumerate(VB):
                    mm = pe.matmul(yp[t % 2][:, 0:D], oT[t % 2][0:cn, c, :], wo[0:cn, c, :], start=(c == 0), stop=(c == 1))
                mm.then_inc(y_done, 1)


def delta_constants():
    r, t = np.arange(P)[:, None], np.arange(P)[None, :]
    tri = np.stack([r <= t, r > t, np.ones((P, P), bool)], 1).astype(np.float32)
    causal = np.where(t < r, np.float32(NEG), np.float32(0))
    blocks = np.stack([(r // (2 * n) == t // (2 * n)) & (t % (2 * n) >= n) & (r % (2 * n) < n)
                       for n in (1 << l for l in range(LEVELS))], 1).astype(np.float32)
    return np.ascontiguousarray(tri), causal, np.ascontiguousarray(blocks)


def pack_delta_weights(q_w, k_w, v_w, a_w, b_w, g_w, o_w, conv_q_w, conv_k_w, conv_v_w):
    w_qkv = np.ascontiguousarray(np.concatenate([q_w, k_w, v_w], 0).T)
    w_abg = np.ascontiguousarray(np.concatenate([a_w, b_w, g_w], 0).T)
    conv = np.zeros((NBLK * P, KCONV), np.float32)
    conv[0:2 * KD + VD] = np.concatenate([conv_q_w, conv_k_w, conv_v_w], 0)
    wo = np.zeros((len(VB) * P, D), np.float32)
    wo[0:VD] = o_w.T
    return (w_qkv, w_abg, np.ascontiguousarray(conv.reshape(NBLK, P, KCONV).transpose(1, 0, 2)),
            np.ascontiguousarray(wo.reshape(len(VB), P, D).transpose(1, 0, 2)))

DEPTH, HEADS, DH, WIN = 6, 16, 64, 32
INNER = HEADS * DH
DFF = int(D * 4 * 2 / 3)
HP = HEADS // 2
NWIN = P // WIN
FB = [(0, 128), (128, 128), (256, DFF - 256)]
C_QKV, C_WO = 0, 3 * INNER
C_W1 = C_WO + HP * D
C_W2 = C_W1 + 2 * DFF
C_B1 = C_W2 + len(FB) * D
C_LN = C_B1 + 2 * len(FB)
NWC = C_LN + 2
PADK = P - WIN


def local_layers(nc, h, ident, identb, dram):
    with ExitStack() as ctx:
        sb, ps, sem = buffers(nc, ctx)

        wts = [sb(f"l_wts{i}", [P, NWC]) for i in range(2)]
        scales = [sb(f"l_scales{i}", [P, 4, DH]) for i in range(2)]
        b2row = [sb(f"l_b2row{i}", [1, D]) for i in range(2)]
        raw_tab = sb("l_raw_tab", [P, 4, TB, DH])
        tab = sb("l_tab", [P, 4, NT, DH])
        maskb = sb("l_maskb", [P, NT, 2 * WIN], BF16)
        carried = sb("l_carried", [P, NT])
        ones_row = sb("l_ones_row", [1, P])
        hcur = [sb(f"l_hcur{i}", [P, D]) for i in range(2)]
        xs = [sb(f"l_xs{i}", [P, 1 + P]) for i in range(2)]
        sq = sb("l_sq", [P, 2, 512])
        ss = sb("l_ss", [P, 2 * HEADS])
        rn = sb("l_rn", [P, 2 * HEADS])
        rn_tmp = sb("l_rn_tmp", [P, 2 * HEADS])
        rot_a = sb("l_rot_a", [P, 4, 512])
        rot_b = sb("l_rot_b", [P, 4, 512])
        qk = sb("l_qk", [P, 4, 512])
        qT = [sb(f"l_qT{i}", [P, HP, P]) for i in range(2)]
        kT = [sb(f"l_kT{i}", [P, HP, WIN + P]) for i in range(2)]
        v = [sb(f"l_v{i}", [P, HEADS, DH + 1]) for i in range(2)]
        vprev = sb("l_vprev", [P, HEADS, DH + 1])
        mx = sb("l_mx", [P, HEADS])
        sd = sb("l_sd", [P, HEADS, 2 * WIN])
        pw = sb("l_pw", [P, HEADS + 1, 2 * WIN])
        pT = sb("l_pT", [P, 2, HP, P])
        rsum = sb("l_rsum", [P, HEADS])
        on = sb("l_on", [P, HEADS, DH])
        oT = sb("l_oT", [P, HP, P])
        GT = 4
        NG = NT // GT
        hgrp = [sb(f"l_hgrp{i}", [P, GT, D]) for i in range(2)]
        xs4 = [sb(f"l_xs4{i}", [P, 1 + GT * P]) for i in range(2)]
        st = [sb(f"l_st{i}", [P, GT, 6]) for i in range(2)]
        mv = [sb(f"l_mv{i}", [P, GT, 2]) for i in range(2)]
        rstd = [sb(f"l_rstd{i}", [P, GT]) for i in range(2)]
        rstd_tmp = [sb(f"l_rstd_tmp{i}", [P, GT]) for i in range(2)]
        xn = sb("l_xn", [P, GT, D])
        xnT = sb("l_xnT", [P, GT * P])
        gl = sb("l_gl", [P, 3, 512])
        u = sb("l_u", [P, 3, 512])

        bank = [ps(f"l_bank{i}", [P, 512]) for i in range(2)]
        score = ps("l_score", [P, HEADS, 2 * WIN])
        tp = [ps(f"l_tp{i}", [P, 512]) for i in range(2)]
        misc = [ps(f"l_misc{i}", [P, 512]) for i in range(2)]

        wide = [misc[0][:], misc[1][:], score[:, 0:8, :].rearrange("p a b -> p (a b)")]
        y_ps = score[:, 8:16, :].rearrange("p a b -> p (a b)")

        const_ld = sem("l_const_ld")
        init = sem("l_init")
        w_ld = [sem(f"l_w_ld{i}") for i in range(2)]
        layer_done = sem("l_layer_done")
        tab_rdy = sem("l_tab_rdy")
        hcur_rdy = sem("l_hcur_rdy")
        xT_done = sem("l_xT_done")
        xs_rdy = sem("l_xs_rdy")
        carry_rdy = sem("l_carry_rdy")
        proj_done = sem("l_proj_done")
        vproj_done = sem("l_vproj_done")
        sq_rdy = sem("l_sq_rdy")
        v_rdy = sem("l_v_rdy")
        ss_rdy = sem("l_ss_rdy")
        rope_rdy = sem("l_rope_rdy")
        rn_rdy = sem("l_rn_rdy")
        rot_sum = sem("l_rot_sum")
        qk_rdy = sem("l_qk_rdy")
        qkT_done = sem("l_qkT_done")
        qkT_rdy = sem("l_qkT_rdy")
        kprev_rdy = sem("l_kprev_rdy")
        s_done = sem("l_s_done")
        mx_rdy = sem("l_mx_rdy")
        sd_rdy = sem("l_sd_rdy")
        p_rdy = sem("l_p_rdy")
        pT_done = sem("l_pT_done")
        pT_rdy = sem("l_pT_rdy")
        pv_own = sem("l_pv_own")
        pv_done = sem("l_pv_done")
        vprev_rdy = sem("l_vprev_rdy")
        rs_rdy = sem("l_rs_rdy")
        on_rdy = sem("l_on_rdy")
        oT_done = sem("l_oT_done")
        oT_rdy = sem("l_oT_rdy")
        y_done = sem("l_y_done")
        h_rdy = sem("l_h_rdy")
        g_hgrp = sem("l_g_hgrp")
        g_xT = sem("l_g_xT")
        g_xs = sem("l_g_xs")
        g_back = sem("l_g_back")
        g_st = sem("l_g_st")
        g_mv = sem("l_g_mv")
        g_rstd = sem("l_g_rstd")
        g_xn = sem("l_g_xn")
        g_xnT = sem("l_g_xnT")
        g_xnT_rdy = sem("l_g_xnT_rdy")
        g_w1 = sem("l_g_w1")
        g_gl = sem("l_g_gl")
        g_u = sem("l_g_u")
        g_y = sem("l_g_y")
        g_h = sem("l_g_h")
        tick = {e: sem(f"l_tick_{e}") for e in ("pe", "act", "dve", "pool")}

        PAIRS = DEPTH // 2
        block = ctx.enter_context(nc.Block())

        def by_layer(eng, attention, geglu):
            with eng.Fori(0, PAIRS) as lp:
                for par in range(2):
                    attention(lp, par, lp * (2 * NT) + par * NT)
                    geglu(lp, par, lp * 8 + par * 4)

        def slot(head):
            return HP * (head % 2) + head // 2

        def by_tile(start, tile, finish, eng, n0):
            start()
            tile(0, n0, 0, False, True, True)
            with eng.Fori(0, (NT - 4) // 2) as j:
                tile(j * 2 + 1, n0 + j * 2 + 1, 1, True, True, True)
                tile(j * 2 + 2, n0 + j * 2 + 2, 0, True, True, True)
            tile(NT - 3, n0 + NT - 3, 1, True, True, True)
            tile(NT - 2, n0 + NT - 2, 0, True, True, False)
            tile(NT - 1, n0 + NT - 1, 1, True, False, False)
            finish()

        @block.sync
        def _(sp):
            sp.dma_start(raw_tab[:], dram["l_tables"]).then_inc(const_ld, 16)
            sp.dma_start(maskb[:], dram["l_mask"]).then_inc(const_ld, 16)
            sp.dma_start(carried[:], dram["l_carried"]).then_inc(const_ld, 16)
            with sp.Fori(0, PAIRS) as lp:
                for par in range(2):
                    sp.wait_ge(layer_done, lp * 2 + par + 1)
                    sp.dma_start(wts[par][:], dram["l_wts"][bass.ds(lp * 2 + par, 1)].rearrange("a p n -> (a p) n")).then_inc(w_ld[par], 16)
                    sp.dma_start(scales[par][:].rearrange("p a d -> p (a d)"),
                                 dram["l_scales"][bass.ds(lp * 2 + par, 1)].broadcast_to([P, 4 * DH])).then_inc(w_ld[par], 16)
                    sp.dma_start(b2row[par][:], dram["l_b2"][bass.ds(lp * 2 + par, 1)]).then_inc(w_ld[par], 16)

        @block.tensor
        def _(pe):
            def attention(lp, par, n0):
                w = wts[par]

                def scores_masked(t, n):
                    pe.wait_ge(qkT_rdy, n * 4 + 4 + 1)
                    pe.wait_ge(kprev_rdy, n + 1)
                    for c in range(2):
                        pe.matmul(score[:, 8 * c:8 * c + 8, :], identb[:],
                                  maskb[:, bass.ds(t, 1), :].to_broadcast([P, 8, 2 * WIN]),
                                  start=True, stop=False, skip_group_check=True)

                def scores(p, wds):
                    for wd in wds:
                        for hh in range(HEADS):
                            r = slice(DH * (hh % 2), DH * (hh % 2) + DH)
                            keys = kT[p][r, hh // 2, WIN * wd:WIN * wd + 2 * WIN].rearrange("d (b k) -> d b k", b=2)
                            if wd % 2 == 0:
                                keys = keys[:, ::-1, :]
                            last = pe.matmul(score[WIN * wd:WIN * wd + WIN, slot(hh), :],
                                             qT[p][r, hh // 2, WIN * wd:WIN * wd + WIN], keys,
                                             start=False, stop=True, skip_group_check=True)
                    if wd == NWIN - 1:
                        last.then_inc(s_done, 1)

                def turn_in(n, p):
                    pe.wait_ge(hcur_rdy, n + 1)
                    pe.transpose(tp[1][:, 0:P], hcur[p][:], ident[:]).then_inc(xT_done, 1)

                def project(n, p, vs, js):
                    for j in js:
                        if j == 0:
                            pe.wait_ge(carry_rdy, n + 1)
                            pe.wait_ge(xs_rdy, n + 2)
                        if j < 2:
                            pe.wait_ge(v_rdy, vs * 2 + j + 1)
                        pe.wait_ge(rope_rdy, n * 4 + j - 2 + 3)
                        pe.wait_ge(sq_rdy, n * 4 + j - 2 + 3)
                        pe.matmul(bank[j % 2][:], xs[p][:, 0:P], w[:, C_QKV + 512 * j:C_QKV + 512 * j + 512],
                                  start=True, stop=True).then_inc(proj_done, 1)

                def project_v(n, p, ahead, j):
                    pe.wait_ge(rope_rdy, (n + ahead) * 4 + j + 3 + 2)
                    pe.wait_ge(v_rdy, n * 2 + j + 1)
                    c = C_QKV + 2 * INNER + 512 * j
                    pe.matmul(bank[j][:], xs[p][:, 0:P], w[:, c:c + 512], start=True, stop=True).then_inc(vproj_done, 1)

                def turn_probs(m, ahead):
                    pe.wait_ge(p_rdy, m + 1)
                    for c in range(4):
                        if c >= 2:
                            pe.wait_ge(pT_rdy, m * 4 + c - 1)
                        elif ahead:
                            pe.wait_ge(qkT_rdy, m * 4 + 4 + c + 3 + 1)
                        for k in range(4):
                            first = 2 * (4 * (c // 2) + k) - (c % 2 == 0)
                            first = first % HEADS if first < 0 else first
                            pair = pw[:, first:first + 2, :].rearrange("q a k -> q (a k)")
                            last = pe.transpose(tp[c % 2][:, P * k:P * k + P], pair, ident[:])
                        last.then_inc(pT_done, 1)

                def probs(s, upper, keys, queries):
                    if (s % 2 == 0) == upper:
                        return pT[keys, 1, s // 2, queries]
                    return pT[keys, 0, (s + 1) // 2 % HP, queries]

                def values(m, p, half):
                    pe.wait_ge(vprev_rdy, m + 2)
                    pe.wait_ge(v_rdy, m * 2 + 4)
                    win = [slice(WIN * wd, WIN * wd + WIN) for wd in range(NWIN)]
                    low, high = slice(0, 2 * WIN), slice(2 * WIN, 4 * WIN)

                    def part(c, step):
                        o = misc[(c + 1) % 2]
                        for k in range(4):
                            s = 4 * c + k
                            hh = 2 * (s % HP) + s // HP
                            cols = slice(65 * k, 65 * k + 65)
                            if step == 0:
                                todo = ((1, True, low, v[p]), (3, False, high, v[p]), (0, True, win[0], v[p]), (2, False, win[2], v[p]))
                            else:
                                todo = ((0, False, win[3], vprev), (2, True, win[1], v[p]))
                            for wd, upper, keys, vals in todo:
                                last = pe.matmul(o[win[wd], cols], probs(s, upper, keys, win[wd]), vals[keys, hh, :],
                                                 start=(step == 0 and k == 0), stop=(step == 1 or wd % 2 == 1), skip_group_check=True)
                        last.then_inc(pv_own if step == 0 else pv_done, 1)

                    for c in (2 * half, 2 * half + 1):
                        if c < 3:
                            pe.wait_ge(pT_rdy, m * 4 + c + 2)
                        if c == 0:
                            pe.wait_ge(h_rdy, m + 2)
                        if c >= 2:
                            pe.wait_ge(on_rdy, m * 4 + c - 1)
                        pe.sem_inc(tick["pe"], 1)
                        part(c, 0)
                    for c in (2 * half, 2 * half + 1):
                        pe.wait_ge(pv_own, m * 4 + c + 1)
                        pe.sem_inc(tick["pe"], 1)
                        part(c, 1)

                def turn_out(m):
                    for c in range(2):
                        pe.wait_ge(on_rdy, m * 4 + 3 + c)
                        for k in range(4):
                            last = pe.transpose(misc[(c + 1) % 2][:, P * k:P * k + P],
                                                on[:, 8 * c + 2 * k:8 * c + 2 * k + 2, :].rearrange("p a d -> p (a d)"),
                                                ident[:])
                        last.then_inc(oT_done, 1)

                def output(m):
                    pe.wait_ge(oT_rdy, m * 2 + 2)
                    for k in range(HP):
                        last = pe.matmul(misc[1][:, 0:D], oT[:, k, :], w[:, C_WO + D * k:C_WO + D * k + D],
                                         start=(k == 0), stop=(k == HP - 1))
                    last.then_inc(y_done, 1)

                def turn_qk(n):
                    for c in range(4):
                        pe.wait_ge(qk_rdy, n * 4 + c + 1 + 4)
                        if c >= 2:
                            pe.wait_ge(qkT_rdy, n * 4 + c - 1 + 1)
                        for k in range(4):
                            last = pe.transpose(tp[c % 2][:, P * k:P * k + P], qk[:, c, P * k:P * k + P], ident[:])
                        last.then_inc(qkT_done, 1)

                def start():
                    for t in range(2):
                        turn_in(n0 + t, t)
                        project(n0 + t, t, n0, range(4))
                    for j in range(2):
                        project_v(n0, 0, 1, j)
                    turn_qk(n0)

                def tile(t, m, p, last, next1, next2):
                    if next2:
                        turn_in(m + 2, p)
                    scores_masked(t, m)
                    scores(p, (0, 1))
                    if next2:
                        project(m + 2, p, m + 1, (0,))
                    scores(p, (2, 3))
                    if last:
                        turn_out(m - 1)
                    if next2:
                        project(m + 2, p, m + 1, (1,))
                    if last:
                        output(m - 1)
                    if next1:
                        turn_qk(m + 1)
                    if next2:
                        project(m + 2, p, m + 1, (2, 3))
                    turn_probs(m, next1)
                    for half in range(2):
                        values(m, p, half)
                        if next1:
                            project_v(m + 1, 1 - p, 1 if next2 else 0, half)

                def finish():
                    turn_out(n0 + NT - 1)
                    output(n0 + NT - 1)

                pe.wait_ge(w_ld[par], lp * 48 + 48)
                if par == 0:
                    pe.wait_ge(const_ld, 48)
                    pe.wait_ge(init, 1)
                by_tile(start, tile, finish, pe, n0)

            def geglu(lp, par, k0):
                w = wts[par]

                def turn_in(g):
                    k = k0 + g
                    pe.wait_ge(g_hgrp, k + 1)
                    for i in range(GT):
                        last = pe.transpose(bank[g % 2][:, P * i:P * i + P], hgrp[g % 2][:, i, :], ident[:])
                    last.then_inc(g_xT, 1)

                def turn_back(g):
                    pe.wait_ge(g_xs, (k0 + g) * 3 + 4)
                    for i in range(GT):
                        last = pe.transpose(tp[g % 2][:, P * i:P * i + P], xs4[g % 2][:, P * i:P * i + P], ident[:])
                    last.then_inc(g_back, 1)

                def turn_norm(g):
                    pe.wait_ge(g_xn, (k0 + g) * GT + GT)
                    for i in range(GT):
                        last = pe.transpose(bank[g % 2][:, P * i:P * i + P], xn[:, i, :], ident[:])
                    last.then_inc(g_xnT, 1)

                def widen(g):
                    k = k0 + g
                    pe.wait_ge(g_xnT_rdy, k + 1)
                    for half in range(2):
                        for i, (c0, cn) in enumerate(FB):
                            if half == 0:
                                pe.wait_ge(g_u, k * 3 + i + 1)
                            else:
                                pe.wait_ge(g_gl, k * 3 + i + 1)
                            c = C_W1 + (DFF if half == 0 else 0) + c0
                            pe.matmul(wide[i][0:cn, :], w[:, c:c + cn], xnT[:], start=True, stop=True).then_inc(g_w1, 1)

                def narrow(g):
                    k = k0 + g
                    pe.wait_ge(g_h, k + 1)
                    pe.wait_ge(g_u, k * 3 + 6)
                    for i in range(GT):
                        y = y_ps[:, D * i:D * i + D]
                        pe.matmul(y, ones_row[:], b2row[par][:], start=True, stop=False, skip_group_check=True)
                        for f, (c0, cn) in enumerate(FB):
                            last = pe.matmul(y, u[0:cn, f, P * i:P * i + P], w[0:cn, C_W2 + D * f:C_W2 + D * f + D],
                                             start=False, stop=(f == len(FB) - 1), skip_group_check=True)
                    last.then_inc(g_y, 1)

                for g in range(2):
                    turn_in(g)
                    turn_back(g)
                turn_norm(0)
                for g in range(NG):
                    widen(g)
                    if g + 2 < NG:
                        turn_in(g + 2)
                        turn_back(g + 2)
                    if g + 1 < NG:
                        turn_norm(g + 1)
                    narrow(g)

            by_layer(pe, attention, geglu)

        @block.scalar
        def _(act):
            def attention(lp, par, n0):
                def shift(t, n, p):
                    act.wait_ge(xT_done, n + 1 + 2)
                    act.wait_ge(xs_rdy, n + 1)
                    act.sem_inc(tick["act"], 1)
                    act.activation(xs[p][DH:P, 0:1], xs[1 - p][DH:P, P:P + 1], ACT.Copy,
                                   scale=carried[DH:P, bass.ds(t, 1)]).then_inc(carry_rdy, 1)
                    act.activation(xs[p][0:DH, 0:P], tp[1][0:DH, 0:P], ACT.Copy)
                    act.activation(xs[p][DH:P, 1:1 + P], tp[1][DH:P, 0:P], ACT.Copy).then_inc(xs_rdy, 1)

                def square(n, j):
                    act.wait_ge(proj_done, n * 4 + j + 1)
                    act.wait_ge(ss_rdy, n * 4 + j + 1)
                    act.activation(sq[:, j % 2, :], bank[j % 2][:], ACT.Square).then_inc(sq_rdy, 1)

                def values_before(m, p):
                    act.wait_ge(pv_done, m * 4 + 5)
                    act.sem_inc(tick["act"], 1)
                    act.activation(vprev[PADK:P], v[p][PADK:P], ACT.Copy).then_inc(vprev_rdy, 1)

                def keep_v(n, p):
                    for j in range(2):
                        act.wait_ge(vproj_done, n * 2 + j + 1)
                        act.wait_ge(vprev_rdy, n + 1)
                        act.activation(v[p][:, 8 * j:8 * j + 8, 0:DH], bank[j][:].rearrange("p (a d) -> p a d", d=DH),
                                       ACT.Copy).then_inc(v_rdy, 1)

                def exps(m):
                    act.wait_ge(sd_rdy, m + 1)
                    act.activation(pw[:, 0:HEADS], sd[:], ACT.Exp)
                    act.activation(pw[:, HEADS], sd[:, 0], ACT.Exp).then_inc(p_rdy, 1)

                def keep_pT(m):
                    act.wait_ge(pv_done, m * 4 + 1)
                    for c in range(4):
                        act.wait_ge(pT_done, m * 4 + 1 + c)
                        act.activation(pT[:, c % 2, 4 * (c // 2):4 * (c // 2) + 4, :],
                                       tp[c % 2][:].rearrange("p (a q) -> p a q", q=P), ACT.Copy).then_inc(pT_rdy, 1)

                def keep_oT(m):
                    for c in range(2):
                        act.wait_ge(oT_done, m * 2 + c + 1)
                        act.activation(oT[:, 4 * c:4 * c + 4, :], misc[(c + 1) % 2][:].rearrange("p (a q) -> p a q", q=P),
                                       ACT.Copy).then_inc(oT_rdy, 1)

                def keep_qkT(n, p):
                    for c in range(4):
                        act.wait_ge(qkT_done, n * 4 + c + 1)
                        src = tp[c % 2][:].rearrange("p (a q) -> p a q", q=P)
                        dst = qT[p][:, 4 * c:4 * c + 4, :] if c < 2 else kT[p][:, 4 * (c - 2):4 * (c - 2) + 4, WIN:WIN + P]
                        act.activation(dst, src, ACT.Copy).then_inc(qkT_rdy, 1)

                def start():
                    for t in range(2):
                        shift(t, n0 + t, t)
                        for j in range(4):
                            square(n0 + t, j)
                    keep_v(n0, 0)
                    keep_qkT(n0, 0)

                def tile(t, m, p, last, next1, next2):
                    if next2:
                        shift(t + 2, m + 2, p)
                    if last:
                        values_before(m - 1, 1 - p)
                    if next2:
                        square(m + 2, 0)
                    if last:
                        keep_oT(m - 1)
                    if next2:
                        square(m + 2, 1)
                    exps(m)
                    if next1:
                        keep_qkT(m + 1, 1 - p)
                    if next2:
                        square(m + 2, 2)
                        square(m + 2, 3)
                    keep_pT(m)
                    if next1:
                        keep_v(m + 1, 1 - p)

                def finish():
                    values_before(n0 + NT - 1, 1)
                    keep_oT(n0 + NT - 1)

                if par == 0:
                    act.wait_ge(const_ld, 48)
                    act.wait_ge(init, 1)
                by_tile(start, tile, finish, act, n0)

            def geglu(lp, par, k0):
                w = wts[par]

                def shift(g):
                    k = k0 + g
                    x, turned = xs4[g % 2], bank[g % 2]
                    act.wait_ge(g_xT, k + 3)
                    act.wait_ge(g_xs, k * 3 + 1)
                    act.sem_inc(tick["act"], 1)
                    act.activation(x[0:DH, 0:GT * P], turned[0:DH, :], ACT.Copy).then_inc(g_xs, 1)
                    act.activation(x[DH:P, 1:1 + GT * P], turned[DH:P, :], ACT.Copy).then_inc(g_xs, 1)
                    if g % 2 == 0:
                        act.sem_inc(g_xs, 1)
                    else:
                        act.activation(x[DH:P, 0:1], xs4[0][DH:P, GT * P:GT * P + 1], ACT.Copy).then_inc(g_xs, 1)

                def keep_norm(g):
                    act.wait_ge(g_xnT, k0 + g + 2)
                    act.sem_inc(tick["act"], 1)
                    act.activation(xnT[:], bank[g % 2][:], ACT.Identity, scale=w[:, C_LN:C_LN + 1],
                                   bias=w[:, C_LN + 1:C_LN + 2]).then_inc(g_xnT_rdy, 1)

                def gates(g):
                    k = k0 + g
                    for i, (c0, cn) in enumerate(FB):
                        act.wait_ge(g_u, k * 3 + i + 1)
                        act.wait_ge(g_w1, k * 6 + i + 1)
                        act.sem_inc(tick["act"], 1)
                        act.activation(gl[0:cn, i, :], wide[i][0:cn, :], ACT.Gelu,
                                       bias=w[0:cn, C_B1 + i:C_B1 + i + 1]).then_inc(g_gl, 1)

                act.wait_ge(w_ld[par], lp * 48 + 48)
                act.sem_inc(tick["act"], 1)
                for g in range(2):
                    shift(g)
                keep_norm(0)
                for g in range(NG):
                    gates(g)
                    if g + 2 < NG:
                        shift(g + 2)
                    if g + 1 < NG:
                        keep_norm(g + 1)

            by_layer(act, attention, geglu)

        @block.vector
        def _(dve):
            def attention(lp, par, n0):
                def rope(t, n, j):
                    src = bank[j % 2][:]
                    tb = 2 * (j // 2)
                    dve.wait_ge(qk_rdy, n * 4 + j + 1)
                    dve.wait_ge(sq_rdy, n * 4 + j + 1 + 2)
                    dve.tensor_reduce(ss[:, 8 * j:8 * j + 8], sq[:, j % 2, :].rearrange("p (a d) -> p a d", d=DH),
                                      AX, ALU.add).then_inc(ss_rdy, 1)
                    dve.tensor_tensor(rot_a[:, j, :].rearrange("p (a d) -> p a d", d=DH),
                                      src.rearrange("p (a d) -> p a d", d=DH),
                                      tab[:, tb, bass.ds(t, 1), :].to_broadcast([P, 8, DH]), ALU.mult)
                    swapped = src.rearrange("p (a e d) -> p a e d", a=8, e=2)[:, :, ::-1, :]
                    sins = tab[:, tb + 1, bass.ds(t, 1), :].rearrange("p a (e d) -> p a e d", e=2)
                    dve.tensor_tensor(rot_b[:, j, :].rearrange("p (a e d) -> p a e d", a=8, e=2), swapped,
                                      sins.to_broadcast([P, 8, 2, DH // 2]), ALU.mult).then_inc(rope_rdy, 1)

                def soft_shift(m):
                    dve.wait_ge(s_done, m + 1 + 2)
                    dve.tensor_reduce(mx[:], score[:], AX, ALU.max).then_inc(mx_rdy, 1)
                    dve.wait_ge(mx_rdy, m + 1)
                    dve.tensor_tensor(sd[:], score[:], mx[:].rearrange("p (a o) -> p a o", o=1).to_broadcast([P, HEADS, 2 * WIN]),
                                      ALU.subtract).then_inc(sd_rdy, 1)

                def normalise(m):
                    for c in range(4):
                        o = misc[(c + 1) % 2][:, 0:260].rearrange("p (a d) -> p a d", d=DH + 1)
                        dve.wait_ge(pv_done, m * 4 + c + 2)
                        dve.reciprocal(rsum[:, 4 * c:4 * c + 4], o[:, :, DH]).then_inc(rs_rdy, 1)
                        dve.wait_ge(rs_rdy, m * 4 + c + 1)
                        dve.tensor_tensor(on[:].rearrange("p (a e) d -> p a e d", e=2)[:, 4 * (c % 2):4 * (c % 2) + 4, c // 2, :],
                                          o[:, :, 0:DH],
                                          rsum[:, 4 * c:4 * c + 4].rearrange("p (a o) -> p a o", o=1).to_broadcast([P, 4, DH]),
                                          ALU.mult).then_inc(on_rdy, 1)

                def add_back(t, m):
                    dve.wait_ge(y_done, m + 1)
                    dve.tensor_tensor(h[:, bass.ds(t, 1), :].rearrange("p a d -> p (a d)"), misc[1][:, 0:D],
                                      h[:, bass.ds(t, 1), :].rearrange("p a d -> p (a d)"), ALU.add).then_inc(h_rdy, 1)

                def start():
                    for t in range(2):
                        for j in range(4):
                            rope(t, n0 + t, j)

                def tile(t, m, p, last, next1, next2):
                    if next2:
                        rope(t + 2, m + 2, 0)
                    soft_shift(m)
                    if next2:
                        rope(t + 2, m + 2, 1)
                    if last:
                        add_back(t - 1, m - 1)
                    if next2:
                        rope(t + 2, m + 2, 2)
                        rope(t + 2, m + 2, 3)
                    normalise(m)

                def finish():
                    add_back(NT - 1, n0 + NT - 1)

                dve.wait_ge(tab_rdy, lp * 8 + par * 4 + 4)
                dve.sem_inc(tick["dve"], 1)
                by_tile(start, tile, finish, dve, n0)

            def geglu(lp, par, k0):
                w = wts[par]

                def rows(g):
                    return h[:, GT * g:GT * g + GT, :].rearrange("p a d -> p (a d)")

                def copy_in(g):
                    dve.wait_ge(g_xT, k0 + g + 1)
                    dve.sem_inc(tick["dve"], 1)
                    dve.tensor_copy(hgrp[g % 2][:].rearrange("p a d -> p (a d)"), rows(g)).then_inc(g_hgrp, 1)

                def moments(g):
                    k = k0 + g
                    dve.wait_ge(g_back, k + 1)
                    dve.sem_inc(tick["dve"], 1)
                    for i in range(GT):
                        dve.bn_stats(st[g % 2][:, i, :], tp[g % 2][:, P * i:P * i + P]).then_inc(g_st, 1)
                    dve.wait_ge(g_st, k * GT + GT)
                    dve.sem_inc(tick["dve"], 1)
                    for i in range(GT):
                        dve.bn_aggr(mv[g % 2][:, i, :], st[g % 2][:, i, :]).then_inc(g_mv, 1)

                def norm(g):
                    k = k0 + g
                    dve.wait_ge(g_rstd, k * RSQRT_STEPS + RSQRT_STEPS)
                    dve.wait_ge(g_xnT, k + 1)
                    dve.sem_inc(tick["dve"], 1)
                    for i in range(GT):
                        dve.tensor_scalar(xn[:, i, :], tp[g % 2][:, P * i:P * i + P], mv[g % 2][:, i, 0:1], rstd[g % 2][:, i:i + 1],
                                          ALU.subtract, ALU.mult).then_inc(g_xn, 1)

                def product(g):
                    k = k0 + g
                    dve.wait_ge(g_y, k + 1)
                    for i, (c0, cn) in enumerate(FB):
                        dve.wait_ge(g_w1, k * 6 + 3 + i + 1)
                        dve.sem_inc(tick["dve"], 1)
                        dve.scalar_tensor_tensor(u[0:cn, i, :], wide[i][0:cn, :], w[0:cn, C_B1 + 3 + i:C_B1 + 4 + i],
                                                 gl[0:cn, i, :], ALU.add, ALU.mult).then_inc(g_u, 1)

                def add_back(g):
                    dve.wait_ge(g_y, k0 + g + 2)
                    dve.tensor_tensor(rows(g), y_ps, rows(g), ALU.add).then_inc(g_h, 1)

                dve.wait_ge(w_ld[par], lp * 48 + 48)
                dve.wait_ge(h_rdy, lp * 32 + par * 16 + 18)
                dve.sem_inc(tick["dve"], 1)
                copy_in(0)
                copy_in(1)
                moments(0)
                norm(0)
                moments(1)
                for g in range(NG):
                    if g + 2 < NG:
                        copy_in(g + 2)
                    product(g)
                    if g + 1 < NG:
                        norm(g + 1)
                    if g + 2 < NG:
                        moments(g + 2)
                    add_back(g)
                dve.wait_ge(g_h, k0 + NG + 1)
                dve.sem_inc(layer_done, 1)

            dve.memset(xs[1][:], 0.0)
            dve.memset(xs4[0][:], 0.0)
            dve.memset(ones_row[:], 1.0)
            for p in range(2):
                dve.memset(kT[p][:], 0.0)
                dve.memset(v[p][:], 1.0)
            dve.memset(vprev[:], 1.0).then_inc(xs_rdy, 1)
            dve.wait_ge(xs_rdy, 1)
            dve.sem_inc(init, 1)
            dve.sem_inc(layer_done, 2)
            dve.sem_inc(rope_rdy, 2)
            dve.sem_inc(sq_rdy, 2)
            dve.sem_inc(xT_done, 2)
            dve.sem_inc(qkT_rdy, 1)
            dve.sem_inc(s_done, 2)
            dve.sem_inc(g_xT, 2)
            dve.sem_inc(g_y, 1)
            dve.sem_inc(g_xnT, 1)
            dve.sem_inc(ss_rdy, 2)
            dve.sem_inc(v_rdy, 2)
            dve.sem_inc(h_rdy, 2)
            dve.sem_inc(g_u, 3)
            dve.sem_inc(g_xs, 1)
            dve.sem_inc(g_h, 1)
            by_layer(dve, attention, geglu)

        @block.gpsimd
        def _(pool):
            def attention(lp, par, n0):
                def copy_in(t, n, p):
                    pool.wait_ge(xT_done, n - 2 + 1 + 2)
                    pool.sem_inc(tick["pool"], 1)
                    pool.tensor_copy(hcur[p][:], h[:, bass.ds(t, 1), :].rearrange("p a d -> p (a d)")).then_inc(hcur_rdy, 1)

                def rope(n):
                    for j in range(4):
                        pool.wait_ge(rope_rdy, n * 4 + j + 1 + 2)
                        pool.tensor_tensor(rot_a[:, j, :], rot_a[:, j, :], rot_b[:, j, :], ALU.add).then_inc(rot_sum, 1)
                    pool.wait_ge(ss_rdy, n * 4 + 6)
                    pool.sem_inc(tick["pool"], 1)
                    rsqrt(pool, rn[:], ss[:], rn_tmp[:], 1e-24, 0.0, rn_rdy, n * RSQRT_STEPS, tick["pool"])
                    pool.wait_ge(qkT_rdy, n * 4 + 1)
                    pool.wait_ge(rn_rdy, n * RSQRT_STEPS + RSQRT_STEPS)
                    for j in range(4):
                        pool.wait_ge(rot_sum, n * 4 + j + 1)
                        pool.tensor_tensor(qk[:, j, :].rearrange("p (a d) -> p a d", d=DH),
                                           rot_a[:, j, :].rearrange("p (a d) -> p a d", d=DH),
                                           rn[:, 8 * j:8 * j + 8].rearrange("p (a o) -> p a o", o=1).to_broadcast([P, 8, DH]),
                                           ALU.mult).then_inc(qk_rdy, 1)

                def keys_before(t, n, p):
                    pool.wait_ge(qkT_rdy, n * 4 + 1)
                    pool.wait_ge(s_done, n - 2 + 1 + 2)
                    pool.tensor_tensor(kT[p][:, :, 0:WIN], kT[1 - p][:, :, P:P + WIN],
                                       carried[:, bass.ds(t, 1)].rearrange("p (a o) -> p a o", o=1).to_broadcast([P, HP, WIN]),
                                       ALU.mult).then_inc(kprev_rdy, 1)

                def start():
                    copy_in(0, n0, 0)
                    copy_in(1, n0 + 1, 1)
                    rope(n0)
                    keys_before(0, n0, 0)
                    rope(n0 + 1)
                    copy_in(2, n0 + 2, 0)

                def tile(t, m, p, last, next1, next2):
                    if next2 and not (isinstance(t, int) and t == NT - 3):
                        copy_in(t + 3, m + 3, 1 - p)
                    if next1:
                        keys_before(t + 1, m + 1, 1 - p)
                    if next2:
                        rope(m + 2)

                pool.wait_ge(w_ld[par], lp * 48 + 48)
                pool.wait_ge(const_ld, 48)
                pool.wait_ge(rope_rdy, n0 * 4 + 2)
                pool.sem_inc(tick["pool"], 1)
                for a in range(4):
                    for b in range(BATCH):
                        last = pool.tensor_tensor(tab[:, a, TB * b:TB * b + TB, :], raw_tab[:, a, :, :],
                                                  scales[par][:, a:a + 1, :].to_broadcast([P, TB, DH]), ALU.mult)
                    last.then_inc(tab_rdy, 1)
                pool.wait_ge(g_h, k_of(lp, par) + 1)
                pool.sem_inc(tick["pool"], 1)
                by_tile(start, tile, lambda: None, pool, n0)

            def k_of(lp, par):
                return lp * 8 + par * 4

            def geglu(lp, par, k0):
                for g in range(NG):
                    k = k0 + g
                    pool.wait_ge(g_mv, k * GT + GT)
                    pool.sem_inc(tick["pool"], 1)
                    rsqrt(pool, rstd[g % 2][:], mv[g % 2][:, :, 1], rstd_tmp[g % 2][:], 0.0, 1e-5, g_rstd, k * RSQRT_STEPS, tick["pool"])

            pool.wait_ge(init, 1)
            pool.sem_inc(qk_rdy, 4)
            pool.sem_inc(pv_done, 1)
            pool.sem_inc(vprev_rdy, 2)
            by_layer(pool, attention, geglu)


def local_layer_constants():
    half = np.arange(0, DH, 2, dtype=np.float32)
    inv_freq = (np.float32(1.0) / np.float32(10000.0) ** (half / np.float32(DH))).astype(np.float32)
    pos = np.arange(SEQ, dtype=np.float32)
    freqs = np.concatenate([pos[:, None] * inv_freq[None, :]] * 2, -1)
    base = (half + np.float32(0.4 * DH)) / np.float32(1.4 * DH)
    power = (pos - SEQ // 2) / np.float32(WIN // 2)
    scale = np.concatenate([base[None, :] ** power[:, None]] * 2, -1).astype(np.float32)
    cos, sin = np.cos(freqs), np.sin(freqs)
    sign = np.where(np.arange(DH) < DH // 2, -1, 1).astype(np.float32)
    tabs = np.stack([cos * scale * 8.0, sin * sign * scale * 8.0, cos / scale, sin * sign / scale])
    tables = tabs.reshape(4, TB, P, DH).transpose(2, 0, 1, 3).astype(np.float32)
    i, j = np.arange(P)[:, None, None] % WIN, np.arange(2 * WIN)[None, None, :]
    j = np.where(np.arange(P)[:, None, None] // WIN % 2 == 0, (j + WIN) % (2 * WIN), j)
    out = (j < i) | (j > i + WIN)
    first = (np.arange(NT)[None, :, None] % TB == 0) & (np.arange(P)[:, None, None] < WIN) & (j < WIN)
    mask = np.where(out | first, np.float32(NEG), np.float32(0))
    carried = np.broadcast_to((np.arange(NT) % TB != 0).astype(np.float32), (P, NT))
    return np.ascontiguousarray(tables), mask, np.ascontiguousarray(carried)


def pack_local_weights(Wqkv, q_scale, k_scale, Wo, ln_g, ln_b, W1, b1, W2, b2):
    wts = np.zeros((DEPTH, P, NWC), np.float32)
    wts[:, :, C_QKV:C_WO] = Wqkv
    wts[:, :, C_WO:C_W1] = Wo.reshape(DEPTH, HP, P, D).transpose(0, 2, 1, 3).reshape(DEPTH, P, HP * D)
    wts[:, :, C_W1:C_W2] = W1
    for f, (c0, cn) in enumerate(FB):
        wts[:, 0:cn, C_W2 + D * f:C_W2 + D * f + D] = W2[:, c0:c0 + cn]
        wts[:, 0:cn, C_B1 + f] = b1[:, DFF + c0:DFF + c0 + cn]
        wts[:, 0:cn, C_B1 + 3 + f] = b1[:, c0:c0 + cn]
    wts[:, :, C_LN], wts[:, :, C_LN + 1] = ln_g, ln_b
    swap = lambda s: np.concatenate([s[:, DH // 2:], s[:, :DH // 2]], 1)
    scales = np.concatenate([q_scale, swap(q_scale), k_scale, swap(k_scale)], 1)
    return wts, np.ascontiguousarray(scales), np.ascontiguousarray(b2)

AH, AD = 16, D // 16
SPAN = 3 * P
APR = AH // 2
VW = 32
QUADS = AH * VW // P


def windowed_attention(nc, x, xnT, ident, identb, dram):
    with ExitStack() as ctx:
        sb, ps, sem = buffers(nc, ctx)
        w = sb("a_w", [P, 3, D])
        wo = sb("a_wo", [P, QUADS, D])
        bias = sb("a_bias", [P, 2])
        bias_q = sb("a_bias_q", [P, 1])
        row_b = sb("a_row_b", [1, 2, D])
        ones_row = sb("a_ones_row", [1, P])
        heads = sb("a_heads", [P, AH])
        spread = sb("a_spread", [P, P])
        maskb = sb("a_mask", [P, NT, 2, P], BF16)
        qT = sb("a_qT", [P, NT * P])
        kT = sb("a_kT", [P, P + NT * P + P])
        v = sb("a_v", [P, NT + 2, AH, AD])
        vwin = [sb(f"a_vwin{i}", [P, 3, AH, VW]) for i in range(2)]
        qz = sb("a_qz", [P, AH, P])
        negmax = sb("a_negmax", [P, APR, 2])
        pr = [sb(f"a_pr{i}", [P, 2, SPAN]) for i in range(2)]
        pT = [sb(f"a_pT{i}", [P, 2, SPAN]) for i in range(2)]
        oT = sb("a_oT", [P, QUADS * P])
        inv = sb("a_inv", [P, QUADS * P])
        s_ps = [ps(f"a_s{i}", [P, 2, 512]) for i in range(2)]
        t_ps = ps("a_t", [P, 2, 512])
        o_ps = ps("a_o", [P, 512])
        y_ps = ps("a_y", [P, 512])

        (w_ld, init, bq_rdy, proj_done, proj_rdy, v_rdy, vwin_rdy, qz_rdy, s_done, mx_rdy, p_rdy, t_done, t_rdy, pv_done,
         oT_rdy, sum_done, inv_rdy, on_rdy, y_done, x_rdy) = (sem("a_" + s) for s in (
            "w_ld init bq_rdy proj_done proj_rdy v_rdy vwin_rdy qz_rdy s_done mx_rdy p_rdy t_done t_rdy pv_done "
            "oT_rdy sum_done inv_rdy on_rdy y_done x_rdy").split())
        tick = {e: sem(f"a_tick_{e}") for e in ("pe", "act", "dve", "pool")}
        NC = NT * P // 512
        ACT_TURNS = (1, 4, 7)
        loads = ((w, "a_w"), (wo, "a_wo"), (bias, "a_bias"), (row_b, "a_row_b"), (heads, "a_heads"), (spread, "a_spread"),
                 (maskb, "a_mask"))
        LOADED = 16 * len(loads)
        block = ctx.enter_context(nc.Block())

        def by_tile(eng, tile, last):
            tile(0, 0, True)
            with eng.Fori(0, NT // 2 - 1) as j:
                tile(j * 2 + 1, 1, False)
                tile(j * 2 + 2, 0, False)
            tile(NT - 1, 1, False)
            last(NT - 1)

        @block.sync
        def _(sp):
            for dst, name in loads:
                sp.dma_start(dst[:], dram[name]).then_inc(w_ld, 16)

        @block.tensor
        def _(pe):
            pe.wait_ge(w_ld, LOADED)
            pe.wait_ge(init, 1)
            for a in range(2):
                for c in range(NC):
                    n = NC * a + c
                    if n >= 2:
                        pe.wait_ge(proj_rdy, n - 1)
                    pe.matmul(s_ps[n % 2][:, 0, :], w[:, a, :], xnT[:, 512 * c:512 * c + 512], start=True, stop=True)\
                      .then_inc(proj_done, 1)
            for t in range(NT):
                if t >= 2:
                    pe.wait_ge(v_rdy, t - 1)
                else:
                    pe.wait_ge(proj_rdy, 2 * NC - 1 + t)
                pe.matmul(s_ps[t % 2][:, 0, 0:D], ones_row[:], row_b[:, 0, :], start=True, stop=False)
                pe.matmul(s_ps[t % 2][:, 0, 0:D], xnT[:, P * t:P * t + P], w[:, 2, :], start=False, stop=True)\
                  .then_inc(proj_done, 1)
            pe.wait_ge(v_rdy, NT)

            def scores(t, p):
                q = t * APR + p
                pe.wait_ge(p_rdy, q - 2 + 3)
                pe.wait_ge(qz_rdy, q * 2 + 2)
                for e in range(2):
                    pe.matmul(s_ps[p % 2][:, e, 0:SPAN], qz[:, 2 * p + e, :], kT[:, bass.ds(t * P, SPAN)], start=True,
                              stop=False, skip_group_check=True)
                for e in range(2):
                    s = s_ps[p % 2][:, e, 0:SPAN].rearrange("q (a k) -> q a k", a=3)[:, 0:3:2, :]
                    mm = pe.matmul(s, identb[:], maskb[:, bass.ds(t, 1), :, :].rearrange("q o a k -> q (o a) k"),
                                   start=False, stop=True, skip_group_check=True)
                mm.then_inc(s_done, 1)

            def turn(t, p):
                q = t * APR + p
                pe.wait_ge(t_rdy, q + 1)
                pe.wait_ge(p_rdy, q + 1 + 2)
                for e in range(2):
                    for a in range(3):
                        mm = pe.transpose(t_ps[:, e, P * a:P * a + P], pr[p % 2][:, e, P * a:P * a + P], ident[:])
                mm.then_inc(t_done, 1)

            def values(t, p, par):
                q = t * APR + p
                pe.wait_ge(t_rdy, q + 2)
                if p == 0:
                    pe.wait_ge(vwin_rdy, t + 1)
                    pe.wait_ge(oT_rdy, t + 1)
                pe.sem_inc(tick["pe"], 1)
                for a in range(3):
                    for e in range(2):
                        h = 2 * p + e
                        g, c = h % 4, h // 4
                        mm = pe.matmul(o_ps[VW * g:VW * g + VW, P * c:P * c + P], vwin[par][:, a, h, :],
                                       pT[p % 2][:, e, P * a:P * a + P], start=(a == 0), stop=(a == 2), skip_group_check=True)
                mm.then_inc(pv_done, 1)

            def spread_sums(t):
                pe.wait_ge(oT_rdy, t + 2)
                pe.wait_ge(x_rdy, t + 1)
                pe.matmul(y_ps[:], spread[:], oT[:], start=True, stop=True).then_inc(sum_done, 1)

            def project_out(t):
                pe.wait_ge(on_rdy, (t + 1) * QUADS)
                pe.matmul(y_ps[:, 0:D], ones_row[:], row_b[:, 1, :], start=True, stop=False)
                for c in range(QUADS):
                    mm = pe.matmul(y_ps[:, 0:D], oT[:, P * c:P * c + P], wo[:, c, :], start=False, stop=(c == QUADS - 1))
                mm.then_inc(y_done, 1)

            def tile(t, par, first):
                for p in range(APR + 2):
                    if p < APR:
                        scores(t, p)
                    if 1 <= p <= APR:
                        turn(t, p - 1)
                    if p >= 2:
                        values(t, p - 2, par)
                    if p == 1 and not first:
                        spread_sums(t - 1)
                    if p == 7 and not first:
                        project_out(t - 1)

            def last(t):
                spread_sums(t)
                project_out(t)

            by_tile(pe, tile, last)

        @block.scalar
        def _(act):
            act.wait_ge(bq_rdy, 1)
            for a in range(2):
                for c in range(NC):
                    n = NC * a + c
                    act.wait_ge(proj_done, n + 1)
                    dst = qT[:, 512 * c:512 * c + 512] if a == 0 else kT[:, P + 512 * c:P + 512 * c + 512]
                    act.activation(dst, s_ps[n % 2][:, 0, :], ACT.Identity, bias=bias_q[:] if a == 0 else bias[:, 1:2],
                                   scale=float(AD) ** -0.5 if a == 0 else 1.0).then_inc(proj_rdy, 1)
            for t in range(NT):
                act.wait_ge(proj_done, 2 * NC + t + 1)
                act.activation(v[:, t + 1, :, :], s_ps[t % 2][:, 0, 0:D].rearrange("k (h d) -> k h d", h=AH), ACT.Copy)\
                   .then_inc(v_rdy, 1)
            act.wait_ge(v_rdy, NT)

            def window(t, par):
                act.wait_ge(pv_done, (t - 1) * APR + 2 * APR)
                act.sem_inc(tick["act"], 1)
                act.activation(vwin[par][:, :, :, 0:AD], v[:, bass.ds(t, 3), :, :], ACT.Copy).then_inc(vwin_rdy, 1)

            def weights(t, p):
                q = t * APR + p
                act.wait_ge(mx_rdy, q + 1)
                for e in range(2):
                    ins = act.activation(pr[p % 2][:, e, :], s_ps[p % 2][:, e, 0:SPAN], ACT.Exp, bias=negmax[:, p, e:e + 1])
                ins.then_inc(p_rdy, 1)

            def keep_turned(t, p):
                q = t * APR + p
                act.wait_ge(t_done, q + 1)
                act.activation(pT[p % 2][:], t_ps[:, :, 0:SPAN], ACT.Copy).then_inc(t_rdy, 1)

            def keep_out(t):
                act.wait_ge(pv_done, (t + 1) * APR + 2 * APR)
                act.activation(oT[:], o_ps[:], ACT.Copy).then_inc(oT_rdy, 1)

            def tile(t, par, first):
                window(t, par)
                for p in range(APR + 1):
                    if p < APR:
                        weights(t, p)
                    if p >= 1 and (p - 1) in ACT_TURNS:
                        keep_turned(t, p - 1)
                    if p == 0 and not first:
                        keep_out(t - 1)

            by_tile(act, tile, keep_out)

        @block.vector
        def _(dve):
            dve.memset(ones_row[:], 1.0)
            dve.memset(kT[:, 0:P], 0.0)
            dve.memset(kT[:, P + NT * P:], 0.0)
            dve.memset(v[:], 0.0)
            dve.memset(vwin[0][:], 1.0)
            dve.memset(vwin[1][:], 1.0).then_inc(init, 1)
            dve.sem_inc(p_rdy, 2)
            dve.sem_inc(pv_done, 2 * APR)
            for s in (t_rdy, oT_rdy, x_rdy):
                dve.sem_inc(s, 1)
            dve.wait_ge(w_ld, LOADED)
            dve.tensor_scalar(bias_q[:], bias[:, 0:1], float(AD) ** -0.5, None, ALU.mult).then_inc(bq_rdy, 1)

            def maxima(t, p):
                q = t * APR + p
                dve.wait_ge(s_done, q + 1)
                dve.tensor_reduce(negmax[:, p, :], s_ps[p % 2][:, :, 0:SPAN], AX, ALU.max, negate=True).then_inc(mx_rdy, 1)

            def keep_turned(t, p):
                q = t * APR + p
                dve.wait_ge(t_done, q + 1)
                dve.tensor_copy(pT[p % 2][:], t_ps[:, :, 0:SPAN]).then_inc(t_rdy, 1)

            def divide(t, c):
                quad = slice(P * c, P * c + P)
                dve.wait_ge(sum_done, t + 1)
                dve.reciprocal(inv[:, quad], y_ps[:, quad]).then_inc(inv_rdy, 1)
                dve.wait_ge(inv_rdy, t * QUADS + c + 1)
                dve.tensor_tensor(oT[:, quad], oT[:, quad], inv[:, quad], ALU.mult).then_inc(on_rdy, 1)

            def add(t):
                dve.wait_ge(y_done, t + 1)
                xt = x[:, bass.ds(t, 1), :].rearrange("q a d -> q (a d)")
                dve.tensor_tensor(xt, xt, y_ps[:, 0:D], ALU.add).then_inc(x_rdy, 1)

            def tile(t, par, first):
                for p in range(APR + 1):
                    if p < APR:
                        maxima(t, p)
                    if 2 <= p < 2 + QUADS and not first:
                        divide(t - 1, p - 2)
                    if p >= 1 and (p - 1) not in ACT_TURNS:
                        keep_turned(t, p - 1)
                    if p == APR and not first:
                        add(t - 1)

            def last(t):
                for c in range(QUADS):
                    divide(t, c)
                add(t)
                dve.wait_ge(x_rdy, NT + 1)

            by_tile(dve, tile, last)

        @block.gpsimd
        def _(pool):
            pool.wait_ge(w_ld, LOADED)
            pool.wait_ge(proj_rdy, 2 * NC)

            def tile(t, par, first):
                for h in range(AH):
                    if not first and h % 2 == 0:
                        pool.wait_ge(s_done, t * APR - APR + h // 2 + 1)
                        pool.sem_inc(tick["pool"], 1)
                    pool.tensor_tensor(qz[:, h, :], qT[:, bass.ds(t * P, P)], heads[:, h:h + 1].to_broadcast([P, P]),
                                       ALU.mult).then_inc(qz_rdy, 1)

            by_tile(pool, tile, lambda t: None)


def pack_attention_weights(Wq, Wk, Wv, Wo):
    wo = np.zeros((4, VW, QUADS, D), np.float32)
    wo[:, 0:AD] = Wo.reshape(QUADS, 4, AD, D).transpose(1, 2, 0, 3)
    return np.ascontiguousarray(np.stack([Wq, Wk, Wv], 1)), wo.reshape(P, QUADS, D)


def attention_constants():
    i, j = np.arange(P)[:, None], np.arange(P)[None, :]
    before, behind = j < i, j > i
    never = np.ones((P, P), bool)
    tiles = [np.stack([never if t % TB == 0 else before, never if t % TB == TB - 1 else behind], 1) for t in range(NT)]
    mask = np.where(np.stack(tiles, 1), np.float32(NEG), np.float32(0))
    heads = (np.arange(P)[:, None] // AD == np.arange(AH)[None, :]).astype(np.float32)
    spread = (i == j // VW * VW + AD).astype(np.float32)
    return mask, heads, spread


NCOL, NNEU = 16, 32
GATE_H = D // 2
CB = NCOL * NNEU // P


def column_mixture(nc, x, xn, xnT, ident, dram):
    with ExitStack() as ctx:
        sb, ps, sem = buffers(nc, ctx)
        w = sb("m_w", [P, CB * P])
        pw = sb("m_pw", [P, CB, D])
        gw1 = sb("m_gw1", [P, GATE_H])
        gw2 = sb("m_gw2", [GATE_H, NCOL])
        bcol = sb("m_bcol", [P, CB + 1])
        rows = sb("m_rows", [1, NCOL + D])
        lng = sb("m_lng", [P, 2, D])
        emb = sb("m_emb", [NCOL, D])
        spread = sb("m_spread", [NCOL, CB * P])
        order = sb("m_order", [P, NCOL])
        ones_row = sb("m_ones_row", [1, P])
        embT = sb("m_embT", [P, NCOL])
        esq = sb("m_esq", [NCOL, D])
        ess, ers, etm = (sb("m_" + n, [NCOL, 1]) for n in ("ess", "ers", "etm"))
        xsq = sb("m_xsq", [P, NT, D])
        xss, xrs, xtm = (sb("m_" + n, [P, NT]) for n in ("xss", "xrs", "xtm"))
        hT = sb("m_hT", [GATE_H, NT * P])
        cT = sb("m_cT", [P, CB, NT * P])
        sg, lg, ex, ca = (sb("m_" + n, [P, NT, NCOL]) for n in ("sg", "lg", "ex", "ca"))
        best, tot, top = (sb("m_" + n, [P, NT]) for n in ("best", "tot", "top"))
        wT = sb("m_wT", [NCOL, NT * P])
        y = xsq
        st = sb("m_st", [P, NT, 6])
        mv = sb("m_mv", [P, NT, 2])
        rstd, rtm = (sb("m_" + n, [P, NT]) for n in ("rstd", "rtm"))
        gp = [ps(f"m_gp{i}", [P, 512]) for i in range(4)]
        sim = ps("m_sim", [P, NT, NCOL])
        gat = ps("m_gat", [P, NT, NCOL])
        yp = [ps(f"m_yp{i}", [P, 512]) for i in range(2)]
        (w_ld, emb_step, ess_rdy, ers_step, embT_done, embT_rdy, xss_rdy, xrs_step, g_done, g_rdy, sim_done, gat_done, step, act_step,
         wT_done, wT_rdy, sp_done, comb_rdy, y_done, y_rdy, st_rdy, mv_rdy, rs_step, out_step, init, tick, ptick) = (sem("m_" + s) for s in (
            "w_ld emb_step ess_rdy ers_step embT_done embT_rdy xss_rdy xrs_step g_done g_rdy sim_done gat_done step act_step "
            "wT_done wT_rdy sp_done comb_rdy y_done y_rdy st_rdy mv_rdy rs_step out_step init tick ptick").split())
        NG = NT * P // 512
        NGELU = NG * (1 + CB)
        MIX_EX, MIX_STEPS = 7, 15
        loads = ((w[:], "m_w"), (pw[:], "m_pw"), (gw1[:], "m_gw1"), (gw2[:], "m_gw2"), (bcol[:], "m_bcol"), (rows[:], "m_rows"),
                 (emb[:], "m_emb"), (spread[:], "m_spread"))
        wide = ((lng[:].rearrange("p a d -> p (a d)"), "m_lng", 2 * D), (order[:], "m_order", NCOL))
        LOADED = 16 * (len(loads) + len(wide))
        block = ctx.enter_context(nc.Block())

        def over(small, n):
            return small.rearrange("p (t o) -> p t o", o=1).to_broadcast([P, NT, n])

        @block.sync
        def _(sp):
            for dst, name in loads:
                sp.dma_start(dst, dram[name]).then_inc(w_ld, 16)
            for dst, name, n in wide:
                sp.dma_start(dst, dram[name].broadcast_to([P, n])).then_inc(w_ld, 16)

        @block.tensor
        def _(pe):
            pe.wait_ge(w_ld, LOADED)
            pe.wait_ge(init, 1)
            for g in range(NG):
                for c in range(1 + CB):
                    n = g * (1 + CB) + c
                    if n >= 4:
                        pe.wait_ge(g_rdy, n - 3)
                    lhs, m = (gw1[:], GATE_H) if c == 0 else (w[:, P * (c - 1):P * c], P)
                    pe.matmul(gp[n % 4][0:m, :], lhs, xnT[:, 512 * g:512 * g + 512], start=True, stop=True).then_inc(g_done, 1)
            pe.wait_ge(ers_step, RSQRT_STEPS + 1)
            pe.transpose(yp[0][:, 0:NCOL], emb[:], ident[0:NCOL, 0:NCOL]).then_inc(embT_done, 1)
            pe.wait_ge(embT_rdy, 1)
            for t in range(NT):
                mm = pe.matmul(sim[:, t, :], xnT[:, P * t:P * t + P], embT[:], start=True, stop=True, skip_group_check=True)
            mm.then_inc(sim_done, 1)
            pe.wait_ge(g_rdy, NGELU)
            for t in range(NT):
                pe.matmul(gat[:, t, :], ones_row[:], rows[:, 0:NCOL], start=True, stop=False, skip_group_check=True)
                mm = pe.matmul(gat[:, t, :], hT[:, P * t:P * t + P], gw2[:], start=False, stop=True, skip_group_check=True)
            mm.then_inc(gat_done, 1)
            pe.wait_ge(step, MIX_STEPS)
            for g in range(NG):
                for k in range(4):
                    t = 4 * g + k
                    mm = pe.transpose(gp[g][0:NCOL, P * k:P * k + P], ca[:, t, :], ident[:])
                mm.then_inc(wT_done, 1)
            for g in range(NG):
                pe.wait_ge(wT_rdy, NG)
                for c in range(CB):
                    n = g * CB + c
                    if n >= 4:
                        pe.wait_ge(comb_rdy, n - 3)
                    pe.matmul(gp[n % 4][:], spread[:, P * c:P * c + P], wT[:, 512 * g:512 * g + 512], start=True, stop=True)\
                      .then_inc(sp_done, 1)
            for g in range(NG):
                pe.wait_ge(comb_rdy, CB * (g + 1))
                if g >= 2:
                    pe.wait_ge(y_rdy, g - 1)
                for k in range(4):
                    t = 4 * g + k
                    yt = yp[g % 2][:, D * k:D * k + D]
                    pe.matmul(yt, ones_row[:], rows[:, NCOL:], start=True, stop=False, skip_group_check=True)
                    for c in range(CB):
                        mm = pe.matmul(yt, cT[:, c, P * t:P * t + P], pw[:, c, :], start=False, stop=(c == CB - 1),
                                       skip_group_check=True)
                mm.then_inc(y_done, 1)

        @block.scalar
        def _(act):
            act.wait_ge(w_ld, LOADED)
            for g in range(NG):
                for c in range(1 + CB):
                    n = g * (1 + CB) + c
                    act.wait_ge(g_done, n + 1)
                    if c == 0:
                        ins = act.activation(hT[:, 512 * g:512 * g + 512], gp[n % 4][0:GATE_H, :], ACT.Gelu,
                                             bias=bcol[0:GATE_H, CB:CB + 1])
                    else:
                        ins = act.activation(cT[:, c - 1, 512 * g:512 * g + 512], gp[n % 4][:], ACT.Gelu, bias=bcol[:, c - 1:c])
                    ins.then_inc(g_rdy, 1)
            act.wait_ge(embT_done, 1)
            act.activation(embT[:], yp[0][:, 0:NCOL], ACT.Copy).then_inc(embT_rdy, 1)
            act.wait_ge(step, 2)
            act.activation(sg[:], sg[:], ACT.Exp, scale=-1.0).then_inc(act_step, 1)
            act.wait_ge(step, MIX_EX)
            act.activation(ex[:], ex[:], ACT.Exp).then_inc(act_step, 1)
            for g in range(NG):
                act.wait_ge(wT_done, g + 1)
                act.activation(wT[:, 512 * g:512 * g + 512], gp[g][0:NCOL, :], ACT.Copy).then_inc(wT_rdy, 1)

        @block.vector
        def _(dve):
            dve.memset(ones_row[:], 1.0).then_inc(init, 1)
            dve.tensor_tensor(xsq[:], xn[:], xn[:], ALU.mult).then_inc(xss_rdy, 1)
            dve.wait_ge(w_ld, LOADED)
            dve.tensor_tensor(esq[:], emb[:], emb[:], ALU.mult).then_inc(emb_step, 1)
            dve.wait_ge(emb_step, 1)
            dve.tensor_reduce(ess[:], esq[:], AX, ALU.add).then_inc(ess_rdy, 1)
            dve.wait_ge(xss_rdy, 1)
            dve.tensor_reduce(xss[:], xsq[:], AX, ALU.add).then_inc(xss_rdy, 1)
            dve.wait_ge(ers_step, RSQRT_STEPS)
            dve.tensor_scalar(emb[:], emb[:], ers[:], None, ALU.mult).then_inc(ers_step, 1)

            steps = 0

            def link(ins):
                nonlocal steps
                steps += 1
                ins.then_inc(step, 1)
                dve.wait_ge(step, steps)

            dve.wait_ge(sim_done, 1)
            dve.wait_ge(xrs_step, RSQRT_STEPS)
            link(dve.tensor_tensor(lg[:], sim[:], over(xrs[:], NCOL), ALU.mult))
            dve.wait_ge(gat_done, 1)
            link(dve.tensor_scalar(sg[:], gat[:], -EXP_MAX, None, ALU.max))
            dve.wait_ge(act_step, 1)
            link(dve.tensor_scalar(sg[:], sg[:], 1.0, None, ALU.add))
            link(dve.reciprocal(sg[:], sg[:]))
            link(dve.tensor_tensor(lg[:], lg[:], sg[:], ALU.add))
            link(dve.tensor_reduce(best[:], lg[:], AX, ALU.max))
            link(dve.tensor_tensor(ex[:], lg[:], over(best[:], NCOL), ALU.subtract))
            assert steps == MIX_EX
            link(dve.tensor_tensor(ca[:], lg[:], over(best[:], NCOL), ALU.is_equal))
            link(dve.tensor_tensor(ca[:], ca[:], order[:].rearrange("p (o c) -> p o c", o=1).to_broadcast([P, NT, NCOL]), ALU.mult))
            link(dve.tensor_reduce(top[:], ca[:], AX, ALU.max))
            link(dve.tensor_tensor(ca[:], ca[:], over(top[:], NCOL), ALU.is_equal))
            dve.wait_ge(act_step, 2)
            link(dve.tensor_reduce(tot[:], ex[:], AX, ALU.add))
            link(dve.reciprocal(tot[:], tot[:]))
            link(dve.tensor_tensor(ex[:], ex[:], over(tot[:], NCOL), ALU.mult))
            assert steps == MIX_STEPS - 1
            link(dve.tensor_tensor(ca[:], ca[:], ex[:], ALU.mult))
            for g in range(NG):
                for c in range(CB):
                    n = g * CB + c
                    dve.wait_ge(sp_done, n + 1)
                    part = cT[:, c, 512 * g:512 * g + 512]
                    dve.tensor_tensor(part, part, gp[n % 4][:], ALU.mult).then_inc(comb_rdy, 1)
            for g in range(NG):
                s = slice(4 * g, 4 * g + 4)
                dve.wait_ge(y_done, g + 1)
                dve.tensor_tensor(y[:, s, :], yp[g % 2][:].rearrange("p (t d) -> p t d", d=D), xn[:, s, :], ALU.add).then_inc(y_rdy, 1)
            for t in range(NT):
                dve.wait_ge(y_rdy, t // 4 + 1)
                dve.bn_stats(st[:, t, :], y[:, t, :]).then_inc(st_rdy, 1)
            dve.wait_ge(st_rdy, NT)
            for t in range(NT):
                dve.bn_aggr(mv[:, t, :], st[:, t, :]).then_inc(mv_rdy, 1)
            dve.wait_ge(mv_rdy, NT)
            dve.tensor_tensor(y[:], y[:], mv[:, :, 0:1].to_broadcast([P, NT, D]), ALU.subtract).then_inc(out_step, 1)
            dve.wait_ge(rs_step, RSQRT_STEPS)
            dve.wait_ge(out_step, 1)
            dve.tensor_tensor(y[:], y[:], over(rstd[:], D), ALU.mult).then_inc(out_step, 1)
            dve.wait_ge(out_step, 2)
            dve.tensor_tensor(y[:], y[:], lng[:, 0:1, :].to_broadcast([P, NT, D]), ALU.mult).then_inc(out_step, 1)
            dve.tensor_tensor(x[:], x[:], lng[:, 1:2, :].to_broadcast([P, NT, D]), ALU.add).then_inc(out_step, 1)
            dve.wait_ge(out_step, 4)
            dve.tensor_tensor(x[:], x[:], y[:], ALU.add).then_inc(out_step, 1)
            dve.wait_ge(out_step, 5)

        @block.gpsimd
        def _(pool):
            pool.wait_ge(ess_rdy, 1)
            rsqrt(pool, ers[:], ess[:], etm[:], 1e-24, 0.0, ers_step, 0, ptick)
            pool.wait_ge(ers_step, RSQRT_STEPS)
            pool.wait_ge(xss_rdy, 2)
            rsqrt(pool, xrs[:], xss[:], xtm[:], 1e-24, 0.0, xrs_step, 0, ptick)
            pool.wait_ge(xrs_step, RSQRT_STEPS)
            pool.wait_ge(mv_rdy, NT)
            rsqrt(pool, rstd[:], mv[:, :, 1], rtm[:], 0.0, 1e-5, rs_step, 0, ptick)


def pack_mixture_weights(W_cols, b_cols, gate_b1, gate_b2, proj_w, proj_b, ln_g, ln_b):
    w = np.ascontiguousarray(W_cols.transpose(1, 0, 2).reshape(D, NCOL * NNEU))
    pw = np.ascontiguousarray(proj_w.reshape(CB, P, D).transpose(1, 0, 2))
    bcol = np.zeros((P, CB + 1), np.float32)
    bcol[:, 0:CB] = b_cols.reshape(CB, P).T
    bcol[0:GATE_H, CB] = gate_b1
    return w, pw, bcol, np.concatenate([gate_b2, proj_b])[None], np.concatenate([ln_g, ln_b])[None]


def mixture_constants():
    spread = (np.arange(CB * P)[None, :] // NNEU == np.arange(NCOL)[:, None]).astype(np.float32)
    return spread, np.arange(NCOL, 0, -1, dtype=np.float32)[None]

def program(nc, dram):
    with ExitStack() as ctx:
        sb, ps, sem = buffers(nc, ctx)
        x = sb("x", [P, NT, D])
        xn = sb("xn", [P, NT, D])
        ident = sb("ident", [P, P])
        identb = sb("identb", [P, P], BF16)
        loaded, stored = sem("loaded"), sem("stored")
        with nc.Block() as block:
            @block.sync
            def _(sp):
                for dst, src in ((x[:], dram["x"].rearrange("(t p) d -> p t d", p=P)), (ident[:], dram["ident"]),
                                 (identb[:], dram["identb"])):
                    sp.dma_start(dst, src).then_inc(loaded, 16)
                sp.wait_ge(loaded, 48)
        gated_delta(nc, x, xn, ident, identb, dram)
        local_layers(nc, xn, ident, identb, dram)
        with ExitStack() as second:
            xnT = second.enter_context(nc.sbuf_tensor("xnT2", [P, NT * P], F32))
            normalise(nc, x, xn, lambda t, n: xnT[:, P * t:P * (t + n)], ident, "n1", add=xn)
            windowed_attention(nc, x, xnT, ident, identb, dram)
            column_mixture(nc, x, xn, xnT, ident, dram)
        with nc.Block() as block:
            @block.sync
            def _(sp):
                sp.dma_start(dram["out"].rearrange("(t p) d -> p t d", p=P), x[:]).then_inc(stored, 16)
                sp.wait_ge(stored, 16)


def kernel(L0_attn_hidden_states, L0_attn_q_w, L0_attn_k_w, L0_attn_v_w, L0_attn_a_w, L0_attn_b_w, L0_attn_g_w, L0_attn_o_w,
           L0_attn_conv_q_w, L0_attn_conv_k_w, L0_attn_conv_v_w, L0_attn_A_log, L0_attn_dt_bias, L0_attn_norm_weight,
           L0_ffn_Wqkv, L0_ffn_q_scale, L0_ffn_k_scale, L0_ffn_Wo, L0_ffn_ln_g, L0_ffn_ln_b, L0_ffn_W1, L0_ffn_b1, L0_ffn_W2,
           L0_ffn_b2, L1_attn_Wq, L1_attn_bq, L1_attn_Wk, L1_attn_bk, L1_attn_Wv, L1_attn_bv, L1_attn_Wo, L1_attn_bo,
           L1_ffn_col_emb, L1_ffn_gate_w1, L1_ffn_gate_b1, L1_ffn_gate_w2, L1_ffn_gate_b2, L1_ffn_W_cols, L1_ffn_b_cols,
           L1_ffn_proj_w, L1_ffn_proj_b, L1_ffn_ln_g, L1_ffn_ln_b):
    import concourse.bacc as bacc
    from concourse.bass_utils import run_bass_kernel_spmd
    import ml_dtypes
    A = np.ascontiguousarray
    bf16 = ml_dtypes.bfloat16
    w_qkv, w_abg, w_conv, wo = pack_delta_weights(*[A(a) for a in (
        L0_attn_q_w, L0_attn_k_w, L0_attn_v_w, L0_attn_a_w, L0_attn_b_w, L0_attn_g_w, L0_attn_o_w,
        L0_attn_conv_q_w, L0_attn_conv_k_w, L0_attn_conv_v_w)])
    tri, causal, blocks = delta_constants()
    l_wts, l_scales, l_b2 = pack_local_weights(*[A(a) for a in (
        L0_ffn_Wqkv, L0_ffn_q_scale, L0_ffn_k_scale, L0_ffn_Wo, L0_ffn_ln_g, L0_ffn_ln_b, L0_ffn_W1, L0_ffn_b1, L0_ffn_W2,
        L0_ffn_b2)])
    l_tables, l_mask, l_carried = local_layer_constants()
    a_mask, a_heads, a_spread = attention_constants()
    a_w, a_wo = pack_attention_weights(*[A(a) for a in (L1_attn_Wq, L1_attn_Wk, L1_attn_Wv, L1_attn_Wo)])
    m_w, m_pw, m_bcol, m_rows, m_lng = pack_mixture_weights(*[A(a) for a in (
        L1_ffn_W_cols, L1_ffn_b_cols, L1_ffn_gate_b1, L1_ffn_gate_b2, L1_ffn_proj_w, L1_ffn_proj_b, L1_ffn_ln_g, L1_ffn_ln_b)])
    m_spread, m_order = mixture_constants()
    arrays = {"x": A(L0_attn_hidden_states).reshape(-1, D), "ident": np.eye(P, dtype=np.float32), "identb": np.eye(P, dtype=bf16),
              "d_w_qkv": w_qkv, "d_w_abg": w_abg, "d_w_conv": w_conv, "d_wo": wo, "d_dt_bias": A(L0_attn_dt_bias)[None],
              "d_a_log": A(L0_attn_A_log)[None], "d_nw": A(L0_attn_norm_weight)[None], "d_tri": tri,
              "d_causal": causal.astype(bf16), "d_blocks": blocks.astype(bf16),
              "l_wts": l_wts, "l_scales": l_scales, "l_b2": l_b2, "l_tables": l_tables, "l_mask": A(l_mask).astype(bf16),
              "l_carried": l_carried,
              "a_w": a_w, "a_wo": a_wo, "a_bias": A(np.stack([A(L1_attn_bq), A(L1_attn_bk)], 1)),
              "a_row_b": A(np.stack([A(L1_attn_bv), A(L1_attn_bo)])[None]), "a_heads": a_heads, "a_spread": a_spread, "a_mask": a_mask.astype(bf16),
              "m_w": m_w, "m_pw": m_pw, "m_gw1": A(L1_ffn_gate_w1), "m_gw2": A(L1_ffn_gate_w2), "m_bcol": m_bcol,
              "m_rows": m_rows, "m_emb": A(L1_ffn_col_emb), "m_spread": m_spread, "m_lng": m_lng, "m_order": m_order}
    nc = bacc.Bacc("TRN2", target_bir_lowering=False, num_devices=1)
    dram = {k: nc.dram_tensor("in_" + k, a.shape, mybir.dt.from_np(a.dtype), kind="ExternalInput").ap() for k, a in arrays.items()}
    dram["out"] = nc.dram_tensor("result", (BATCH * SEQ, D), F32, kind="ExternalOutput").ap()
    program(nc, dram)
    r = run_bass_kernel_spmd(nc, [{"in_" + k: a for k, a in arrays.items()}], core_ids=[0])
    return r.results[0]["result"].reshape(BATCH, SEQ, D)
```

```python
from contextlib import ExitStack

import numpy as np

import concourse.bass as bass
from concourse import mybir

F32 = mybir.dt.float32
BF16 = mybir.dt.bfloat16
I32 = mybir.dt.int32
ALU = mybir.AluOpType
ACT = mybir.ActivationFunctionType
AX = mybir.AxisListType.X

P = 128
BATCH, SEQ, D = 2, 1024, 128
NT = BATCH * SEQ // P
TB = SEQ // P
NEG = -1e30
EXP_MAX = 87.0


def buffers(nc, ctx):
    taken = []

    def sb(name, shape, dt=F32):
        return ctx.enter_context(nc.sbuf_tensor(name, shape, dt))

    def ps(name, shape, dt=F32):
        return ctx.enter_context(nc.psum_tensor(name, shape, dt))

    def sem(name):
        taken.append(nc.alloc_semaphore(name))
        return taken[-1]

    def clear():
        if taken:
            nc.clear_and_free_semaphores(taken)
            nc.all_engine_barrier()

    ctx.callback(clear)
    return sb, ps, sem


RSQRT_STEPS = 15


def rsqrt(eng, y, x, tmp, low, shift, done, n, tick):
    def step(ins, k):
        ins.then_inc(done, 1)
        eng.wait_ge(done, n + k)
        eng.sem_inc(tick, 1)

    step(eng.tensor_scalar(x, x, shift, low, ALU.add, ALU.max), 1)
    step(eng.tensor_scalar(y.bitcast(I32), x.bitcast(I32), -0.5, float(0x5F3759DF), ALU.mult, ALU.add), 2)
    step(eng.tensor_scalar(x, x, -0.5, None, ALU.mult), 3)
    for i in range(3):
        step(eng.tensor_tensor(tmp, y, y, ALU.mult), 4 * i + 4)
        step(eng.tensor_tensor(tmp, tmp, x, ALU.mult), 4 * i + 5)
        step(eng.tensor_scalar(tmp, tmp, 1.5, None, ALU.add), 4 * i + 6)
        last = eng.tensor_tensor(y, tmp, y, ALU.mult)
        if i < 2:
            step(last, 4 * i + 7)
    last.then_inc(done, 1)

def normalise(nc, x, xn, xnT, ident, tag, add=None):
    GT = 4
    with ExitStack() as ctx:
        sb, ps, sem = buffers(nc, ctx)
        st = sb(tag + "_st", [P, NT, 6])
        mv = sb(tag + "_mv", [P, NT, 2])
        rstd = sb(tag + "_rstd", [P, NT])
        tmp = sb(tag + "_tmp", [P, NT])
        tp = [ps(f"{tag}_tp{i}", [P, GT, P]) for i in range(2)]
        sum_rdy, st_rdy, mv_rdy, rs_rdy, centred, xn_rdy, tp_done, xnT_rdy, tick = (sem(f"{tag}_{s}") for s in (
            "sum_rdy", "st_rdy", "mv_rdy", "rs_rdy", "centred", "xn_rdy", "tp_done", "xnT_rdy", "tick"))
        block = ctx.enter_context(nc.Block())

        @block.vector
        def _(dve):
            if add is not None:
                dve.tensor_tensor(x[:], x[:], add[:], ALU.add).then_inc(sum_rdy, 1)
                dve.wait_ge(sum_rdy, 1)
            for t in range(NT):
                dve.bn_stats(st[:, t, :], x[:, t, :]).then_inc(st_rdy, 1)
            dve.wait_ge(st_rdy, NT)
            for t in range(NT):
                dve.bn_aggr(mv[:, t, :], st[:, t, :]).then_inc(mv_rdy, 1)
            dve.wait_ge(mv_rdy, NT)
            for g in range(NT // GT):
                s = slice(GT * g, GT * g + GT)
                dve.tensor_tensor(xn[:, s, :], x[:, s, :], mv[:, s, 0:1].to_broadcast([P, GT, D]), ALU.subtract).then_inc(centred, 1)
            dve.wait_ge(rs_rdy, RSQRT_STEPS)
            for g in range(NT // GT):
                s = slice(GT * g, GT * g + GT)
                dve.wait_ge(centred, g + 1)
                dve.tensor_tensor(xn[:, s, :], xn[:, s, :],
                                  rstd[:, s].rearrange("p (t o) -> p t o", o=1).to_broadcast([P, GT, D]), ALU.mult).then_inc(xn_rdy, 1)

        @block.gpsimd
        def _(pool):
            pool.wait_ge(mv_rdy, NT)
            rsqrt(pool, rstd[:], mv[:, :, 1], tmp[:], 0.0, 1e-5, rs_rdy, 0, tick)

        @block.tensor
        def _(pe):
            for g in range(NT // GT):
                pe.wait_ge(xn_rdy, g + 1)
                if g >= 2:
                    pe.wait_ge(xnT_rdy, g - 1)
                for k in range(GT):
                    mm = pe.transpose(tp[g % 2][:, k, :], xn[:, GT * g + k, :], ident[:])
                mm.then_inc(tp_done, 1)

        @block.scalar
        def _(act):
            for g in range(NT // GT):
                act.wait_ge(tp_done, g + 1)
                act.activation(xnT(GT * g, GT), tp[g % 2][:].rearrange("p t q -> p (t q)"), ACT.Copy).then_inc(xnT_rdy, 1)
            act.wait_ge(xnT_rdy, NT // GT)


def gated_delta(nc, x, xn, ident, identb, dram):
    with ExitStack() as ctx:
        sb, ps, sem = buffers(nc, ctx)
        qT = sb("qT", [P, GH, BATCH * SEQ])
        kT = sb("kT", [P, GH, BATCH * SEQ])
        vT = sb("vT", [P, len(VB), BATCH * SEQ])
        gate = sb("gate", [P, NT, VD])
        beta = sb("beta", [P, NT, GH])
        logdecay = sb("logdecay", [P, NT, GH])
        decay = sb("decay", [P, 3, NT, GH])
        rinv = sb("rinv", [P, 2 * GH, NT])
        cleared = sem("cleared")
        with ExitStack() as first:
            xnT = first.enter_context(nc.sbuf_tensor("xnT", [P, BATCH, KCONV - 1 + SEQ], F32))
            with nc.Block() as block:
                @block.vector
                def _(dve):
                    dve.memset(xnT[:, :, 0:KCONV - 1], 0.0)
                    dve.memset(vT[:], 0.0).then_inc(cleared, 1)
                    dve.wait_ge(cleared, 1)
            normalise(nc, x, xn, lambda t, n: xnT[:, t // TB, KCONV - 1 + P * (t % TB):KCONV - 1 + P * (t % TB + n)], ident, "n0")
            delta_inputs(nc, ident, xnT, qT, kT, vT, gate, (beta, logdecay), rinv, decay, dram)
        delta_chunks(nc, x[:].rearrange("p t d -> p (t d)"), ident, identb, qT, kT, vT, gate, beta, logdecay, rinv, decay, dram)
        delta_outputs(nc, x, ident, gate, dram)

GH, HK, HV, KCONV = 6, 128, 32, 4
KD, VD = GH * HK, GH * HV
VB = [(0, 128), (128, VD - 128)]
NBLK = 2 * GH + len(VB)
LEVELS = 7
SMALL = NT * GH
SERIES = range(15, 1, -2)
GATE_G = 13 + len(SERIES)


def delta_inputs(nc, ident, xnT, qT, kT, vT, gate, beta, rinv, decay, dram):
    beta, logdecay = beta
    with ExitStack() as ctx:
        sb, ps, sem = buffers(nc, ctx)
        w_qkv = sb("d_w_qkv", [P, 2 * KD + VD])
        w_abg = sb("d_w_abg", [P, 2 * GH + VD])
        w_conv = sb("d_w_conv", [P, NBLK, KCONV])
        dt_bias = sb("d_dt_bias", [P, GH])
        a_log = sb("d_a_log", [P, GH])
        tri = sb("d_tri", [P, 3, P])
        raw = [sb(f"d_raw{i}", [P, KCONV - 1 + SEQ]) for i in range(2)]
        conv = [sb(f"d_conv{i}", [P, SEQ]) for i in range(2)]
        sqd = [sb(f"d_sqd{i}", [P, SEQ]) for i in range(2)]
        rs_tmp = sb("d_rs_tmp", [P, 2 * GH * NT])
        zab = sb("d_zab", [P, NT, 2 * GH])
        za = sb("d_za", [P, NT, GH])
        e1 = sb("d_e1", [P, NT, GH])
        s1 = sb("d_s1", [P, NT, GH])
        s2 = sb("d_s2", [P, NT, GH])
        pl = sb("d_pl", [P, NT, GH])
        ssq = sb("d_ssq", [P, 2 * GH * NT])
        ssqT = sb("d_ssqT", [2 * GH, BATCH, SEQ])
        unit = sb("d_unit", [P, 4 * GH - 1])

        proj = [ps(f"d_proj{i}", [P, SEQ]) for i in range(2)]
        norms = [ps(f"d_norms{i}", [P, 512]) for i in range(2)]
        zp = [ps(f"d_zp{i}", [P, 512]) for i in range(2)]
        sums = norms[1]

        w_ld = sem("d_w_ld")
        init = sem("d_init")
        unit_rdy = sem("d_unit_rdy")
        proj_done = sem("d_proj_done")
        raw_rdy = sem("d_raw_rdy")
        conv_rdy = sem("d_conv_rdy")
        tap_rdy = sem("d_tap_rdy")
        silu_rdy = sem("d_silu_rdy")
        sqd_rdy = sem("d_sqd_rdy")
        norm_done = sem("d_norm_done")
        norm_rdy = sem("d_norm_rdy")
        norm_turned = sem("d_norm_turned")
        z_done = sem("d_z_done")
        z_rdy = sem("d_z_rdy")
        gate_step = sem("d_gate_step")
        act_step = sem("d_act_step")
        ssq_rdy = sem("d_ssq_rdy")
        rinv_step = sem("d_rinv_step")
        rinv_rdy = sem("d_rinv_rdy")
        sums_done = sem("d_sums_done")
        tick = {e: sem(f"d_tick_{e}") for e in ("pe", "act", "dve", "pool")}

        def rows(f):
            return P if f < 2 * GH else VB[f - 2 * GH][1]

        def convolved(f, b):
            if f < GH:
                return qT[:, f, bass.ds(b * SEQ, SEQ)]
            if f < 2 * GH:
                return kT[:, f - GH, bass.ds(b * SEQ, SEQ)]
            return vT[0:rows(f), f - 2 * GH, bass.ds(b * SEQ, SEQ)]

        block = ctx.enter_context(nc.Block())

        @block.sync
        def _(sp):
            for dst, src in ((w_qkv[:], dram["d_w_qkv"]), (w_abg[:], dram["d_w_abg"]), (w_conv[:], dram["d_w_conv"]),
                             (dt_bias[:], dram["d_dt_bias"].broadcast_to([P, GH])),
                             (a_log[:], dram["d_a_log"].broadcast_to([P, GH])), (tri[:], dram["d_tri"])):
                sp.dma_start(dst, src).then_inc(w_ld, 16)

        @block.tensor
        def _(pe):
            pe.wait_ge(w_ld, 96)
            pe.wait_ge(init, 1)
            with pe.Fori(0, BATCH) as b:
                for f in range(NBLK):
                    i = b * NBLK + f
                    m = rows(f)
                    pe.wait_ge(raw_rdy, i + 1)
                    pe.sem_inc(tick["pe"], 1)
                    for c in range(SEQ // 512):
                        mm = pe.matmul(proj[f % 2][0:m, 512 * c:512 * c + 512], w_qkv[:, P * f:P * f + m],
                                       xnT[:, bass.ds(b, 1), KCONV - 1 + 512 * c:KCONV - 1 + 512 * c + 512],
                                       start=True, stop=True)
                    mm.then_inc(proj_done, 1)
                    if f >= 2:
                        head = f - 2
                        if head == 0:
                            pe.wait_ge(norm_rdy, b + 1)
                        pe.wait_ge(sqd_rdy, b * 2 * GH + head + 1)
                        pe.sem_inc(tick["pe"], 1)
                        for c in range(SEQ // 512):
                            mm = pe.matmul(norms[c][0:2 * GH, :], unit[:, 2 * GH - 1 - head:4 * GH - 1 - head],
                                           sqd[f % 2][:, 512 * c:512 * c + 512], start=(head == 0), stop=(head == 2 * GH - 1),
                                           skip_group_check=True)
                        mm.then_inc(norm_done, 1)
            pe.wait_ge(norm_rdy, BATCH + 1)
            for t in range(NT):
                b, k = t // TB, t % TB
                mm = pe.transpose(norms[0][:, 2 * GH * t:2 * GH * t + 2 * GH], ssqT[:, b, P * k:P * k + P],
                                  ident[0:2 * GH, 0:2 * GH])
            mm.then_inc(norm_turned, 1)
            for t in range(NT):
                b, k = t // TB, t % TB
                if t >= 2:
                    pe.wait_ge(z_rdy, t - 1)
                pe.matmul(zp[t % 2][:, 0:2 * GH + VD], xnT[:, b, KCONV - 1 + P * k:KCONV - 1 + P * k + P], w_abg[:],
                          start=True, stop=True).then_inc(z_done, 1)
            pe.wait_ge(gate_step, GATE_G)
            for a in range(3):
                mm = pe.matmul(sums[:, SMALL * a:SMALL * a + SMALL], tri[:, a, :], logdecay[:].rearrange("p t h -> p (t h)"),
                               start=True, stop=True, skip_group_check=True)
            mm.then_inc(sums_done, 1)

        @block.scalar
        def _(act):
            act.wait_ge(init, 1)
            with act.Fori(0, BATCH) as b:
                def keep_raw(f):
                    i = b * NBLK + f
                    m = rows(f)
                    act.wait_ge(proj_done, i + 1)
                    act.wait_ge(conv_rdy, i + 1)
                    act.activation(raw[f % 2][0:m, KCONV - 1:], proj[f % 2][0:m, :], ACT.Copy).then_inc(raw_rdy, 1)

                keep_raw(0)
                for f in range(NBLK):
                    i = b * NBLK + f
                    m = rows(f)
                    if f + 1 < NBLK:
                        keep_raw(f + 1)
                    act.wait_ge(conv_rdy, i + 3)
                    act.sem_inc(tick["act"], 1)
                    act.activation(convolved(f, b), conv[f % 2][0:m, :], ACT.Silu).then_inc(silu_rdy, 1)
                    if f < 2 * GH:
                        act.wait_ge(silu_rdy, i + 3)
                        act.wait_ge(norm_done, b * 2 * GH + f + 1)
                        act.sem_inc(tick["act"], 1)
                        act.activation(sqd[f % 2][:], convolved(f, b), ACT.Square).then_inc(sqd_rdy, 1)
                act.wait_ge(norm_done, b * 2 * GH + 2 * GH + 2)
                act.sem_inc(tick["act"], 1)
                for c in range(2):
                    last = act.activation(ssqT[:, bass.ds(b, 1), 512 * c:512 * c + 512].rearrange("p a t -> p (a t)"),
                                          norms[c][0:2 * GH, :], ACT.Copy)
                last.then_inc(norm_rdy, 1)
            for t in range(NT):
                act.wait_ge(z_done, t + 1)
                act.activation(gate[:, t, :], zp[t % 2][:, 2 * GH:2 * GH + VD], ACT.Silu)
                act.activation(zab[:, t, :], zp[t % 2][:, 0:2 * GH], ACT.Copy).then_inc(z_rdy, 1)
            act.wait_ge(z_rdy, NT)
            act.wait_ge(gate_step, 1)
            act.activation(beta[:], beta[:], ACT.Exp, scale=-1.0).then_inc(act_step, 1)
            act.activation(a_log[:], a_log[:], ACT.Exp).then_inc(act_step, 1)
            act.wait_ge(gate_step, 3)
            act.activation(e1[:], s1[:], ACT.Exp, scale=-1.0).then_inc(act_step, 1)
            act.wait_ge(sums_done, 1)
            act.activation(decay[:].rearrange("p a t h -> p (a t h)"), sums[:, 0:3 * SMALL], ACT.Exp).then_inc(act_step, 1)
            act.wait_ge(act_step, 4)

        @block.vector
        def _(dve):
            dve.memset(unit[:], 0.0).then_inc(unit_rdy, 1)
            dve.wait_ge(unit_rdy, 1)
            dve.memset(unit[:, 2 * GH - 1:2 * GH], 1.0)
            for i in range(2):
                last = dve.memset(raw[i][:, 0:KCONV - 1], 0.0)
            last.then_inc(init, 1)
            dve.sem_inc(raw_rdy, 2)
            dve.sem_inc(conv_rdy, 2)
            dve.sem_inc(silu_rdy, 2)
            dve.sem_inc(norm_done, 2)
            dve.sem_inc(norm_rdy, 1)
            dve.wait_ge(w_ld, 96)
            with dve.Fori(0, BATCH) as b:
                for f in range(NBLK):
                    i = b * NBLK + f
                    m = rows(f)
                    x, y = raw[f % 2], conv[f % 2][0:m, :]
                    dve.wait_ge(raw_rdy, i + 3)
                    dve.wait_ge(silu_rdy, i + 1)
                    dve.tensor_scalar(y, x[0:m, 0:SEQ], w_conv[0:m, f, 0:1], None, ALU.mult).then_inc(tap_rdy, 1)
                    for j in range(1, KCONV):
                        dve.wait_ge(tap_rdy, i * (KCONV - 1) + j)
                        dve.sem_inc(tick["dve"], 1)
                        dve.scalar_tensor_tensor(y, x[0:m, j:j + SEQ], w_conv[0:m, f, j:j + 1], y, ALU.mult, ALU.add)\
                           .then_inc(tap_rdy if j < KCONV - 1 else conv_rdy, 1)
            dve.wait_ge(norm_turned, 1)
            dve.tensor_copy(ssq[:].rearrange("p (f t) -> p t f", t=NT),
                            norms[0][:, 0:2 * GH * NT].rearrange("p (t f) -> p t f", f=2 * GH)).then_inc(ssq_rdy, 1)

            steps = 0

            def step(ins):
                nonlocal steps
                steps += 1
                ins.then_inc(gate_step, 1)
                dve.wait_ge(gate_step, steps)

            def over(row):
                return row[:].rearrange("p (o h) -> p o h", o=1).to_broadcast([P, NT, GH])

            dve.wait_ge(z_rdy, NT)
            step(dve.tensor_scalar(beta[:], zab[:, :, GH:2 * GH], -EXP_MAX, None, ALU.max))
            step(dve.tensor_tensor(za[:], zab[:, :, 0:GH], over(dt_bias), ALU.add))
            step(dve.scalar_tensor_tensor(s1[:], za[:], -1.0, za[:], ALU.mult, ALU.max))
            dve.wait_ge(act_step, 3)
            step(dve.tensor_scalar(s2[:], e1[:], 2.0, None, ALU.add))
            step(dve.reciprocal(s2[:], s2[:]))
            step(dve.tensor_tensor(s1[:], e1[:], s2[:], ALU.mult))
            step(dve.tensor_tensor(s2[:], s1[:], s1[:], ALU.mult))
            step(dve.tensor_scalar(pl[:], s2[:], 1.0 / 17, None, ALU.mult))
            for k in SERIES:
                step(dve.scalar_tensor_tensor(pl[:], pl[:], 1.0 / k, s2[:], ALU.add, ALU.mult))
            step(dve.scalar_tensor_tensor(pl[:], pl[:], 1.0, s1[:], ALU.add, ALU.mult))
            step(dve.tensor_scalar(za[:], za[:], 0.0, None, ALU.max))
            step(dve.scalar_tensor_tensor(pl[:], pl[:], 2.0, za[:], ALU.mult, ALU.add))
            step(dve.scalar_tensor_tensor(logdecay[:], pl[:], -1.0, over(a_log), ALU.mult, ALU.mult))
            assert steps == GATE_G - 1
            step(dve.tensor_scalar(logdecay[:], logdecay[:], NEG, None, ALU.max))
            step(dve.tensor_scalar(beta[:], beta[:], 1.0, None, ALU.add))
            step(dve.reciprocal(beta[:], beta[:]))

        @block.gpsimd
        def _(pool):
            pool.wait_ge(ssq_rdy, 1)
            flat = rinv[:].rearrange("p f t -> p (f t)")
            rsqrt(pool, flat, ssq[:], rs_tmp[:], 0.0, 1e-6, rinv_step, 0, tick["pool"])
            pool.wait_ge(rinv_step, RSQRT_STEPS)
            pool.tensor_scalar(rinv[:, 0:GH, :], rinv[:, 0:GH, :], float(HK) ** -0.5, None, ALU.mult).then_inc(rinv_rdy, 1)
            pool.wait_ge(rinv_rdy, 1)


def delta_chunks(nc, spare, ident, identb, qT, kT, vT, gate, beta, logdecay, rinv, decay, dram):
    with ExitStack() as ctx:
        sb, ps, sem = buffers(nc, ctx)
        tri = sb("c_tri", [P, 3, P])
        causal = sb("c_causal", [P, P], BF16)
        blocks = sb("c_blocks", [P, LEVELS, P], BF16)
        two = range(BATCH)

        def each(name, shape, dt=F32):
            return [sb(f"c_{name}{b}", shape, dt) for b in two]

        kt_in = each("kt_in", [P, GH, P])
        kq = each("kq", [P, GH, 2, P])
        vt_in = each("vt_in", [P, 2, P])
        kn = each("kn", [P, GH, P])
        kb = each("kb", [P, GH, P])
        m1 = each("m1", [P, GH, P])
        atm1 = each("atm1", [P, GH, P])
        gt = each("gt", [P, GH, P])
        at = each("at", [P, GH, P])
        mt = [spare[:, GH * P * b:GH * P * (b + 1)].rearrange("p (h t) -> p h t", h=GH) for b in two]
        bv = [spare[:, 2 * GH * P + VD * b:2 * GH * P + VD * (b + 1)].rearrange("p (h v) -> p h v", h=GH) for b in two]
        rhs = each("rhs", [P, GH, HV])
        upd = each("upd", [P, GH, HV])
        state = each("state", [P, GH, HV])
        knT, inv, invT, out = kt_in, kt_in, gt, bv
        u = [kb[b][:, :, 0:P // 2].rearrange("p h t -> p h t") for b in two]
        atm = [m1, atm1]

        g0 = [ps(f"c_g0{b}", [P, 1024]) for b in two]
        g1 = [ps(f"c_g1{b}", [P, 1024]) for b in two]

        def heads(buf):
            return buf[:, 0:GH * P].rearrange("p (h t) -> p h t", h=GH)

        def half_heads(buf):
            return buf[:, 0:GH * P // 2].rearrange("p (h t) -> p h t", h=GH)

        def columns(x, l, odd):
            lead = " ".join("abc"[:len(x.shape) - 1])
            x = x.rearrange(f"{lead} (n e s) -> {lead} n e s", e=2, s=1 << l)
            return x[..., odd, :]

        def blocked(x, l):
            lead = " ".join("abc"[:len(x.shape) - 1])
            return x.rearrange(f"{lead} (n s) -> {lead} n s", s=1 << l)

        def sems(name):
            return [sem(f"c_{name}{b}") for b in two]

        const_ld = sem("c_const_ld")
        init = sem("c_init")
        tile_in, turned, kn_rdy, m1_rdy, kb_rdy, kdec_rdy = (sems(x) for x in
            ("tile_in", "turned", "kn_rdy", "m1_rdy", "kb_rdy", "kdec_rdy"))
        kT_done, kT_rdy, gam_done, gt_rdy, kk_done, qk_done = (sems(x) for x in
            ("kT_done", "kT_rdy", "gam_done", "gt_rdy", "kk_done", "qk_done"))
        at_rdy, mt_rdy, atm_rdy, tt0_rdy, t0_done, t0_rdy = (sems(x) for x in
            ("at_rdy", "mt_rdy", "atm_rdy", "tt0_rdy", "t0_done", "t0_rdy"))
        u_done, u_rdy, w_done, t_rdy, tt_done, tt_rdy, ttf_rdy = (sems(x) for x in
            ("u_done", "u_rdy", "w_done", "t_rdy", "tt_done", "tt_rdy", "ttf_rdy"))
        po_done, rhs_step, d_done, d_rdy, od_done, s_step, s_rdy, o_step, out_rdy = (sems(x) for x in
            ("po_done", "rhs_step", "d_done", "d_rdy", "od_done", "s_step", "s_rdy", "o_step", "out_rdy"))
        tick = {e: sem(f"c_tick_{e}") for e in ("pe", "act", "dve", "pool")}
        LV = LEVELS - 1
        block = ctx.enter_context(nc.Block())

        @block.sync
        def _(sp):
            sp.dma_start(tri[:], dram["d_tri"]).then_inc(const_ld, 16)
            sp.dma_start(causal[:], dram["d_causal"]).then_inc(const_ld, 16)
            sp.dma_start(blocks[:], dram["d_blocks"]).then_inc(const_ld, 16)

        @block.tensor
        def _(pe):
            pe.wait_ge(const_ld, 48)
            pe.wait_ge(init, 1)
            with pe.Fori(0, TB) as i:
                for b in two:
                    pe.wait_ge(tile_in[b], i + 1)
                    pe.wait_ge(out_rdy[b], i + 1)
                    for h in range(GH):
                        pe.transpose(heads(g0[b])[:, h, :], kt_in[b][:, h, :], ident[:])
                    for c, (c0, cn) in enumerate(VB):
                        mm = pe.transpose(g1[b][:, c0:c0 + cn], vt_in[b][0:cn, c, :], ident[0:cn, 0:cn])
                    mm.then_inc(turned[b], 1)
                for b in two:
                    pe.wait_ge(kn_rdy[b], i + 1)
                    for h in range(GH):
                        mm = pe.transpose(heads(g0[b])[:, h, :], kn[b][:, h, :], ident[:])
                    mm.then_inc(kT_done[b], 1)
                    pe.wait_ge(kb_rdy[b], i + 1)
                    for h in range(GH):
                        mm = pe.transpose(heads(g1[b])[:, h, :], kb[b][:, h, :], ident[:])
                    mm.then_inc(kT_done[b], 1)
                for b in two:
                    pe.wait_ge(kT_rdy[b], i * 2 + 1)
                    pe.wait_ge(m1_rdy[b], i + 1)
                    for h0, hn in ((0, 4), (4, 2)):
                        pe.matmul(heads(g0[b])[:, h0:h0 + hn, :], identb[:],
                                  causal[:].rearrange("p (o t) -> p o t", o=1).to_broadcast([P, hn, P]),
                                  start=True, stop=False, skip_group_check=True)
                        for h in range(h0, h0 + hn):
                            mm = pe.matmul(heads(g0[b])[:, h, :], m1[b][:, h, :], tri[:, 0, :], start=False, stop=True,
                                           skip_group_check=True)
                    mm.then_inc(gam_done[b], 1)
                for b in two:
                    pe.wait_ge(kT_rdy[b], i * 2 + 2)
                    for h in range(GH):
                        mm = pe.matmul(heads(g1[b])[:, h, :], knT[b][:, h, :], kq[b][:, h, 0, :], start=True, stop=True,
                                       skip_group_check=True)
                    mm.then_inc(kk_done[b], 1)
                    pe.wait_ge(gt_rdy[b], i + 1)
                    for h in range(GH):
                        mm = pe.matmul(heads(g0[b])[:, h, :], knT[b][:, h, :], kq[b][:, h, 1, :], start=True, stop=True,
                                       skip_group_check=True)
                    mm.then_inc(qk_done[b], 1)
                for b in two:
                    pe.wait_ge(tt0_rdy[b], i + 1)
                    for h in range(GH):
                        mm = pe.transpose(heads(g1[b])[:, h, :], invT[b][:, h, :], ident[:])
                    mm.then_inc(t0_done[b], 1)
                for l in range(1, LEVELS):
                    for b in two:
                        pe.wait_ge(atm_rdy[b], i * LEVELS + l + 1)
                        if l == 1:
                            pe.wait_ge(t0_rdy[b], i + 1)
                            pe.wait_ge(mt_rdy[b], i + 1)
                        else:
                            pe.wait_ge(t_rdy[b], i * (LV - 1) + l - 1)
                            pe.wait_ge(tt_rdy[b], i * (LV - 1) + l - 1)
                        for h in range(GH):
                            mm = pe.matmul(half_heads(g0[b])[:, h, :], atm[l % 2][b][:, h, :],
                                           columns(inv[b][:, h, :], l, 0), start=True, stop=True, skip_group_check=True)
                        mm.then_inc(u_done[b], 1)
                    for b in two:
                        pe.wait_ge(u_rdy[b], i * LV + l)
                        for h in range(GH):
                            if l < LV:
                                mm = pe.matmul(half_heads(g1[b])[:, h, :], invT[b][:, h, :], u[b][:, h, :], start=True,
                                               stop=True, skip_group_check=True)
                            else:
                                mm = pe.matmul(half_heads(g1[b])[0:P // 2, h, :], u[b][:, h, :],
                                               columns(invT[b][:, h, :], l, 1), start=True, stop=True, skip_group_check=True)
                        mm.then_inc(w_done[b], 1)
                    if l < LV:
                        for b in two:
                            pe.wait_ge(t_rdy[b], i * (LV - 1) + l)
                            for h in range(GH):
                                mm = pe.transpose(heads(g0[b])[:, h, :], inv[b][:, h, :], ident[:])
                            mm.then_inc(tt_done[b], 1)
                for b in two:
                    pe.wait_ge(ttf_rdy[b], i + 1)
                    pe.wait_ge(s_rdy[b], i + 1)
                    for a in range(2):
                        for h in range(GH):
                            mm = pe.matmul(g1[b][:, VD * a + HV * h:VD * a + HV * h + HV], kq[b][:, h, a, :],
                                           state[b][:, h, :], start=True, stop=True, skip_group_check=True)
                    mm.then_inc(po_done[b], 1)
                for b in two:
                    pe.wait_ge(rhs_step[b], i * 2 + 2)
                    for h in range(GH):
                        mm = pe.matmul(g0[b][:, HV * h:HV * h + HV], invT[b][:, h, :], rhs[b][:, h, :], start=True,
                                       stop=True, skip_group_check=True)
                    mm.then_inc(d_done[b], 1)
                for b in two:
                    pe.wait_ge(d_rdy[b], i + 1)
                    pe.wait_ge(kdec_rdy[b], i + 1)
                    for h in range(GH):
                        pe.matmul(g0[b][:, 512 + HV * h:512 + HV * h + HV], mt[b][:, h, :], upd[b][:, h, :], start=True,
                                  stop=True, skip_group_check=True)
                    for h in range(GH):
                        mm = pe.matmul(g0[b][:, 512 + VD + HV * h:512 + VD + HV * h + HV], kn[b][:, h, :],
                                       upd[b][:, h, :], start=True, stop=True, skip_group_check=True)
                    mm.then_inc(od_done[b], 1)

        @block.scalar
        def _(act):
            def keep(dst, src, done, value, rdy, func=ACT.Copy):
                act.wait_ge(done, value)
                act.activation(dst, src, func).then_inc(rdy, 1)

            with act.Fori(0, TB) as i:
                for b in two:
                    keep(knT[b][:], heads(g0[b]), kT_done[b], i * 2 + 1, kT_rdy[b])
                    keep(kq[b][:, :, 0, :], heads(g1[b]), kT_done[b], i * 2 + 2, kT_rdy[b])
                for b in two:
                    keep(gt[b][:], heads(g0[b]), gam_done[b], i + 1, gt_rdy[b], ACT.Exp)
                for b in two:
                    keep(inv[b][:], heads(g1[b]), t0_done[b], i + 1, t0_rdy[b])
                for l in range(1, LEVELS):
                    for b in two:
                        keep(u[b][:], half_heads(g0[b]), u_done[b], i * LV + l + 1, u_rdy[b])
                    if l < LV:
                        for b in two:
                            keep(invT[b][:], heads(g0[b]), tt_done[b], i * (LV - 1) + l, tt_rdy[b])
                for b in two:
                    keep(upd[b][:].rearrange("p h v -> p (h v)"), g0[b][:, 0:VD], d_done[b], i + 1, d_rdy[b])

        @block.vector
        def _(dve):
            def across(small, n):
                return small.rearrange("p (h o) -> p h o", o=1).to_broadcast([P, GH, n])

            for b in two:
                mm = dve.memset(state[b][:], 0.0)
            mm.then_inc(init, 1)
            for b in two:
                dve.sem_inc(s_rdy[b], 1)
                dve.sem_inc(out_rdy[b], 1)
                dve.sem_inc(u_done[b], 1)
            dve.wait_ge(const_ld, 48)
            with dve.Fori(0, TB) as i:
                for b in two:
                    t0 = i * P + b * SEQ
                    dve.tensor_copy(kq[b][:, :, 1, :], qT[:, :, bass.ds(t0, P)])
                    dve.tensor_copy(vt_in[b][:], vT[:, :, bass.ds(t0, P)])
                    dve.tensor_copy(kt_in[b][:], kT[:, :, bass.ds(t0, P)]).then_inc(tile_in[b], 1)
                for b in two:
                    t = i + b * TB
                    small = lambda x: x.rearrange("p a h -> p (a h)")
                    dve.wait_ge(turned[b], i + 1)
                    dve.tensor_tensor(bv[b], g1[b][:, 0:VD].rearrange("p (h v) -> p h v", h=GH),
                                      across(small(beta[:, bass.ds(t, 1), :]), HV), ALU.mult)
                    dve.tensor_tensor(kn[b][:], heads(g0[b]),
                                      across(rinv[:, GH:2 * GH, bass.ds(t, 1)].rearrange("p h a -> p (h a)"), P),
                                      ALU.mult).then_inc(kn_rdy[b], 1)
                for b in two:
                    dve.wait_ge(gt_rdy[b], i + 1)
                    dve.wait_ge(kk_done[b], i + 1)
                    dve.tensor_tensor(at[b][:], heads(g1[b]), gt[b][:], ALU.mult).then_inc(at_rdy[b], 1)
                    dve.wait_ge(qk_done[b], i + 1)
                    dve.tensor_tensor(mt[b], heads(g0[b]), gt[b][:], ALU.mult).then_inc(mt_rdy[b], 1)
                for b in two:
                    dve.wait_ge(mt_rdy[b], i + 1)
                    dve.wait_ge(atm_rdy[b], i * LEVELS + 1)
                    dve.tensor_tensor(invT[b][:], ident[:].rearrange("p (o t) -> p o t", o=1).to_broadcast([P, GH, P]),
                                      atm[0][b][:], ALU.subtract).then_inc(tt0_rdy[b], 1)
                for l in range(1, LV):
                    for b in two:
                        dve.wait_ge(w_done[b], i * LV + l)
                        changed = columns(inv[b][:], l, 0)
                        dve.tensor_tensor(changed, changed, blocked(half_heads(g1[b]), l), ALU.subtract).then_inc(t_rdy[b], 1)
                for b in two:
                    dve.wait_ge(w_done[b], i * LV + LV)
                    changed = invT[b][0:P // 2, :, P // 2:P]
                    dve.tensor_tensor(changed, changed, half_heads(g1[b])[0:P // 2], ALU.subtract).then_inc(ttf_rdy[b], 1)
                small = lambda x: x.rearrange("p a h -> p (a h)")
                for b in two:
                    t = i + b * TB
                    upto = across(small(decay[:, 0, bass.ds(t, 1), :]), HV)
                    whole = across(small(decay[:, 2, bass.ds(t, 1), :]), HV)
                    po = g1[b][:, 0:2 * VD].rearrange("p (a h v) -> p a h v", a=2, h=GH)
                    dve.wait_ge(po_done[b], i + 1)
                    dve.tensor_tensor(rhs[b][:], po[:, 0], upto, ALU.mult).then_inc(rhs_step[b], 1)
                    dve.wait_ge(rhs_step[b], i * 2 + 1)
                    dve.tensor_tensor(rhs[b][:], bv[b], rhs[b][:], ALU.subtract).then_inc(rhs_step[b], 1)
                    dve.tensor_tensor(state[b][:], state[b][:], whole, ALU.mult).then_inc(s_step[b], 1)
                    dve.wait_ge(rhs_step[b], i * 2 + 2)
                    dve.tensor_tensor(out[b], po[:, 1], upto, ALU.mult).then_inc(o_step[b], 1)
                for b in two:
                    t = i + b * TB
                    od = g0[b][:, 512:512 + 2 * VD].rearrange("p (a h v) -> p a h v", a=2, h=GH)
                    dve.wait_ge(od_done[b], i + 1)
                    dve.wait_ge(s_step[b], i + 1)
                    dve.tensor_tensor(state[b][:], state[b][:], od[:, 1], ALU.add).then_inc(s_rdy[b], 1)
                    dve.wait_ge(o_step[b], i * 3 + 1)
                    dve.tensor_tensor(out[b], out[b], od[:, 0], ALU.add).then_inc(o_step[b], 1)
                    dve.wait_ge(o_step[b], i * 3 + 2)
                    dve.tensor_tensor(out[b], out[b],
                                      across(rinv[:, 0:GH, bass.ds(t, 1)].rearrange("p h a -> p (h a)"), HV),
                                      ALU.mult).then_inc(o_step[b], 1)
                    dve.wait_ge(o_step[b], i * 3 + 3)
                    gt_tile = gate[:, bass.ds(t, 1), :].rearrange("p a f -> p (a f)")
                    dve.tensor_tensor(gt_tile, out[b].rearrange("p h v -> p (h v)"), gt_tile, ALU.mult)\
                       .then_inc(out_rdy[b], 1)
            for b in two:
                dve.wait_ge(out_rdy[b], TB + 1)

        @block.gpsimd
        def _(pool):
            def across(small):
                return small.rearrange("p a h -> p (a h)").rearrange("p (h o) -> p h o", o=1).to_broadcast([P, GH, P])

            def over(mask):
                return mask.rearrange("p (o t) -> p o t", o=1).to_broadcast([P, GH, P])

            pool.wait_ge(const_ld, 48)
            with pool.Fori(0, TB) as i:
                for b in two:
                    t = i + b * TB
                    pool.wait_ge(u_done[b], i * LV + 1)
                    pool.sem_inc(tick["pool"], 1)
                    pool.tensor_tensor(m1[b][:], over(tri[:, 1, :]), across(logdecay[:, bass.ds(t, 1), :]),
                                       ALU.mult).then_inc(m1_rdy[b], 1)
                for b in two:
                    t = i + b * TB
                    pool.wait_ge(kn_rdy[b], i + 1)
                    pool.sem_inc(tick["pool"], 1)
                    pool.tensor_tensor(kb[b][:], kn[b][:], across(beta[:, bass.ds(t, 1), :]), ALU.mult).then_inc(kb_rdy[b], 1)
                for b in two:
                    t = i + b * TB
                    pool.wait_ge(kT_done[b], i * 2 + 1)
                    pool.wait_ge(kb_rdy[b], i + 1)
                    pool.sem_inc(tick["pool"], 1)
                    pool.tensor_tensor(kn[b][:], kn[b][:], across(decay[:, 1, bass.ds(t, 1), :]), ALU.mult)\
                        .then_inc(kdec_rdy[b], 1)
                for l in range(LEVELS):
                    for b in two:
                        if l == 0:
                            pool.wait_ge(at_rdy[b], i + 1)
                        elif l == 2:
                            pool.wait_ge(tt0_rdy[b], i + 1)
                        elif l > 2:
                            pool.wait_ge(u_done[b], i * LV + l - 1)
                        pool.tensor_tensor(atm[l % 2][b][:], at[b][:], over(blocks[:, l, :]), ALU.mult)\
                            .then_inc(atm_rdy[b], 1)


def delta_outputs(nc, x, ident, og, dram):
    with ExitStack() as ctx:
        sb, ps, sem = buffers(nc, ctx)
        nw = sb("o_nw", [P, VD])
        wo = sb("o_wo", [P, len(VB), D])
        sq = [sb(f"o_sq{i}", [P, VD]) for i in range(2)]
        ms = sb("o_ms", [P, NT])
        rstd = sb("o_rstd", [P, NT])
        tmp = sb("o_tmp", [P, NT])
        on = [sb(f"o_on{i}", [P, VD]) for i in range(2)]
        oT = [sb(f"o_oT{i}", [P, len(VB), P]) for i in range(2)]
        tp = [ps(f"o_tp{i}", [P, 512]) for i in range(2)]
        yp = [ps(f"o_yp{i}", [P, 512]) for i in range(2)]
        x_ld, w_ld, ms_rdy, rs_rdy, on_rdy, tp_done, oT_rdy, y_done, x_rdy, tick = (sem("o_" + s) for s in (
            "x_ld", "w_ld", "ms_rdy", "rs_rdy", "on_rdy", "tp_done", "oT_rdy", "y_done", "x_rdy", "tick"))
        block = ctx.enter_context(nc.Block())

        @block.sync
        def _(sp):
            sp.dma_start(nw[:], dram["d_nw"].broadcast_to([P, VD])).then_inc(w_ld, 16)
            sp.dma_start(wo[:], dram["d_wo"]).then_inc(w_ld, 16)

        @block.scalar
        def _(act):
            act.dma_start(x[:], dram["x"].rearrange("(t p) d -> p t d", p=P)).then_inc(x_ld, 16)
            for t in range(NT):
                if t >= 2:
                    act.wait_ge(ms_rdy, t - 1)
                act.activation(sq[t % 2][:], og[:, t, :], ACT.Square, scale=float(VD) ** -0.5, accum_out=ms[:, t:t + 1]).then_inc(ms_rdy, 1)
            for t in range(NT):
                act.wait_ge(tp_done, t + 1)
                for c, (c0, cn) in enumerate(VB):
                    last = act.activation(oT[t % 2][0:cn, c, :], tp[t % 2][0:cn, P * c:P * c + P], ACT.Copy)
                last.then_inc(oT_rdy, 1)

        @block.gpsimd
        def _(pool):
            pool.wait_ge(ms_rdy, NT)
            rsqrt(pool, rstd[:], ms[:], tmp[:], 0.0, 1e-5, rs_rdy, 0, tick)

        @block.vector
        def _(dve):
            dve.wait_ge(w_ld, 32)
            dve.wait_ge(rs_rdy, RSQRT_STEPS)
            dve.wait_ge(x_ld, 16)
            for t in range(NT):
                if t >= 2:
                    dve.wait_ge(tp_done, t - 1)
                dve.scalar_tensor_tensor(on[t % 2][:], og[:, t, :], rstd[:, t:t + 1], nw[:], ALU.mult, ALU.mult).then_inc(on_rdy, 1)
                if t >= 1:
                    dve.wait_ge(y_done, t)
                    dve.tensor_tensor(x[:, t - 1, :], x[:, t - 1, :], yp[(t - 1) % 2][:, 0:D], ALU.add).then_inc(x_rdy, 1)
            dve.wait_ge(y_done, NT)
            dve.tensor_tensor(x[:, NT - 1, :], x[:, NT - 1, :], yp[(NT - 1) % 2][:, 0:D], ALU.add).then_inc(x_rdy, 1)
            dve.wait_ge(x_rdy, NT)

        @block.tensor
        def _(pe):
            pe.wait_ge(w_ld, 32)
            for t in range(NT):
                pe.wait_ge(on_rdy, t + 1)
                if t >= 2:
                    pe.wait_ge(oT_rdy, t - 1)
                for c, (c0, cn) in enumerate(VB):
                    mm = pe.transpose(tp[t % 2][0:cn, P * c:P * c + P], on[t % 2][:, c0:c0 + cn], ident[:])
                mm.then_inc(tp_done, 1)
                pe.wait_ge(oT_rdy, t + 1)
                if t >= 2:
                    pe.wait_ge(x_rdy, t - 1)
                for c, (c0, cn) in enumerate(VB):
                    mm = pe.matmul(yp[t % 2][:, 0:D], oT[t % 2][0:cn, c, :], wo[0:cn, c, :], start=(c == 0), stop=(c == 1))
                mm.then_inc(y_done, 1)


def delta_constants():
    r, t = np.arange(P)[:, None], np.arange(P)[None, :]
    tri = np.stack([r <= t, r > t, np.ones((P, P), bool)], 1).astype(np.float32)
    causal = np.where(t < r, np.float32(NEG), np.float32(0))
    blocks = np.stack([(r // (2 * n) == t // (2 * n)) & (t % (2 * n) >= n) & (r % (2 * n) < n)
                       for n in (1 << l for l in range(LEVELS))], 1).astype(np.float32)
    return np.ascontiguousarray(tri), causal, np.ascontiguousarray(blocks)


def pack_delta_weights(q_w, k_w, v_w, a_w, b_w, g_w, o_w, conv_q_w, conv_k_w, conv_v_w):
    w_qkv = np.ascontiguousarray(np.concatenate([q_w, k_w, v_w], 0).T)
    w_abg = np.ascontiguousarray(np.concatenate([a_w, b_w, g_w], 0).T)
    conv = np.zeros((NBLK * P, KCONV), np.float32)
    conv[0:2 * KD + VD] = np.concatenate([conv_q_w, conv_k_w, conv_v_w], 0)
    wo = np.zeros((len(VB) * P, D), np.float32)
    wo[0:VD] = o_w.T
    return (w_qkv, w_abg, np.ascontiguousarray(conv.reshape(NBLK, P, KCONV).transpose(1, 0, 2)),
            np.ascontiguousarray(wo.reshape(len(VB), P, D).transpose(1, 0, 2)))

DEPTH, HEADS, DH, WIN = 6, 16, 64, 32
INNER = HEADS * DH
DFF = int(D * 4 * 2 / 3)
HP = HEADS // 2
NWIN = P // WIN
FB = [(0, 128), (128, 128), (256, DFF - 256)]
C_QKV, C_WO = 0, 3 * INNER
C_W1 = C_WO + HP * D
C_W2 = C_W1 + 2 * DFF
C_B1 = C_W2 + len(FB) * D
C_LN = C_B1 + 2 * len(FB)
NWC = C_LN + 2


def local_layers(nc, h, ident, identb, dram):
    with ExitStack() as ctx:
        sb, ps, sem = buffers(nc, ctx)

        wts = [sb(f"l_wts{i}", [P, NWC]) for i in range(2)]
        scales = [sb(f"l_scales{i}", [P, 4, DH]) for i in range(2)]
        b2row = [sb(f"l_b2row{i}", [1, D]) for i in range(2)]
        raw_tab = sb("l_raw_tab", [P, 4, TB, DH])
        tab = sb("l_tab", [P, 4, NT, DH])
        maskb = sb("l_maskb", [P, NT, 2 * WIN], BF16)
        carried = sb("l_carried", [P, NT])
        ones_row = sb("l_ones_row", [1, P])
        hcur = [sb(f"l_hcur{i}", [P, D]) for i in range(2)]
        xs = [sb(f"l_xs{i}", [P, 1 + P]) for i in range(2)]
        sq = sb("l_sq", [P, 2, 512])
        ss = [sb(f"l_ss{i}", [P, 2 * HEADS]) for i in range(2)]
        rn = sb("l_rn", [P, 2 * HEADS])
        rn_tmp = sb("l_rn_tmp", [P, 2 * HEADS])
        rot_a = [sb(f"l_rot_a{i}", [P, 4, 512]) for i in range(2)]
        rot_b = sb("l_rot_b", [P, 4, 512])
        qk = sb("l_qk", [P, 4, 512])
        qT = [sb(f"l_qT{i}", [P, HP, P]) for i in range(2)]
        kT = [sb(f"l_kT{i}", [P, HP, WIN + P]) for i in range(2)]
        v = [sb(f"l_v{i}", [P, HEADS, DH]) for i in range(2)]
        vprev = sb("l_vprev", [P, 4, DH])
        mx = sb("l_mx", [P, HEADS])
        sd = sb("l_sd", [P, HEADS, 2 * WIN])
        pw = sb("l_pw", [P, HEADS, P])
        pprev = sb("l_pprev", [WIN, 4, 4, WIN])
        pT = sb("l_pT", [P, HEADS, P])
        pTprev = sb("l_pTprev", [P, 4, WIN])
        rsum = sb("l_rsum", [P, HEADS])
        oT = sb("l_oT", [P, HP, P])
        GT = 4
        NG = NT // GT
        hgrp = [sb(f"l_hgrp{i}", [P, GT, D]) for i in range(2)]
        xs4 = [sb(f"l_xs4{i}", [P, 1 + GT * P]) for i in range(2)]
        st = [sb(f"l_st{i}", [P, GT, 6]) for i in range(2)]
        mv = [sb(f"l_mv{i}", [P, GT, 2]) for i in range(2)]
        rstd = [sb(f"l_rstd{i}", [P, GT]) for i in range(2)]
        rstd_tmp = [sb(f"l_rstd_tmp{i}", [P, GT]) for i in range(2)]
        xn = sb("l_xn", [P, GT, D])
        xnT = sb("l_xnT", [P, GT * P])
        gl = sb("l_gl", [P, 3, 512])
        u = sb("l_u", [P, 3, 512])

        bank = [ps(f"l_bank{i}", [P, 512]) for i in range(2)]
        score = ps("l_score", [P, HEADS, 2 * WIN])
        tp = [ps(f"l_tp{i}", [P, 512]) for i in range(2)]
        misc = [ps(f"l_misc{i}", [P, 512]) for i in range(2)]

        v_bank = [misc[0], tp[0]]
        wide = [misc[0][:], misc[1][:], score[:, 0:8, :].rearrange("p a b -> p (a b)")]
        y_ps = score[:, 8:16, :].rearrange("p a b -> p (a b)")

        const_ld = sem("l_const_ld")
        init = sem("l_init")
        w_ld = [sem(f"l_w_ld{i}") for i in range(2)]
        layer_done = sem("l_layer_done")
        tab_rdy = sem("l_tab_rdy")
        hcur_rdy = sem("l_hcur_rdy")
        xT_done = sem("l_xT_done")
        xs_rdy = sem("l_xs_rdy")
        carry_rdy = sem("l_carry_rdy")
        proj_done = sem("l_proj_done")
        vproj_done = sem("l_vproj_done")
        sq_rdy = sem("l_sq_rdy")
        v_rdy = sem("l_v_rdy")
        ss_rdy = sem("l_ss_rdy")
        rope_rdy = sem("l_rope_rdy")
        rn_rdy = sem("l_rn_rdy")
        rot_sum = sem("l_rot_sum")
        qk_rdy = sem("l_qk_rdy")
        qkT_done = sem("l_qkT_done")
        qkT_rdy = sem("l_qkT_rdy")
        kprev_rdy = sem("l_kprev_rdy")
        s_done = sem("l_s_done")
        mx_rdy = sem("l_mx_rdy")
        sd_rdy = sem("l_sd_rdy")
        p_rdy = sem("l_p_rdy")
        pT_done = sem("l_pT_done")
        pT_rdy = sem("l_pT_rdy")
        pv_own = sem("l_pv_own")
        pv_done = sem("l_pv_done")
        vprev_rdy = sem("l_vprev_rdy")
        e_rdy = sem("l_e_rdy")
        rs_step = sem("l_rs_step")
        oT_rdy = sem("l_oT_rdy")
        y_done = sem("l_y_done")
        h_rdy = sem("l_h_rdy")
        g_hgrp = sem("l_g_hgrp")
        g_xT = sem("l_g_xT")
        g_xs = sem("l_g_xs")
        g_back = sem("l_g_back")
        g_st = sem("l_g_st")
        g_mv = sem("l_g_mv")
        g_rstd = sem("l_g_rstd")
        g_xn = sem("l_g_xn")
        g_xnT = sem("l_g_xnT")
        g_xnT_rdy = sem("l_g_xnT_rdy")
        g_w1 = sem("l_g_w1")
        g_gl = sem("l_g_gl")
        g_u = sem("l_g_u")
        g_y = sem("l_g_y")
        g_h = sem("l_g_h")
        tick = {e: sem(f"l_tick_{e}") for e in ("pe", "act", "dve", "pool")}

        PAIRS = DEPTH // 2
        block = ctx.enter_context(nc.Block())

        def groups_before(lp, par):
            return lp * (2 * NG) + par * NG

        def by_layer(eng, attention, geglu):
            with eng.Fori(0, PAIRS) as lp:
                for par in range(2):
                    attention(lp, par, lp * (2 * NT) + par * NT)
                    geglu(lp, par, groups_before(lp, par))

        def slot(head):
            return HP * (head % 2) + head // 2

        def by_tile(start, tile, finish, eng, n0):
            start()
            tile(0, n0, 0, False, True, True, True)
            with eng.Fori(0, (NT - 4) // 2) as j:
                tile(j * 2 + 1, n0 + j * 2 + 1, 1, True, True, True, True)
                tile(j * 2 + 2, n0 + j * 2 + 2, 0, True, True, True, True)
            tile(NT - 3, n0 + NT - 3, 1, True, True, True, False)
            tile(NT - 2, n0 + NT - 2, 0, True, True, False, False)
            tile(NT - 1, n0 + NT - 1, 1, True, False, False, False)
            finish()

        @block.sync
        def _(sp):
            sp.dma_start(raw_tab[:], dram["l_tables"]).then_inc(const_ld, 16)
            sp.dma_start(maskb[:], dram["l_mask"]).then_inc(const_ld, 16)
            sp.dma_start(carried[:], dram["l_carried"]).then_inc(const_ld, 16)
            with sp.Fori(0, PAIRS) as lp:
                for par in range(2):
                    sp.wait_ge(layer_done, lp * 2 + par + 1)
                    sp.dma_start(wts[par][:], dram["l_wts"][bass.ds(lp * 2 + par, 1)].rearrange("a p n -> (a p) n")).then_inc(w_ld[par], 16)
                    sp.dma_start(scales[par][:].rearrange("p a d -> p (a d)"),
                                 dram["l_scales"][bass.ds(lp * 2 + par, 1)].broadcast_to([P, 4 * DH])).then_inc(w_ld[par], 16)
                    sp.dma_start(b2row[par][:], dram["l_b2"][bass.ds(lp * 2 + par, 1)]).then_inc(w_ld[par], 16)

        @block.tensor
        def _(pe):
            def group_in(k0, g):
                k = k0 + g
                pe.wait_ge(g_hgrp, k + 1)
                for i in range(GT):
                    last = pe.transpose(bank[g % 2][:, P * i:P * i + P], hgrp[g % 2][:, i, :], ident[:])
                last.then_inc(g_xT, 1)

            def group_back(k0, g):
                pe.wait_ge(g_xs, (k0 + g) * 3 + 4)
                for i in range(GT):
                    last = pe.transpose(bank[g % 2][:, P * i:P * i + P], xs4[g % 2][:, P * i:P * i + P], ident[:])
                last.then_inc(g_back, 1)

            def attention(lp, par, n0):
                w = wts[par]

                def scores_masked(t, n):
                    pe.wait_ge(qkT_rdy, n * 4 + 4 + 1)
                    pe.wait_ge(kprev_rdy, n + 1)
                    pe.wait_ge(sd_rdy, n + 1)
                    for c in range(2):
                        pe.matmul(score[:, 8 * c:8 * c + 8, :], identb[:],
                                  maskb[:, bass.ds(t, 1), :].to_broadcast([P, 8, 2 * WIN]),
                                  start=True, stop=False, skip_group_check=True)

                def scores(p, wds):
                    for wd in wds:
                        for hh in range(HEADS):
                            r = slice(DH * (hh % 2), DH * (hh % 2) + DH)
                            last = pe.matmul(score[WIN * wd:WIN * wd + WIN, slot(hh), :],
                                             qT[p][r, hh // 2, WIN * wd:WIN * wd + WIN],
                                             kT[p][r, hh // 2, WIN * wd:WIN * wd + 2 * WIN],
                                             start=False, stop=True, skip_group_check=True)
                    if wd == NWIN - 1:
                        last.then_inc(s_done, 1)

                def turn_in(n, p, keys=None):
                    if keys is not None:
                        pe.wait_ge(qkT_rdy, keys * 4 + 4 + 1)
                    pe.wait_ge(hcur_rdy, n + 1)
                    pe.transpose(tp[1][:, 0:P], hcur[p][:], ident[:]).then_inc(xT_done, 1)

                def project(n, p, js):
                    for j in js:
                        if j == 0:
                            pe.wait_ge(carry_rdy, n + 1)
                            pe.wait_ge(xs_rdy, n + 2)
                        pe.wait_ge(rope_rdy, n * 4 + j - 2 + 3)
                        pe.wait_ge(sq_rdy, n * 4 + j - 2 + 3)
                        pe.matmul(bank[j % 2][:], xs[p][:, 0:P], w[:, C_QKV + 512 * j:C_QKV + 512 * j + 512],
                                  start=True, stop=True).then_inc(proj_done, 1)

                def project_v(n, p, last):
                    for j in range(2):
                        if j == 1:
                            pe.wait_ge(qkT_rdy, n * 4 + 3 + 1)
                        elif last:
                            pe.wait_ge(oT_rdy, n * 2 - 3)
                        c = C_QKV + 2 * INNER + 512 * j
                        pe.matmul(v_bank[j][:], xs[p][:, 0:P], w[:, c:c + 512], start=True, stop=True).then_inc(vproj_done, 1)

                def turn_probs(m, ahead, half):
                    if half == 0:
                        if ahead:
                            pe.wait_ge(v_rdy, m * 2 + 6)
                        pe.wait_ge(p_rdy, m + 2)
                    for c in (2 * half, 2 * half + 1):
                        if c >= 2:
                            pe.wait_ge(pT_rdy, m * 5 + c - 1)
                        for k in range(4):
                            last = pe.transpose(tp[c % 2][:, P * k:P * k + P], pw[:, 4 * c + k, :], ident[:])
                        last.then_inc(pT_done, 1)
                    if half == 0:
                        return
                    pe.wait_ge(pT_rdy, m * 5 + 3)
                    pe.sem_inc(tick["pe"], 1)
                    for k in range(4):
                        last = pe.transpose(tp[0][:, WIN * k:WIN * k + WIN], pprev[:, k].rearrange("q r k -> q (r k)"),
                                            ident[0:WIN, 0:WIN])
                    last.then_inc(pT_done, 1)

                def values(m, p):
                    pe.wait_ge(v_rdy, m * 2 + 4)
                    pe.wait_ge(h_rdy, m + 2)
                    for c in range(2):
                        pe.wait_ge(pT_rdy, m * 5 + 3 + c)
                        pe.sem_inc(tick["pe"], 1)
                        for g in range(4):
                            for e in range(2):
                                pair = 4 * c + g
                                last = pe.matmul(misc[c][DH * e:DH * e + DH, P * g:P * g + P], v[p][:, 2 * pair + e, :],
                                                 pT[:, HP * e + pair, :], start=(g == 0), stop=False, skip_group_check=True)
                        last.then_inc(pv_own, 1)
                    pe.wait_ge(vprev_rdy, m + 2)
                    pe.wait_ge(pT_rdy, m * 5 + 5)
                    for c in range(2):
                        pe.wait_ge(pv_own, m * 2 + c + 1)
                        pe.sem_inc(tick["pe"], 1)
                        for g in range(4):
                            for e in range(2):
                                rows = slice(WIN * (2 * e + c), WIN * (2 * e + c) + WIN)
                                last = pe.matmul(misc[c][DH * e:DH * e + DH, P * g:P * g + WIN], vprev[rows, g, :],
                                                 pTprev[rows, g, :], start=False, stop=True, skip_group_check=True)
                        last.then_inc(pv_done, 1)

                def output(m):
                    pe.wait_ge(oT_rdy, m * 2 + 2)
                    for k in range(HP):
                        last = pe.matmul(misc[1][:, 0:D], oT[:, k, :], w[:, C_WO + D * k:C_WO + D * k + D],
                                         start=(k == 0), stop=(k == HP - 1))
                    last.then_inc(y_done, 1)

                def turn_qk(n, half):
                    if half == 0:
                        pe.wait_ge(v_rdy, n * 2 + 2)
                    for c in (2 * half, 2 * half + 1):
                        pe.wait_ge(qk_rdy, n * 4 + c + 1 + 8)
                        if c >= 2:
                            pe.wait_ge(qkT_rdy, n * 4 + c - 1 + 1)
                        for k in range(4):
                            last = pe.transpose(tp[c % 2][:, P * k:P * k + P], qk[:, c, P * k:P * k + P], ident[:])
                        last.then_inc(qkT_done, 1)

                def start():
                    for t in range(2):
                        turn_in(n0 + t, t)
                        project(n0 + t, t, range(4))
                    for half in range(2):
                        turn_qk(n0, half)
                    project_v(n0, 0, False)
                    turn_in(n0 + 2, 0, n0)
                    project(n0 + 2, 0, (0,))

                def tile(t, m, p, last, next1, next2, next3):
                    scores_masked(t, m)
                    scores(p, (0, 1))
                    if next2:
                        project(m + 2, p, (1,))
                    scores(p, (2, 3))
                    if last:
                        turn_probs(m - 1, True, 0)
                    if next2:
                        project(m + 2, p, (2,))
                    if last:
                        turn_probs(m - 1, True, 1)
                        values(m - 1, 1 - p)
                    if next1:
                        turn_qk(m + 1, 0)
                    if next2:
                        project(m + 2, p, (3,))
                    if next1:
                        turn_qk(m + 1, 1)
                        project_v(m + 1, 1 - p, last)
                    if next3:
                        turn_in(m + 3, 1 - p, m + 1)
                    if last:
                        output(m - 1)
                    if next3:
                        project(m + 3, 1 - p, (0,))
                    if next1 and not next2:
                        pe.wait_ge(rope_rdy, m * 4 + 4 + 6)
                        for g in range(2):
                            group_in(groups_before(lp, par), g)
                    if not next1:
                        for g in range(2):
                            group_back(groups_before(lp, par), g)

                def finish():
                    for half in range(2):
                        turn_probs(n0 + NT - 1, False, half)
                    values(n0 + NT - 1, 1)
                    output(n0 + NT - 1)

                pe.wait_ge(w_ld[par], lp * 48 + 48)
                if par == 0:
                    pe.wait_ge(const_ld, 48)
                    pe.wait_ge(init, 1)
                by_tile(start, tile, finish, pe, n0)

            def geglu(lp, par, k0):
                w = wts[par]

                def turn_norm(g):
                    pe.wait_ge(g_xn, (k0 + g) * GT + GT)
                    for i in range(GT):
                        last = pe.transpose(bank[g % 2][:, P * i:P * i + P], xn[:, i, :], ident[:])
                    last.then_inc(g_xnT, 1)

                def widen(g):
                    k = k0 + g
                    pe.wait_ge(g_xnT_rdy, k + 1)
                    for half in range(2):
                        if half == 1 and g + 2 < NG:
                            group_in(k0, g + 2)
                        for i, (c0, cn) in enumerate(FB):
                            if half == 0:
                                pe.wait_ge(g_u, k * 3 + i + 1)
                            else:
                                pe.wait_ge(g_gl, k * 3 + i + 1)
                            c = C_W1 + (DFF if half == 0 else 0) + c0
                            pe.matmul(wide[i][0:cn, :], w[:, c:c + cn], xnT[:], start=True, stop=True).then_inc(g_w1, 1)

                def narrow(g):
                    k = k0 + g
                    pe.wait_ge(g_h, k + 1)
                    pe.wait_ge(g_u, k * 3 + 6)
                    pe.matmul(y_ps.rearrange("p (a d) -> p a d", d=D), ones_row[:],
                              b2row[par][:].rearrange("o (a d) -> o a d", a=1).to_broadcast([1, GT, D]),
                              start=True, stop=False, skip_group_check=True)
                    for i in range(GT):
                        y = y_ps[:, D * i:D * i + D]
                        for f, (c0, cn) in enumerate(FB):
                            last = pe.matmul(y, u[0:cn, f, P * i:P * i + P], w[0:cn, C_W2 + D * f:C_W2 + D * f + D],
                                             start=False, stop=(f == len(FB) - 1), skip_group_check=True)
                    last.then_inc(g_y, 1)

                pe.wait_ge(h_rdy, lp * 32 + par * 16 + 18)
                pe.sem_inc(tick["pe"], 1)
                turn_norm(0)
                for g in range(NG):
                    widen(g)
                    if g + 2 < NG:
                        group_back(k0, g + 2)
                    if g + 1 < NG:
                        turn_norm(g + 1)
                    narrow(g)

            by_layer(pe, attention, geglu)

        @block.scalar
        def _(act):
            def group_shift(k0, g):
                k = k0 + g
                x, turned = xs4[g % 2], bank[g % 2]
                act.wait_ge(g_xT, k + 3)
                act.wait_ge(g_xs, k * 3 + 1)
                act.sem_inc(tick["act"], 1)
                act.activation(x[0:DH, 0:GT * P], turned[0:DH, :], ACT.Copy).then_inc(g_xs, 1)
                act.activation(x[DH:P, 1:1 + GT * P], turned[DH:P, :], ACT.Copy).then_inc(g_xs, 1)
                if g % 2 == 0:
                    act.sem_inc(g_xs, 1)
                else:
                    act.activation(x[DH:P, 0:1], xs4[0][DH:P, GT * P:GT * P + 1], ACT.Copy).then_inc(g_xs, 1)

            def attention(lp, par, n0):
                def shift(t, n, p):
                    act.wait_ge(xT_done, n + 1 + 2)
                    act.wait_ge(xs_rdy, n + 1)
                    act.sem_inc(tick["act"], 1)
                    act.activation(xs[p][DH:P, 0:1], xs[1 - p][DH:P, P:P + 1], ACT.Copy,
                                   scale=carried[DH:P, bass.ds(t, 1)]).then_inc(carry_rdy, 1)
                    act.activation(xs[p][0:DH, 0:P], tp[1][0:DH, 0:P], ACT.Copy)
                    act.activation(xs[p][DH:P, 1:1 + P], tp[1][DH:P, 0:P], ACT.Copy).then_inc(xs_rdy, 1)

                def square(n, j):
                    act.wait_ge(proj_done, n * 4 + j + 1)
                    act.wait_ge(ss_rdy, n * 4 + j + 1)
                    act.activation(sq[:, j % 2, :], bank[j % 2][:], ACT.Square).then_inc(sq_rdy, 1)

                def values_before(m, p):
                    act.wait_ge(pv_done, m * 2 + 3)
                    act.sem_inc(tick["act"], 1)
                    for e in range(2):
                        for c in range(2):
                            rows = slice(WIN * (2 * e + c), WIN * (2 * e + c) + WIN)
                            last = act.activation(vprev[rows], v[p][P - WIN:P, HP * c + e:HP * c + e + HP - 1:2, :], ACT.Copy)
                    last.then_inc(vprev_rdy, 1)

                def keep_v(n, p):
                    for j in range(2):
                        act.wait_ge(vproj_done, n * 2 + j + 1)
                        act.wait_ge(vprev_rdy, n + 1)
                        act.activation(v[p][:, 8 * j:8 * j + 8, 0:DH], v_bank[j][:].rearrange("p (a d) -> p a d", d=DH),
                                       ACT.Copy).then_inc(v_rdy, 1)

                def exps(m):
                    act.wait_ge(sd_rdy, m + 2)
                    act.activation(sd[:], sd[:], ACT.Exp).then_inc(e_rdy, 1)

                def keep_pT(m):
                    act.wait_ge(pv_done, m * 2 + 1)
                    for c in range(4):
                        act.wait_ge(pT_done, m * 5 + c + 2)
                        act.activation(pT[:, 4 * c:4 * c + 4, :], tp[c % 2][:].rearrange("p (a q) -> p a q", q=P),
                                       ACT.Copy).then_inc(pT_rdy, 1)
                    act.wait_ge(pT_done, m * 5 + 6)
                    act.activation(pTprev[:], tp[0][:, 0:4 * WIN].rearrange("p (a q) -> p a q", q=WIN),
                                   ACT.Copy).then_inc(pT_rdy, 1)

                def keep_oT(m):
                    for c in range(2):
                        act.wait_ge(pv_done, m * 2 + c + 2)
                        act.activation(oT[:, 4 * c:4 * c + 4, :], misc[c][:].rearrange("p (a q) -> p a q", q=P),
                                       ACT.Copy).then_inc(oT_rdy, 1)

                def keep_qkT(n, p):
                    for c in range(4):
                        act.wait_ge(qkT_done, n * 4 + c + 1)
                        src = tp[c % 2][:].rearrange("p (a q) -> p a q", q=P)
                        dst = qT[p][:, 4 * c:4 * c + 4, :] if c < 2 else kT[p][:, 4 * (c - 2):4 * (c - 2) + 4, WIN:WIN + P]
                        act.activation(dst, src, ACT.Copy).then_inc(qkT_rdy, 1)

                def start():
                    for t in range(2):
                        shift(t, n0 + t, t)
                        for j in range(4):
                            square(n0 + t, j)
                    keep_qkT(n0, 0)
                    keep_v(n0, 0)
                    shift(2, n0 + 2, 0)
                    square(n0 + 2, 0)

                def tile(t, m, p, last, next1, next2, next3):
                    if next2:
                        square(m + 2, 1)
                    if last:
                        keep_pT(m - 1)
                    exps(m)
                    if not next1:
                        for g in range(2):
                            group_shift(groups_before(lp, par), g)
                    if next2:
                        square(m + 2, 2)
                    if last:
                        keep_oT(m - 1)
                    if next1:
                        keep_qkT(m + 1, 1 - p)
                    if next2:
                        square(m + 2, 3)
                    if last:
                        values_before(m - 1, 1 - p)
                    if next3:
                        shift(t + 3, m + 3, 1 - p)
                    if next1:
                        keep_v(m + 1, 1 - p)
                    if next3:
                        square(m + 3, 0)

                def finish():
                    keep_pT(n0 + NT - 1)
                    keep_oT(n0 + NT - 1)
                    values_before(n0 + NT - 1, 1)

                if par == 0:
                    act.wait_ge(const_ld, 48)
                    act.wait_ge(init, 1)
                by_tile(start, tile, finish, act, n0)

            def geglu(lp, par, k0):
                w = wts[par]

                def keep_norm(g):
                    act.wait_ge(g_xnT, k0 + g + 2)
                    act.sem_inc(tick["act"], 1)
                    act.activation(xnT[:], bank[g % 2][:], ACT.Identity, scale=w[:, C_LN:C_LN + 1],
                                   bias=w[:, C_LN + 1:C_LN + 2]).then_inc(g_xnT_rdy, 1)

                def gates(g):
                    k = k0 + g
                    for i, (c0, cn) in enumerate(FB):
                        act.wait_ge(g_u, k * 3 + i + 1)
                        act.wait_ge(g_w1, k * 6 + i + 1)
                        act.sem_inc(tick["act"], 1)
                        act.activation(gl[0:cn, i, :], wide[i][0:cn, :], ACT.Gelu,
                                       bias=w[0:cn, C_B1 + i:C_B1 + i + 1]).then_inc(g_gl, 1)

                act.wait_ge(w_ld[par], lp * 48 + 48)
                act.sem_inc(tick["act"], 1)
                keep_norm(0)
                for g in range(NG):
                    gates(g)
                    if g + 2 < NG:
                        group_shift(k0, g + 2)
                    if g + 1 < NG:
                        keep_norm(g + 1)

            by_layer(act, attention, geglu)

        @block.vector
        def _(dve):
            def rows(g):
                return h[:, GT * g:GT * g + GT, :].rearrange("p a d -> p (a d)")

            def group_copy(k0, g):
                dve.wait_ge(g_xT, k0 + g + 1)
                dve.sem_inc(tick["dve"], 1)
                dve.tensor_copy(hgrp[g % 2][:].rearrange("p a d -> p (a d)"), rows(g)).then_inc(g_hgrp, 1)

            def group_moments(k0, g):
                k = k0 + g
                dve.wait_ge(g_back, k + 1)
                dve.sem_inc(tick["dve"], 1)
                for i in range(GT):
                    dve.bn_stats(st[g % 2][:, i, :], bank[g % 2][:, P * i:P * i + P]).then_inc(g_st, 1)
                dve.wait_ge(g_st, k * GT + GT)
                dve.sem_inc(tick["dve"], 1)
                for i in range(GT):
                    dve.bn_aggr(mv[g % 2][:, i, :], st[g % 2][:, i, :]).then_inc(g_mv, 1)

            def group_norm(k0, g):
                k = k0 + g
                dve.wait_ge(g_rstd, k * RSQRT_STEPS + RSQRT_STEPS)
                dve.wait_ge(g_xnT, k + 1)
                dve.sem_inc(tick["dve"], 1)
                for i in range(GT):
                    dve.tensor_scalar(xn[:, i, :], bank[g % 2][:, P * i:P * i + P], mv[g % 2][:, i, 0:1], rstd[g % 2][:, i:i + 1],
                                      ALU.subtract, ALU.mult).then_inc(g_xn, 1)

            def attention(lp, par, n0):
                def rope(t, n, p, j):
                    src = bank[j % 2][:]
                    tb = 2 * (j // 2)
                    dve.wait_ge(qk_rdy, n * 4 + j + 1)
                    dve.wait_ge(rot_sum, n * 4 + j + 1)
                    dve.wait_ge(sq_rdy, n * 4 + j + 1 + 2)
                    dve.tensor_reduce(ss[p][:, 8 * j:8 * j + 8], sq[:, j % 2, :].rearrange("p (a d) -> p a d", d=DH),
                                      AX, ALU.add).then_inc(ss_rdy, 1)
                    dve.tensor_tensor(rot_a[p][:, j, :].rearrange("p (a d) -> p a d", d=DH),
                                      src.rearrange("p (a d) -> p a d", d=DH),
                                      tab[:, tb, bass.ds(t, 1), :].to_broadcast([P, 8, DH]), ALU.mult)
                    swapped = src.rearrange("p (a e d) -> p a e d", a=8, e=2)[:, :, ::-1, :]
                    sins = tab[:, tb + 1, bass.ds(t, 1), :].rearrange("p a (e d) -> p a e d", e=2)
                    dve.tensor_tensor(rot_b[:, j, :].rearrange("p (a e d) -> p a e d", a=8, e=2), swapped,
                                      sins.to_broadcast([P, 8, 2, DH // 2]), ALU.mult).then_inc(rope_rdy, 1)

                def soft_shift(m):
                    dve.wait_ge(s_done, m + 1 + 2)
                    dve.tensor_reduce(mx[:], score[:], AX, ALU.max).then_inc(mx_rdy, 1)
                    dve.wait_ge(mx_rdy, m + 1)
                    dve.wait_ge(p_rdy, m + 1)
                    dve.tensor_tensor(sd[:], score[:], mx[:].rearrange("p (a o) -> p a o", o=1).to_broadcast([P, HEADS, 2 * WIN]),
                                      ALU.subtract).then_inc(sd_rdy, 1)

                def normalise(m):
                    dve.wait_ge(e_rdy, m + 1)
                    dve.tensor_reduce(rsum[:], sd[:], AX, ALU.add).then_inc(rs_step, 1)
                    dve.wait_ge(rs_step, m * 2 + 1)
                    dve.reciprocal(rsum[:], rsum[:]).then_inc(rs_step, 1)
                    dve.wait_ge(rs_step, m * 2 + 2)
                    dve.wait_ge(pT_done, m * 5 + 1)
                    dve.sem_inc(tick["dve"], 1)
                    for wd in range(NWIN):
                        q = slice(WIN * wd, WIN * wd + WIN)
                        inv = rsum[q].rearrange("p (a o) -> p a o", o=1)
                        if wd == 0:
                            dve.tensor_tensor(pprev[:].rearrange("q g r k -> q r g k"),
                                              sd[q, :, 0:WIN].rearrange("q (r g) k -> q r g k", g=4),
                                              rsum[q].rearrange("q (r g o) -> q r g o", g=4, o=1).to_broadcast([WIN, 4, 4, WIN]),
                                              ALU.mult)
                            dve.tensor_tensor(pw[q, :, 0:WIN], sd[q, :, WIN:2 * WIN], inv.to_broadcast([WIN, HEADS, WIN]), ALU.mult)
                        else:
                            last = dve.tensor_tensor(pw[q, :, WIN * (wd - 1):WIN * (wd + 1)], sd[q],
                                                     inv.to_broadcast([WIN, HEADS, 2 * WIN]), ALU.mult)
                    last.then_inc(p_rdy, 1)

                def add_back(t, m):
                    dve.wait_ge(y_done, m + 1)
                    dve.tensor_tensor(h[:, bass.ds(t, 1), :].rearrange("p a d -> p (a d)"), misc[1][:, 0:D],
                                      h[:, bass.ds(t, 1), :].rearrange("p a d -> p (a d)"), ALU.add).then_inc(h_rdy, 1)

                def start():
                    for t in range(2):
                        for j in range(4):
                            rope(t, n0 + t, t, j)
                    rope(2, n0 + 2, 0, 0)

                def tile(t, m, p, last, next1, next2, next3):
                    if next1 and not next2:
                        dve.wait_ge(h_rdy, m - (NT - 2) + 8 + 2)
                        for g in range(2):
                            group_copy(groups_before(lp, par), g)
                    soft_shift(m)
                    if next2:
                        rope(t + 2, m + 2, p, 1)
                        rope(t + 2, m + 2, p, 2)
                    normalise(m)
                    if next2:
                        rope(t + 2, m + 2, p, 3)
                    if last:
                        add_back(t - 1, m - 1)
                    if next3:
                        rope(t + 3, m + 3, 1 - p, 0)
                    if not next1:
                        for g in range(2):
                            group_moments(groups_before(lp, par), g)

                def finish():
                    group_norm(groups_before(lp, par), 0)
                    add_back(NT - 1, n0 + NT - 1)

                dve.wait_ge(tab_rdy, lp * 8 + par * 4 + 4)
                dve.sem_inc(tick["dve"], 1)
                by_tile(start, tile, finish, dve, n0)

            def geglu(lp, par, k0):
                w = wts[par]

                def product(g):
                    k = k0 + g
                    dve.wait_ge(g_y, k + 1)
                    for i, (c0, cn) in enumerate(FB):
                        dve.wait_ge(g_w1, k * 6 + 3 + i + 1)
                        dve.sem_inc(tick["dve"], 1)
                        dve.scalar_tensor_tensor(u[0:cn, i, :], wide[i][0:cn, :], w[0:cn, C_B1 + 3 + i:C_B1 + 4 + i],
                                                 gl[0:cn, i, :], ALU.add, ALU.mult).then_inc(g_u, 1)

                def add_back(g):
                    dve.wait_ge(g_y, k0 + g + 2)
                    dve.tensor_tensor(rows(g), y_ps, rows(g), ALU.add).then_inc(g_h, 1)

                dve.wait_ge(w_ld[par], lp * 48 + 48)
                dve.wait_ge(h_rdy, lp * 32 + par * 16 + 18)
                dve.sem_inc(tick["dve"], 1)
                for g in range(NG):
                    if g + 2 < NG:
                        group_copy(k0, g + 2)
                    if g + 1 < NG:
                        group_norm(k0, g + 1)
                    product(g)
                    if g + 2 < NG:
                        group_moments(k0, g + 2)
                    add_back(g)
                dve.wait_ge(g_h, k0 + NG + 1)
                dve.sem_inc(layer_done, 1)

            dve.memset(xs[1][:], 0.0)
            dve.memset(xs4[0][:], 0.0)
            dve.memset(ones_row[:], 1.0)
            for p in range(2):
                dve.memset(kT[p][:], 0.0)
            dve.memset(pw[:], 0.0)
            dve.memset(vprev[:], 0.0).then_inc(xs_rdy, 1)
            dve.wait_ge(xs_rdy, 1)
            dve.sem_inc(init, 1)
            dve.sem_inc(layer_done, 2)
            dve.sem_inc(rope_rdy, 2)
            dve.sem_inc(sq_rdy, 2)
            dve.sem_inc(xT_done, 2)
            dve.sem_inc(qkT_rdy, 1)
            dve.sem_inc(s_done, 2)
            dve.sem_inc(sd_rdy, 1)
            dve.sem_inc(p_rdy, 1)
            dve.sem_inc(pT_done, 1)
            dve.sem_inc(g_xT, 2)
            dve.sem_inc(g_y, 1)
            dve.sem_inc(g_xnT, 1)
            dve.sem_inc(ss_rdy, 2)
            dve.sem_inc(v_rdy, 2)
            dve.sem_inc(h_rdy, 2)
            dve.sem_inc(g_u, 3)
            dve.sem_inc(g_xs, 1)
            dve.sem_inc(g_h, 1)
            by_layer(dve, attention, geglu)

        @block.gpsimd
        def _(pool):
            def attention(lp, par, n0):
                def copy_in(t, n, p):
                    pool.wait_ge(xT_done, n - 2 + 1 + 2)
                    pool.sem_inc(tick["pool"], 1)
                    pool.tensor_copy(hcur[p][:], h[:, bass.ds(t, 1), :].rearrange("p a d -> p (a d)")).then_inc(hcur_rdy, 1)

                def rope(n, p):
                    for j in range(4):
                        pool.wait_ge(rope_rdy, n * 4 + j + 1 + 2)
                        pool.tensor_tensor(rot_a[p][:, j, :], rot_a[p][:, j, :], rot_b[:, j, :], ALU.add).then_inc(rot_sum, 1)
                    pool.wait_ge(ss_rdy, n * 4 + 6)
                    pool.sem_inc(tick["pool"], 1)
                    rsqrt(pool, rn[:], ss[p][:], rn_tmp[:], 1e-24, 0.0, rn_rdy, n * RSQRT_STEPS, tick["pool"])
                    pool.wait_ge(qkT_rdy, n * 4 + 1)
                    pool.wait_ge(rn_rdy, n * RSQRT_STEPS + RSQRT_STEPS)
                    for j in range(4):
                        pool.wait_ge(rot_sum, n * 4 + j + 5)
                        pool.tensor_tensor(qk[:, j, :].rearrange("p (a d) -> p a d", d=DH),
                                           rot_a[p][:, j, :].rearrange("p (a d) -> p a d", d=DH),
                                           rn[:, 8 * j:8 * j + 8].rearrange("p (a o) -> p a o", o=1).to_broadcast([P, 8, DH]),
                                           ALU.mult).then_inc(qk_rdy, 1)

                def keys_before(t, n, p):
                    pool.wait_ge(qkT_rdy, n * 4 + 1)
                    pool.wait_ge(s_done, n - 2 + 1 + 2)
                    pool.tensor_tensor(kT[p][:, :, 0:WIN], kT[1 - p][:, :, P:P + WIN],
                                       carried[:, bass.ds(t, 1)].rearrange("p (a o) -> p a o", o=1).to_broadcast([P, HP, WIN]),
                                       ALU.mult).then_inc(kprev_rdy, 1)

                def start():
                    copy_in(0, n0, 0)
                    copy_in(1, n0 + 1, 1)
                    rope(n0, 0)
                    keys_before(0, n0, 0)
                    copy_in(2, n0 + 2, 0)
                    rope(n0 + 1, 1)

                def tile(t, m, p, last, next1, next2, next3):
                    if next3:
                        copy_in(t + 3, m + 3, 1 - p)
                    if next1:
                        keys_before(t + 1, m + 1, 1 - p)
                    if next2:
                        rope(m + 2, p)

                pool.wait_ge(w_ld[par], lp * 48 + 48)
                pool.wait_ge(const_ld, 48)
                pool.wait_ge(rope_rdy, n0 * 4 + 2)
                pool.sem_inc(tick["pool"], 1)
                for a in range(4):
                    for b in range(BATCH):
                        last = pool.tensor_tensor(tab[:, a, TB * b:TB * b + TB, :], raw_tab[:, a, :, :],
                                                  scales[par][:, a:a + 1, :].to_broadcast([P, TB, DH]), ALU.mult)
                    last.then_inc(tab_rdy, 1)
                pool.wait_ge(g_h, groups_before(lp, par) + 1)
                pool.sem_inc(tick["pool"], 1)
                by_tile(start, tile, lambda: None, pool, n0)

            def geglu(lp, par, k0):
                for g in range(NG):
                    k = k0 + g
                    pool.wait_ge(g_mv, k * GT + GT)
                    pool.sem_inc(tick["pool"], 1)
                    rsqrt(pool, rstd[g % 2][:], mv[g % 2][:, :, 1], rstd_tmp[g % 2][:], 0.0, 1e-5, g_rstd, k * RSQRT_STEPS, tick["pool"])

            pool.wait_ge(init, 1)
            pool.sem_inc(qk_rdy, 8)
            pool.sem_inc(rot_sum, 4)
            pool.sem_inc(pv_done, 1)
            pool.sem_inc(vprev_rdy, 2)
            by_layer(pool, attention, geglu)


def local_layer_constants():
    half = np.arange(0, DH, 2, dtype=np.float32)
    inv_freq = (np.float32(1.0) / np.float32(10000.0) ** (half / np.float32(DH))).astype(np.float32)
    pos = np.arange(SEQ, dtype=np.float32)
    freqs = np.concatenate([pos[:, None] * inv_freq[None, :]] * 2, -1)
    base = (half + np.float32(0.4 * DH)) / np.float32(1.4 * DH)
    power = (pos - SEQ // 2) / np.float32(WIN // 2)
    scale = np.concatenate([base[None, :] ** power[:, None]] * 2, -1).astype(np.float32)
    cos, sin = np.cos(freqs), np.sin(freqs)
    sign = np.where(np.arange(DH) < DH // 2, -1, 1).astype(np.float32)
    tabs = np.stack([cos * scale * 8.0, sin * sign * scale * 8.0, cos / scale, sin * sign / scale])
    tables = tabs.reshape(4, TB, P, DH).transpose(2, 0, 1, 3).astype(np.float32)
    i, j = np.arange(P)[:, None, None] % WIN, np.arange(2 * WIN)[None, None, :]
    out = (j < i) | (j > i + WIN)
    first = (np.arange(NT)[None, :, None] % TB == 0) & (np.arange(P)[:, None, None] < WIN) & (j < WIN)
    mask = np.where(out | first, np.float32(NEG), np.float32(0))
    carried = np.broadcast_to((np.arange(NT) % TB != 0).astype(np.float32), (P, NT))
    return np.ascontiguousarray(tables), mask, np.ascontiguousarray(carried)


def pack_local_weights(Wqkv, q_scale, k_scale, Wo, ln_g, ln_b, W1, b1, W2, b2):
    wts = np.zeros((DEPTH, P, NWC), np.float32)
    wts[:, :, C_QKV:C_WO] = Wqkv
    wts[:, :, C_WO:C_W1] = Wo.reshape(DEPTH, HP, P, D).transpose(0, 2, 1, 3).reshape(DEPTH, P, HP * D)
    wts[:, :, C_W1:C_W2] = W1
    for f, (c0, cn) in enumerate(FB):
        wts[:, 0:cn, C_W2 + D * f:C_W2 + D * f + D] = W2[:, c0:c0 + cn]
        wts[:, 0:cn, C_B1 + f] = b1[:, DFF + c0:DFF + c0 + cn]
        wts[:, 0:cn, C_B1 + 3 + f] = b1[:, c0:c0 + cn]
    wts[:, :, C_LN], wts[:, :, C_LN + 1] = ln_g, ln_b
    swap = lambda s: np.concatenate([s[:, DH // 2:], s[:, :DH // 2]], 1)
    scales = np.concatenate([q_scale, swap(q_scale), k_scale, swap(k_scale)], 1)
    return wts, np.ascontiguousarray(scales), np.ascontiguousarray(b2)

AH, AD = 16, D // 16
SPAN = 3 * P
APR = AH // 2
VW = 32
QUADS = AH * VW // P


def windowed_attention(nc, x, xnT, ident, identb, dram):
    with ExitStack() as ctx:
        sb, ps, sem = buffers(nc, ctx)
        w = sb("a_w", [P, 3, D])
        wo = sb("a_wo", [P, QUADS, D])
        bias = sb("a_bias", [P, 2])
        bias_q = sb("a_bias_q", [P, 1])
        row_b = sb("a_row_b", [1, 2, D])
        ones_row = sb("a_ones_row", [1, P])
        heads = sb("a_heads", [P, AH])
        spread = sb("a_spread", [P, P])
        maskb = sb("a_mask", [P, NT, 2, P], BF16)
        qT = sb("a_qT", [P, NT * P])
        kT = sb("a_kT", [P, P + NT * P + P])
        v = sb("a_v", [P, NT + 2, AH, AD])
        vwin = [sb(f"a_vwin{i}", [P, 3, AH, VW]) for i in range(2)]
        qz = sb("a_qz", [P, AH, P])
        negmax = sb("a_negmax", [P, APR, 2])
        pr = [sb(f"a_pr{i}", [P, 2, SPAN]) for i in range(2)]
        pT = [sb(f"a_pT{i}", [P, 2, SPAN]) for i in range(2)]
        oT = sb("a_oT", [P, QUADS * P])
        inv = sb("a_inv", [P, QUADS * P])
        s_ps = [ps(f"a_s{i}", [P, 2, 512]) for i in range(2)]
        t_ps = ps("a_t", [P, 2, 512])
        o_ps = ps("a_o", [P, 512])
        y_ps = ps("a_y", [P, 512])

        (w_ld, init, bq_rdy, proj_done, proj_rdy, v_rdy, vwin_rdy, qz_rdy, s_done, mx_rdy, p_rdy, t_done, t_rdy, pv_done,
         oT_rdy, sum_done, inv_rdy, on_rdy, y_done, x_rdy) = (sem("a_" + s) for s in (
            "w_ld init bq_rdy proj_done proj_rdy v_rdy vwin_rdy qz_rdy s_done mx_rdy p_rdy t_done t_rdy pv_done "
            "oT_rdy sum_done inv_rdy on_rdy y_done x_rdy").split())
        tick = {e: sem(f"a_tick_{e}") for e in ("pe", "act", "dve", "pool")}
        NC = NT * P // 512
        ACT_TURNS = (1, 4, 7)
        loads = ((w, "a_w"), (wo, "a_wo"), (bias, "a_bias"), (row_b, "a_row_b"), (heads, "a_heads"), (spread, "a_spread"),
                 (maskb, "a_mask"))
        LOADED = 16 * len(loads)
        block = ctx.enter_context(nc.Block())

        def by_tile(eng, tile, last):
            tile(0, 0, True)
            with eng.Fori(0, NT // 2 - 1) as j:
                tile(j * 2 + 1, 1, False)
                tile(j * 2 + 2, 0, False)
            tile(NT - 1, 1, False)
            last(NT - 1)

        @block.sync
        def _(sp):
            for dst, name in loads:
                sp.dma_start(dst[:], dram[name]).then_inc(w_ld, 16)

        @block.tensor
        def _(pe):
            pe.wait_ge(w_ld, LOADED)
            pe.wait_ge(init, 1)
            for a in range(2):
                for c in range(NC):
                    n = NC * a + c
                    if n >= 2:
                        pe.wait_ge(proj_rdy, n - 1)
                    pe.matmul(s_ps[n % 2][:, 0, :], w[:, a, :], xnT[:, 512 * c:512 * c + 512], start=True, stop=True)\
                      .then_inc(proj_done, 1)
            for t in range(NT):
                if t >= 2:
                    pe.wait_ge(v_rdy, t - 1)
                else:
                    pe.wait_ge(proj_rdy, 2 * NC - 1 + t)
                pe.matmul(s_ps[t % 2][:, 0, 0:D], ones_row[:], row_b[:, 0, :], start=True, stop=False)
                pe.matmul(s_ps[t % 2][:, 0, 0:D], xnT[:, P * t:P * t + P], w[:, 2, :], start=False, stop=True)\
                  .then_inc(proj_done, 1)
            pe.wait_ge(v_rdy, NT)

            def scores(t, p):
                q = t * APR + p
                pe.wait_ge(p_rdy, q - 2 + 3)
                pe.wait_ge(qz_rdy, q * 2 + 2)
                for e in range(2):
                    pe.matmul(s_ps[p % 2][:, e, 0:SPAN], qz[:, 2 * p + e, :], kT[:, bass.ds(t * P, SPAN)], start=True,
                              stop=False, skip_group_check=True)
                for e in range(2):
                    s = s_ps[p % 2][:, e, 0:SPAN].rearrange("q (a k) -> q a k", a=3)[:, 0:3:2, :]
                    mm = pe.matmul(s, identb[:], maskb[:, bass.ds(t, 1), :, :].rearrange("q o a k -> q (o a) k"),
                                   start=False, stop=True, skip_group_check=True)
                mm.then_inc(s_done, 1)

            def turn(t, p):
                q = t * APR + p
                pe.wait_ge(t_rdy, q + 1)
                pe.wait_ge(p_rdy, q + 1 + 2)
                for e in range(2):
                    for a in range(3):
                        mm = pe.transpose(t_ps[:, e, P * a:P * a + P], pr[p % 2][:, e, P * a:P * a + P], ident[:])
                mm.then_inc(t_done, 1)

            def values(t, p, par):
                q = t * APR + p
                pe.wait_ge(t_rdy, q + 2)
                if p == 0:
                    pe.wait_ge(vwin_rdy, t + 1)
                    pe.wait_ge(oT_rdy, t + 1)
                pe.sem_inc(tick["pe"], 1)
                for a in range(3):
                    for e in range(2):
                        h = 2 * p + e
                        g, c = h % 4, h // 4
                        mm = pe.matmul(o_ps[VW * g:VW * g + VW, P * c:P * c + P], vwin[par][:, a, h, :],
                                       pT[p % 2][:, e, P * a:P * a + P], start=(a == 0), stop=(a == 2), skip_group_check=True)
                mm.then_inc(pv_done, 1)

            def spread_sums(t):
                pe.wait_ge(oT_rdy, t + 2)
                pe.wait_ge(x_rdy, t + 1)
                pe.matmul(y_ps[:], spread[:], oT[:], start=True, stop=True).then_inc(sum_done, 1)

            def project_out(t):
                pe.wait_ge(on_rdy, (t + 1) * QUADS)
                pe.matmul(y_ps[:, 0:D], ones_row[:], row_b[:, 1, :], start=True, stop=False)
                for c in range(QUADS):
                    mm = pe.matmul(y_ps[:, 0:D], oT[:, P * c:P * c + P], wo[:, c, :], start=False, stop=(c == QUADS - 1))
                mm.then_inc(y_done, 1)

            def tile(t, par, first):
                for p in range(APR + 2):
                    if p < APR:
                        scores(t, p)
                    if 1 <= p <= APR:
                        turn(t, p - 1)
                    if p >= 2:
                        values(t, p - 2, par)
                    if p == 1 and not first:
                        spread_sums(t - 1)
                    if p == 7 and not first:
                        project_out(t - 1)

            def last(t):
                spread_sums(t)
                project_out(t)

            by_tile(pe, tile, last)

        @block.scalar
        def _(act):
            act.wait_ge(bq_rdy, 1)
            for a in range(2):
                for c in range(NC):
                    n = NC * a + c
                    act.wait_ge(proj_done, n + 1)
                    dst = qT[:, 512 * c:512 * c + 512] if a == 0 else kT[:, P + 512 * c:P + 512 * c + 512]
                    act.activation(dst, s_ps[n % 2][:, 0, :], ACT.Identity, bias=bias_q[:] if a == 0 else bias[:, 1:2],
                                   scale=float(AD) ** -0.5 if a == 0 else 1.0).then_inc(proj_rdy, 1)
            for t in range(NT):
                act.wait_ge(proj_done, 2 * NC + t + 1)
                act.activation(v[:, t + 1, :, :], s_ps[t % 2][:, 0, 0:D].rearrange("k (h d) -> k h d", h=AH), ACT.Copy)\
                   .then_inc(v_rdy, 1)
            act.wait_ge(v_rdy, NT)

            def window(t, par):
                act.wait_ge(pv_done, (t - 1) * APR + 2 * APR)
                act.sem_inc(tick["act"], 1)
                act.activation(vwin[par][:, :, :, 0:AD], v[:, bass.ds(t, 3), :, :], ACT.Copy).then_inc(vwin_rdy, 1)

            def weights(t, p):
                q = t * APR + p
                act.wait_ge(mx_rdy, q + 1)
                for e in range(2):
                    ins = act.activation(pr[p % 2][:, e, :], s_ps[p % 2][:, e, 0:SPAN], ACT.Exp, bias=negmax[:, p, e:e + 1])
                ins.then_inc(p_rdy, 1)

            def keep_turned(t, p):
                q = t * APR + p
                act.wait_ge(t_done, q + 1)
                act.activation(pT[p % 2][:], t_ps[:, :, 0:SPAN], ACT.Copy).then_inc(t_rdy, 1)

            def keep_out(t):
                act.wait_ge(pv_done, (t + 1) * APR + 2 * APR)
                act.activation(oT[:], o_ps[:], ACT.Copy).then_inc(oT_rdy, 1)

            def tile(t, par, first):
                window(t, par)
                for p in range(APR + 1):
                    if p < APR:
                        weights(t, p)
                    if p >= 1 and (p - 1) in ACT_TURNS:
                        keep_turned(t, p - 1)
                    if p == 0 and not first:
                        keep_out(t - 1)

            by_tile(act, tile, keep_out)

        @block.vector
        def _(dve):
            dve.memset(ones_row[:], 1.0)
            dve.memset(kT[:, 0:P], 0.0)
            dve.memset(kT[:, P + NT * P:], 0.0)
            dve.memset(v[:], 0.0)
            dve.memset(vwin[0][:], 1.0)
            dve.memset(vwin[1][:], 1.0).then_inc(init, 1)
            dve.sem_inc(p_rdy, 2)
            dve.sem_inc(pv_done, 2 * APR)
            for s in (t_rdy, oT_rdy, x_rdy):
                dve.sem_inc(s, 1)
            dve.wait_ge(w_ld, LOADED)
            dve.tensor_scalar(bias_q[:], bias[:, 0:1], float(AD) ** -0.5, None, ALU.mult).then_inc(bq_rdy, 1)

            def maxima(t, p):
                q = t * APR + p
                dve.wait_ge(s_done, q + 1)
                dve.tensor_reduce(negmax[:, p, :], s_ps[p % 2][:, :, 0:SPAN], AX, ALU.max, negate=True).then_inc(mx_rdy, 1)

            def keep_turned(t, p):
                q = t * APR + p
                dve.wait_ge(t_done, q + 1)
                dve.tensor_copy(pT[p % 2][:], t_ps[:, :, 0:SPAN]).then_inc(t_rdy, 1)

            def divide(t, c):
                quad = slice(P * c, P * c + P)
                dve.wait_ge(sum_done, t + 1)
                dve.reciprocal(inv[:, quad], y_ps[:, quad]).then_inc(inv_rdy, 1)
                dve.wait_ge(inv_rdy, t * QUADS + c + 1)
                dve.tensor_tensor(oT[:, quad], oT[:, quad], inv[:, quad], ALU.mult).then_inc(on_rdy, 1)

            def add(t):
                dve.wait_ge(y_done, t + 1)
                xt = x[:, bass.ds(t, 1), :].rearrange("q a d -> q (a d)")
                dve.tensor_tensor(xt, xt, y_ps[:, 0:D], ALU.add).then_inc(x_rdy, 1)

            def tile(t, par, first):
                for p in range(APR + 1):
                    if p < APR:
                        maxima(t, p)
                    if 2 <= p < 2 + QUADS and not first:
                        divide(t - 1, p - 2)
                    if p >= 1 and (p - 1) not in ACT_TURNS:
                        keep_turned(t, p - 1)
                    if p == APR and not first:
                        add(t - 1)

            def last(t):
                for c in range(QUADS):
                    divide(t, c)
                add(t)
                dve.wait_ge(x_rdy, NT + 1)

            by_tile(dve, tile, last)

        @block.gpsimd
        def _(pool):
            pool.wait_ge(w_ld, LOADED)
            pool.wait_ge(proj_rdy, 2 * NC)

            def tile(t, par, first):
                for h in range(AH):
                    if not first and h % 2 == 0:
                        pool.wait_ge(s_done, t * APR - APR + h // 2 + 1)
                        pool.sem_inc(tick["pool"], 1)
                    pool.tensor_tensor(qz[:, h, :], qT[:, bass.ds(t * P, P)], heads[:, h:h + 1].to_broadcast([P, P]),
                                       ALU.mult).then_inc(qz_rdy, 1)

            by_tile(pool, tile, lambda t: None)


def pack_attention_weights(Wq, Wk, Wv, Wo):
    wo = np.zeros((4, VW, QUADS, D), np.float32)
    wo[:, 0:AD] = Wo.reshape(QUADS, 4, AD, D).transpose(1, 2, 0, 3)
    return np.ascontiguousarray(np.stack([Wq, Wk, Wv], 1)), wo.reshape(P, QUADS, D)


def attention_constants():
    i, j = np.arange(P)[:, None], np.arange(P)[None, :]
    before, behind = j < i, j > i
    never = np.ones((P, P), bool)
    tiles = [np.stack([never if t % TB == 0 else before, never if t % TB == TB - 1 else behind], 1) for t in range(NT)]
    mask = np.where(np.stack(tiles, 1), np.float32(NEG), np.float32(0))
    heads = (np.arange(P)[:, None] // AD == np.arange(AH)[None, :]).astype(np.float32)
    spread = (i == j // VW * VW + AD).astype(np.float32)
    return mask, heads, spread


NCOL, NNEU = 16, 32
GATE_H = D // 2
CB = NCOL * NNEU // P


def column_mixture(nc, x, xn, xnT, ident, dram):
    with ExitStack() as ctx:
        sb, ps, sem = buffers(nc, ctx)
        w = sb("m_w", [P, CB * P])
        pw = sb("m_pw", [P, CB, D])
        gw1 = sb("m_gw1", [P, GATE_H])
        gw2 = sb("m_gw2", [GATE_H, NCOL])
        bcol = sb("m_bcol", [P, CB + 1])
        rows = sb("m_rows", [1, NCOL + D])
        lng = sb("m_lng", [P, 2, D])
        emb = sb("m_emb", [NCOL, D])
        spread = sb("m_spread", [NCOL, CB * P])
        order = sb("m_order", [P, NCOL])
        ones_row = sb("m_ones_row", [1, P])
        embT = sb("m_embT", [P, NCOL])
        esq = sb("m_esq", [NCOL, D])
        ess, ers, etm = (sb("m_" + n, [NCOL, 1]) for n in ("ess", "ers", "etm"))
        xsq = sb("m_xsq", [P, NT, D])
        xss, xrs, xtm = (sb("m_" + n, [P, NT]) for n in ("xss", "xrs", "xtm"))
        hT = sb("m_hT", [GATE_H, NT * P])
        cT = sb("m_cT", [P, CB, NT * P])
        sg, lg, ex, ca = (sb("m_" + n, [P, NT, NCOL]) for n in ("sg", "lg", "ex", "ca"))
        best, tot, top = (sb("m_" + n, [P, NT]) for n in ("best", "tot", "top"))
        wT = sb("m_wT", [NCOL, NT * P])
        y = xsq
        st = sb("m_st", [P, NT, 6])
        mv = sb("m_mv", [P, NT, 2])
        rstd, rtm = (sb("m_" + n, [P, NT]) for n in ("rstd", "rtm"))
        gp = [ps(f"m_gp{i}", [P, 512]) for i in range(4)]
        sim = ps("m_sim", [P, NT, NCOL])
        gat = ps("m_gat", [P, NT, NCOL])
        yp = [ps(f"m_yp{i}", [P, 512]) for i in range(2)]
        (w_ld, emb_step, ess_rdy, ers_step, embT_done, embT_rdy, xss_rdy, xrs_step, g_done, g_rdy, sim_done, gat_done, step, act_step,
         wT_done, wT_rdy, sp_done, comb_rdy, y_done, y_rdy, st_rdy, mv_rdy, rs_step, out_step, init, tick, ptick) = (sem("m_" + s) for s in (
            "w_ld emb_step ess_rdy ers_step embT_done embT_rdy xss_rdy xrs_step g_done g_rdy sim_done gat_done step act_step "
            "wT_done wT_rdy sp_done comb_rdy y_done y_rdy st_rdy mv_rdy rs_step out_step init tick ptick").split())
        NG = NT * P // 512
        NGELU = NG * (1 + CB)
        MIX_EX, MIX_STEPS = 7, 15
        loads = ((w[:], "m_w"), (pw[:], "m_pw"), (gw1[:], "m_gw1"), (gw2[:], "m_gw2"), (bcol[:], "m_bcol"), (rows[:], "m_rows"),
                 (emb[:], "m_emb"), (spread[:], "m_spread"))
        wide = ((lng[:].rearrange("p a d -> p (a d)"), "m_lng", 2 * D), (order[:], "m_order", NCOL))
        LOADED = 16 * (len(loads) + len(wide))
        block = ctx.enter_context(nc.Block())

        def over(small, n):
            return small.rearrange("p (t o) -> p t o", o=1).to_broadcast([P, NT, n])

        @block.sync
        def _(sp):
            for dst, name in loads:
                sp.dma_start(dst, dram[name]).then_inc(w_ld, 16)
            for dst, name, n in wide:
                sp.dma_start(dst, dram[name].broadcast_to([P, n])).then_inc(w_ld, 16)

        @block.tensor
        def _(pe):
            pe.wait_ge(w_ld, LOADED)
            pe.wait_ge(init, 1)
            for g in range(NG):
                for c in range(1 + CB):
                    n = g * (1 + CB) + c
                    if n >= 4:
                        pe.wait_ge(g_rdy, n - 3)
                    lhs, m = (gw1[:], GATE_H) if c == 0 else (w[:, P * (c - 1):P * c], P)
                    pe.matmul(gp[n % 4][0:m, :], lhs, xnT[:, 512 * g:512 * g + 512], start=True, stop=True).then_inc(g_done, 1)
            pe.wait_ge(ers_step, RSQRT_STEPS + 1)
            pe.transpose(yp[0][:, 0:NCOL], emb[:], ident[0:NCOL, 0:NCOL]).then_inc(embT_done, 1)
            pe.wait_ge(embT_rdy, 1)
            for t in range(NT):
                mm = pe.matmul(sim[:, t, :], xnT[:, P * t:P * t + P], embT[:], start=True, stop=True, skip_group_check=True)
            mm.then_inc(sim_done, 1)
            pe.wait_ge(g_rdy, NGELU)
            for t in range(NT):
                pe.matmul(gat[:, t, :], ones_row[:], rows[:, 0:NCOL], start=True, stop=False, skip_group_check=True)
                mm = pe.matmul(gat[:, t, :], hT[:, P * t:P * t + P], gw2[:], start=False, stop=True, skip_group_check=True)
            mm.then_inc(gat_done, 1)
            pe.wait_ge(step, MIX_STEPS)
            for g in range(NG):
                for k in range(4):
                    t = 4 * g + k
                    mm = pe.transpose(gp[g][0:NCOL, P * k:P * k + P], ca[:, t, :], ident[:])
                mm.then_inc(wT_done, 1)
            for g in range(NG):
                pe.wait_ge(wT_rdy, NG)
                for c in range(CB):
                    n = g * CB + c
                    if n >= 4:
                        pe.wait_ge(comb_rdy, n - 3)
                    pe.matmul(gp[n % 4][:], spread[:, P * c:P * c + P], wT[:, 512 * g:512 * g + 512], start=True, stop=True)\
                      .then_inc(sp_done, 1)
            for g in range(NG):
                pe.wait_ge(comb_rdy, CB * (g + 1))
                if g >= 2:
                    pe.wait_ge(y_rdy, g - 1)
                for k in range(4):
                    t = 4 * g + k
                    yt = yp[g % 2][:, D * k:D * k + D]
                    pe.matmul(yt, ones_row[:], rows[:, NCOL:], start=True, stop=False, skip_group_check=True)
                    for c in range(CB):
                        mm = pe.matmul(yt, cT[:, c, P * t:P * t + P], pw[:, c, :], start=False, stop=(c == CB - 1),
                                       skip_group_check=True)
                mm.then_inc(y_done, 1)

        @block.scalar
        def _(act):
            act.wait_ge(w_ld, LOADED)
            for g in range(NG):
                for c in range(1 + CB):
                    n = g * (1 + CB) + c
                    act.wait_ge(g_done, n + 1)
                    if c == 0:
                        ins = act.activation(hT[:, 512 * g:512 * g + 512], gp[n % 4][0:GATE_H, :], ACT.Gelu,
                                             bias=bcol[0:GATE_H, CB:CB + 1])
                    else:
                        ins = act.activation(cT[:, c - 1, 512 * g:512 * g + 512], gp[n % 4][:], ACT.Gelu, bias=bcol[:, c - 1:c])
                    ins.then_inc(g_rdy, 1)
            act.wait_ge(embT_done, 1)
            act.activation(embT[:], yp[0][:, 0:NCOL], ACT.Copy).then_inc(embT_rdy, 1)
            act.wait_ge(step, 2)
            act.activation(sg[:], sg[:], ACT.Exp, scale=-1.0).then_inc(act_step, 1)
            act.wait_ge(step, MIX_EX)
            act.activation(ex[:], ex[:], ACT.Exp).then_inc(act_step, 1)
            for g in range(NG):
                act.wait_ge(wT_done, g + 1)
                act.activation(wT[:, 512 * g:512 * g + 512], gp[g][0:NCOL, :], ACT.Copy).then_inc(wT_rdy, 1)

        @block.vector
        def _(dve):
            dve.memset(ones_row[:], 1.0).then_inc(init, 1)
            dve.tensor_tensor(xsq[:], xn[:], xn[:], ALU.mult).then_inc(xss_rdy, 1)
            dve.wait_ge(w_ld, LOADED)
            dve.tensor_tensor(esq[:], emb[:], emb[:], ALU.mult).then_inc(emb_step, 1)
            dve.wait_ge(emb_step, 1)
            dve.tensor_reduce(ess[:], esq[:], AX, ALU.add).then_inc(ess_rdy, 1)
            dve.wait_ge(xss_rdy, 1)
            dve.tensor_reduce(xss[:], xsq[:], AX, ALU.add).then_inc(xss_rdy, 1)
            dve.wait_ge(ers_step, RSQRT_STEPS)
            dve.tensor_scalar(emb[:], emb[:], ers[:], None, ALU.mult).then_inc(ers_step, 1)

            steps = 0

            def link(ins):
                nonlocal steps
                steps += 1
                ins.then_inc(step, 1)
                dve.wait_ge(step, steps)

            dve.wait_ge(sim_done, 1)
            dve.wait_ge(xrs_step, RSQRT_STEPS)
            link(dve.tensor_tensor(lg[:], sim[:], over(xrs[:], NCOL), ALU.mult))
            dve.wait_ge(gat_done, 1)
            link(dve.tensor_scalar(sg[:], gat[:], -EXP_MAX, None, ALU.max))
            dve.wait_ge(act_step, 1)
            link(dve.tensor_scalar(sg[:], sg[:], 1.0, None, ALU.add))
            link(dve.reciprocal(sg[:], sg[:]))
            link(dve.tensor_tensor(lg[:], lg[:], sg[:], ALU.add))
            link(dve.tensor_reduce(best[:], lg[:], AX, ALU.max))
            link(dve.tensor_tensor(ex[:], lg[:], over(best[:], NCOL), ALU.subtract))
            assert steps == MIX_EX
            link(dve.tensor_tensor(ca[:], lg[:], over(best[:], NCOL), ALU.is_equal))
            link(dve.tensor_tensor(ca[:], ca[:], order[:].rearrange("p (o c) -> p o c", o=1).to_broadcast([P, NT, NCOL]), ALU.mult))
            link(dve.tensor_reduce(top[:], ca[:], AX, ALU.max))
            link(dve.tensor_tensor(ca[:], ca[:], over(top[:], NCOL), ALU.is_equal))
            dve.wait_ge(act_step, 2)
            link(dve.tensor_reduce(tot[:], ex[:], AX, ALU.add))
            link(dve.reciprocal(tot[:], tot[:]))
            link(dve.tensor_tensor(ex[:], ex[:], over(tot[:], NCOL), ALU.mult))
            assert steps == MIX_STEPS - 1
            link(dve.tensor_tensor(ca[:], ca[:], ex[:], ALU.mult))
            for g in range(NG):
                for c in range(CB):
                    n = g * CB + c
                    dve.wait_ge(sp_done, n + 1)
                    part = cT[:, c, 512 * g:512 * g + 512]
                    dve.tensor_tensor(part, part, gp[n % 4][:], ALU.mult).then_inc(comb_rdy, 1)
            for g in range(NG):
                s = slice(4 * g, 4 * g + 4)
                dve.wait_ge(y_done, g + 1)
                dve.tensor_tensor(y[:, s, :], yp[g % 2][:].rearrange("p (t d) -> p t d", d=D), xn[:, s, :], ALU.add).then_inc(y_rdy, 1)
            for t in range(NT):
                dve.wait_ge(y_rdy, t // 4 + 1)
                dve.bn_stats(st[:, t, :], y[:, t, :]).then_inc(st_rdy, 1)
            dve.wait_ge(st_rdy, NT)
            for t in range(NT):
                dve.bn_aggr(mv[:, t, :], st[:, t, :]).then_inc(mv_rdy, 1)
            dve.wait_ge(mv_rdy, NT)
            dve.tensor_tensor(y[:], y[:], mv[:, :, 0:1].to_broadcast([P, NT, D]), ALU.subtract).then_inc(out_step, 1)
            dve.wait_ge(rs_step, RSQRT_STEPS)
            dve.wait_ge(out_step, 1)
            dve.tensor_tensor(y[:], y[:], over(rstd[:], D), ALU.mult).then_inc(out_step, 1)
            dve.wait_ge(out_step, 2)
            dve.tensor_tensor(y[:], y[:], lng[:, 0:1, :].to_broadcast([P, NT, D]), ALU.mult).then_inc(out_step, 1)
            dve.tensor_tensor(x[:], x[:], lng[:, 1:2, :].to_broadcast([P, NT, D]), ALU.add).then_inc(out_step, 1)
            dve.wait_ge(out_step, 4)
            dve.tensor_tensor(x[:], x[:], y[:], ALU.add).then_inc(out_step, 1)
            dve.wait_ge(out_step, 5)

        @block.gpsimd
        def _(pool):
            pool.wait_ge(ess_rdy, 1)
            rsqrt(pool, ers[:], ess[:], etm[:], 1e-24, 0.0, ers_step, 0, ptick)
            pool.wait_ge(ers_step, RSQRT_STEPS)
            pool.wait_ge(xss_rdy, 2)
            rsqrt(pool, xrs[:], xss[:], xtm[:], 1e-24, 0.0, xrs_step, 0, ptick)
            pool.wait_ge(xrs_step, RSQRT_STEPS)
            pool.wait_ge(mv_rdy, NT)
            rsqrt(pool, rstd[:], mv[:, :, 1], rtm[:], 0.0, 1e-5, rs_step, 0, ptick)


def pack_mixture_weights(W_cols, b_cols, gate_b1, gate_b2, proj_w, proj_b, ln_g, ln_b):
    w = np.ascontiguousarray(W_cols.transpose(1, 0, 2).reshape(D, NCOL * NNEU))
    pw = np.ascontiguousarray(proj_w.reshape(CB, P, D).transpose(1, 0, 2))
    bcol = np.zeros((P, CB + 1), np.float32)
    bcol[:, 0:CB] = b_cols.reshape(CB, P).T
    bcol[0:GATE_H, CB] = gate_b1
    return w, pw, bcol, np.concatenate([gate_b2, proj_b])[None], np.concatenate([ln_g, ln_b])[None]


def mixture_constants():
    spread = (np.arange(CB * P)[None, :] // NNEU == np.arange(NCOL)[:, None]).astype(np.float32)
    return spread, np.arange(NCOL, 0, -1, dtype=np.float32)[None]

def program(nc, dram):
    with ExitStack() as ctx:
        sb, ps, sem = buffers(nc, ctx)
        x = sb("x", [P, NT, D])
        xn = sb("xn", [P, NT, D])
        ident = sb("ident", [P, P])
        identb = sb("identb", [P, P], BF16)
        loaded, stored = sem("loaded"), sem("stored")
        with nc.Block() as block:
            @block.sync
            def _(sp):
                for dst, src in ((x[:], dram["x"].rearrange("(t p) d -> p t d", p=P)), (ident[:], dram["ident"]),
                                 (identb[:], dram["identb"])):
                    sp.dma_start(dst, src).then_inc(loaded, 16)
                sp.wait_ge(loaded, 48)
        gated_delta(nc, x, xn, ident, identb, dram)
        local_layers(nc, xn, ident, identb, dram)
        with ExitStack() as second:
            xnT = second.enter_context(nc.sbuf_tensor("xnT2", [P, NT * P], F32))
            normalise(nc, x, xn, lambda t, n: xnT[:, P * t:P * (t + n)], ident, "n1", add=xn)
            windowed_attention(nc, x, xnT, ident, identb, dram)
            column_mixture(nc, x, xn, xnT, ident, dram)
        with nc.Block() as block:
            @block.sync
            def _(sp):
                sp.dma_start(dram["out"].rearrange("(t p) d -> p t d", p=P), x[:]).then_inc(stored, 16)
                sp.wait_ge(stored, 16)


def kernel(L0_attn_hidden_states, L0_attn_q_w, L0_attn_k_w, L0_attn_v_w, L0_attn_a_w, L0_attn_b_w, L0_attn_g_w, L0_attn_o_w,
           L0_attn_conv_q_w, L0_attn_conv_k_w, L0_attn_conv_v_w, L0_attn_A_log, L0_attn_dt_bias, L0_attn_norm_weight,
           L0_ffn_Wqkv, L0_ffn_q_scale, L0_ffn_k_scale, L0_ffn_Wo, L0_ffn_ln_g, L0_ffn_ln_b, L0_ffn_W1, L0_ffn_b1, L0_ffn_W2,
           L0_ffn_b2, L1_attn_Wq, L1_attn_bq, L1_attn_Wk, L1_attn_bk, L1_attn_Wv, L1_attn_bv, L1_attn_Wo, L1_attn_bo,
           L1_ffn_col_emb, L1_ffn_gate_w1, L1_ffn_gate_b1, L1_ffn_gate_w2, L1_ffn_gate_b2, L1_ffn_W_cols, L1_ffn_b_cols,
           L1_ffn_proj_w, L1_ffn_proj_b, L1_ffn_ln_g, L1_ffn_ln_b):
    import concourse.bacc as bacc
    from concourse.bass_utils import run_bass_kernel_spmd
    import ml_dtypes
    A = np.ascontiguousarray
    bf16 = ml_dtypes.bfloat16
    w_qkv, w_abg, w_conv, wo = pack_delta_weights(*[A(a) for a in (
        L0_attn_q_w, L0_attn_k_w, L0_attn_v_w, L0_attn_a_w, L0_attn_b_w, L0_attn_g_w, L0_attn_o_w,
        L0_attn_conv_q_w, L0_attn_conv_k_w, L0_attn_conv_v_w)])
    tri, causal, blocks = delta_constants()
    l_wts, l_scales, l_b2 = pack_local_weights(*[A(a) for a in (
        L0_ffn_Wqkv, L0_ffn_q_scale, L0_ffn_k_scale, L0_ffn_Wo, L0_ffn_ln_g, L0_ffn_ln_b, L0_ffn_W1, L0_ffn_b1, L0_ffn_W2,
        L0_ffn_b2)])
    l_tables, l_mask, l_carried = local_layer_constants()
    a_mask, a_heads, a_spread = attention_constants()
    a_w, a_wo = pack_attention_weights(*[A(a) for a in (L1_attn_Wq, L1_attn_Wk, L1_attn_Wv, L1_attn_Wo)])
    m_w, m_pw, m_bcol, m_rows, m_lng = pack_mixture_weights(*[A(a) for a in (
        L1_ffn_W_cols, L1_ffn_b_cols, L1_ffn_gate_b1, L1_ffn_gate_b2, L1_ffn_proj_w, L1_ffn_proj_b, L1_ffn_ln_g, L1_ffn_ln_b)])
    m_spread, m_order = mixture_constants()
    arrays = {"x": A(L0_attn_hidden_states).reshape(-1, D), "ident": np.eye(P, dtype=np.float32), "identb": np.eye(P, dtype=bf16),
              "d_w_qkv": w_qkv, "d_w_abg": w_abg, "d_w_conv": w_conv, "d_wo": wo, "d_dt_bias": A(L0_attn_dt_bias)[None],
              "d_a_log": A(L0_attn_A_log)[None], "d_nw": A(L0_attn_norm_weight)[None], "d_tri": tri,
              "d_causal": causal.astype(bf16), "d_blocks": blocks.astype(bf16),
              "l_wts": l_wts, "l_scales": l_scales, "l_b2": l_b2, "l_tables": l_tables, "l_mask": A(l_mask).astype(bf16),
              "l_carried": l_carried,
              "a_w": a_w, "a_wo": a_wo, "a_bias": A(np.stack([A(L1_attn_bq), A(L1_attn_bk)], 1)),
              "a_row_b": A(np.stack([A(L1_attn_bv), A(L1_attn_bo)])[None]), "a_heads": a_heads, "a_spread": a_spread, "a_mask": a_mask.astype(bf16),
              "m_w": m_w, "m_pw": m_pw, "m_gw1": A(L1_ffn_gate_w1), "m_gw2": A(L1_ffn_gate_w2), "m_bcol": m_bcol,
              "m_rows": m_rows, "m_emb": A(L1_ffn_col_emb), "m_spread": m_spread, "m_lng": m_lng, "m_order": m_order}
    nc = bacc.Bacc("TRN2", target_bir_lowering=False, num_devices=1)
    dram = {k: nc.dram_tensor("in_" + k, a.shape, mybir.dt.from_np(a.dtype), kind="ExternalInput").ap() for k, a in arrays.items()}
    dram["out"] = nc.dram_tensor("result", (BATCH * SEQ, D), F32, kind="ExternalOutput").ap()
    program(nc, dram)
    r = run_bass_kernel_spmd(nc, [{"in_" + k: a for k, a in arrays.items()}], core_ids=[0])
    return r.results[0]["result"].reshape(BATCH, SEQ, D)
```
